# Optimizing a Trainium2 kernel written in Bass

```python
import numpy as np
import jax
import jax.numpy as jnp

def _softmax(x, axis=-1):
    return jax.nn.softmax(x, axis=axis)

def _gelu(x):
    return jax.nn.gelu(x, approximate=True)

def _silu(x):
    return jax.nn.silu(x)

def _sigmoid(x):
    return jax.nn.sigmoid(x)

def _layernorm(x, axis=-1, eps=1e-05):
    m = jnp.mean(x, axis=axis, keepdims=True)
    v = jnp.var(x, axis=axis, keepdims=True)
    return (x - m) / jnp.sqrt(v + eps)

def _scatter_add(tgt, idx, src, axis=0):
    return tgt.at[idx].add(src)

def _segment_sum(src, seg, n):
    return jax.ops.segment_sum(src, seg, n)
kernel_name = 'mk_gnn_resnorm_d2_gnn_r32_268a25'

def setup_inputs(seed: int=0):
    np.random.seed(seed)
    _w = jnp.asarray

    def _rec_inputs():
        import jax
        import jax.numpy as jnp
        _gk = jax.random.key(seed)
        x = -0.0002117 + 1 * jax.random.normal(jax.random.fold_in(_gk, 1), (3125, 256), jnp.float32)
        src = jax.random.randint(jax.random.fold_in(_gk, 2), (50000,), 0, 3125, jnp.int32)
        dst = jax.random.randint(jax.random.fold_in(_gk, 3), (50000,), 0, 3125, jnp.int32)
        _o = jnp.argsort(dst, stable=True)
        src = src[_o]
        dst = dst[_o]
        edge_type_7 = jax.random.randint(jax.random.fold_in(_gk, 13), (50000,), 0, 7, jnp.int32)
        return (x, src, dst, edge_type_7)
    x, src, dst, edge_type_7 = _rec_inputs()

    def _L0_gnn_setup():
        import jax, jax.numpy as jnp
        import numpy as np
        EPS = 1e-05
        BATCH_SIZE = 8
        GROUP = 32
        N_EDGE_TYPE = 7

        def dual_gn(data, batch_id, w, b):
            N, C = data.shape
            cpg = C // GROUP

            def adjust(t):
                t = t.reshape(-1, GROUP, cpg).sum(-1, keepdims=True)
                return jnp.broadcast_to(t, (t.shape[0], GROUP, cpg)).reshape(-1, C)
            ones = jnp.ones((N,), data.dtype)
            count = jax.ops.segment_sum(ones, batch_id, num_segments=BATCH_SIZE) * cpg
            inv_count = 1.0 / (count + EPS)
            mean = adjust(jax.ops.segment_sum(data, batch_id, num_segments=BATCH_SIZE) * inv_count[:, None])
            out = data - mean[batch_id]
            var = adjust(jax.ops.segment_sum(out * out, batch_id, num_segments=BATCH_SIZE) * inv_count[:, None])
            inv_std = 1.0 / jnp.sqrt(var + EPS)
            return out * inv_std[batch_id] * w + b

        def graph_conv(x, row, col, etype, W):
            N, C = x.shape
            idx = row * N_EDGE_TYPE + etype
            gathered = x[col]
            s = jax.ops.segment_sum(gathered, idx, num_segments=N * N_EDGE_TYPE)
            cnt = jax.ops.segment_sum(jnp.ones((col.shape[0],), x.dtype), idx, num_segments=N * N_EDGE_TYPE)
            col_data = s / jnp.maximum(cnt, 1.0)[:, None]
            return col_data.reshape(N, N_EDGE_TYPE * C) @ W

        def silu(x):
            return x * jax.nn.sigmoid(x)
        key = jax.random.key(seed)
        ks = jax.random.split(key, 10)
        N, C, E = (3125, 256, 21875)
        x = jax.random.normal(ks[0], (N, C), dtype=jnp.float32)
        edge_index = jax.random.randint(ks[1], (2, E), 0, N)
        edge_type = jax.random.randint(ks[2], (E,), 0, N_EDGE_TYPE)
        batch_id = jnp.sort(jax.random.randint(ks[3], (N,), 0, BATCH_SIZE))
        a = np.sqrt(3.0) * np.sqrt(2.0 / float(7 * C + 7 * C))
        conv1_w = jax.random.uniform(ks[4], (N_EDGE_TYPE * C, C), dtype=jnp.float32, minval=-a, maxval=a)
        conv2_w = jax.random.uniform(ks[5], (N_EDGE_TYPE * C, C), dtype=jnp.float32, minval=-a, maxval=a)
        gn1_w = jnp.ones((1, C), jnp.float32)
        gn1_b = jnp.zeros((1, C), jnp.float32)
        gn2_w = jnp.ones((1, C), jnp.float32)
        gn2_b = jnp.zeros((1, C), jnp.float32)
        return {'x': x, 'gn1_w': gn1_w, 'gn1_b': gn1_b, 'conv1_w': conv1_w, 'gn2_w': gn2_w, 'gn2_b': gn2_b, 'conv2_w': conv2_w, 'edge_index': edge_index, 'edge_type': edge_type, 'batch_id': batch_id}
    _L0_gnn_all = _L0_gnn_setup()
    _L0_gnn_in = {k: v for k, v in _L0_gnn_all.items() if k in ('gn1_w', 'gn1_b', 'conv1_w', 'gn2_w', 'gn2_b', 'conv2_w')}
    del _L0_gnn_all

    def _L1_gnn_setup():
        import jax, jax.numpy as jnp
        import numpy as np
        N = 50000
        NEG_SLOPE = 0.2

        def _gat_conv(x, src, dst, W, a_src, a_dst, b, heads, out_c):
            n = x.shape[0]
            h = (x @ W).reshape(n, heads, out_c)
            s = jnp.einsum('nhc,hc->nh', h, a_src)
            d = jnp.einsum('nhc,hc->nh', h, a_dst)
            e = jax.nn.leaky_relu(s[src] + d[dst], NEG_SLOPE)
            e_max = jax.ops.segment_max(e, dst, num_segments=n)
            e = jnp.exp(e - e_max[dst])
            denom = jax.ops.segment_sum(e, dst, num_segments=n)
            alpha = e / (denom[dst] + 1e-16)
            msg = h[src] * alpha[:, :, None]
            out = jax.ops.segment_sum(msg, dst, num_segments=n)
            return out.reshape(n, heads * out_c) + b
        key = jax.random.key(seed)
        ks = jax.random.split(key, 11)
        E = 25000
        return {'x': jax.random.normal(ks[0], (N, 256), jnp.float32), 'edge_index': jax.random.randint(ks[1], (2, E), 0, N, jnp.int32), 'W1': jax.random.normal(ks[2], (256, 256), jnp.float32) * 0.06, 'att_src1': jax.random.normal(ks[3], (8, 32), jnp.float32) * 0.1, 'att_dst1': jax.random.normal(ks[4], (8, 32), jnp.float32) * 0.1, 'b1': jax.random.normal(ks[5], (256,), jnp.float32) * 0.02, 'W2': jax.random.normal(ks[6], (256, 256), jnp.float32) * 0.06, 'att_src2': jax.random.normal(ks[7], (1, 256), jnp.float32) * 0.05, 'att_dst2': jax.random.normal(ks[8], (1, 256), jnp.float32) * 0.05, 'b2': jax.random.normal(ks[9], (256,), jnp.float32) * 0.02}
    _L1_gnn_all = _L1_gnn_setup()
    _L1_gnn_in = {k: v for k, v in _L1_gnn_all.items() if k in ('W1', 'att_src1', 'att_dst1', 'b1', 'W2', 'att_src2', 'att_dst2', 'b2')}
    del _L1_gnn_all
    return {'x': x, 'src': src, 'dst': dst, 'edge_type_7': edge_type_7, 'L0_gnn_gn1_w': _L0_gnn_in['gn1_w'], 'L0_gnn_gn1_b': _L0_gnn_in['gn1_b'], 'L0_gnn_conv1_w': _L0_gnn_in['conv1_w'], 'L0_gnn_gn2_w': _L0_gnn_in['gn2_w'], 'L0_gnn_gn2_b': _L0_gnn_in['gn2_b'], 'L0_gnn_conv2_w': _L0_gnn_in['conv2_w'], 'L1_gnn_W1': _L1_gnn_in['W1'], 'L1_gnn_att_src1': _L1_gnn_in['att_src1'], 'L1_gnn_att_dst1': _L1_gnn_in['att_dst1'], 'L1_gnn_b1': _L1_gnn_in['b1'], 'L1_gnn_W2': _L1_gnn_in['W2'], 'L1_gnn_att_src2': _L1_gnn_in['att_src2'], 'L1_gnn_att_dst2': _L1_gnn_in['att_dst2'], 'L1_gnn_b2': _L1_gnn_in['b2']}

def reference(x, src, dst, edge_type_7, L0_gnn_gn1_w, L0_gnn_gn1_b, L0_gnn_conv1_w, L0_gnn_gn2_w, L0_gnn_gn2_b, L0_gnn_conv2_w, L1_gnn_W1, L1_gnn_att_src1, L1_gnn_att_dst1, L1_gnn_b1, L1_gnn_W2, L1_gnn_att_src2, L1_gnn_att_dst2, L1_gnn_b2):
    import jax
    import jax.numpy as jnp

    def _L0_gnn_ref(x, gn1_w, gn1_b, conv1_w, gn2_w, gn2_b, conv2_w, edge_index, edge_type, batch_id):
        import jax, jax.numpy as jnp
        import numpy as np
        EPS = 1e-05
        BATCH_SIZE = 8
        GROUP = 32
        N_EDGE_TYPE = 7

        def dual_gn(data, batch_id, w, b):
            N, C = data.shape
            cpg = C // GROUP

            def adjust(t):
                t = t.reshape(-1, GROUP, cpg).sum(-1, keepdims=True)
                return jnp.broadcast_to(t, (t.shape[0], GROUP, cpg)).reshape(-1, C)
            ones = jnp.ones((N,), data.dtype)
            count = jax.ops.segment_sum(ones, batch_id, num_segments=BATCH_SIZE) * cpg
            inv_count = 1.0 / (count + EPS)
            mean = adjust(jax.ops.segment_sum(data, batch_id, num_segments=BATCH_SIZE) * inv_count[:, None])
            out = data - mean[batch_id]
            var = adjust(jax.ops.segment_sum(out * out, batch_id, num_segments=BATCH_SIZE) * inv_count[:, None])
            inv_std = 1.0 / jnp.sqrt(var + EPS)
            return out * inv_std[batch_id] * w + b

        def graph_conv(x, row, col, etype, W):
            N, C = x.shape
            idx = row * N_EDGE_TYPE + etype
            gathered = x[col]
            s = jax.ops.segment_sum(gathered, idx, num_segments=N * N_EDGE_TYPE)
            cnt = jax.ops.segment_sum(jnp.ones((col.shape[0],), x.dtype), idx, num_segments=N * N_EDGE_TYPE)
            col_data = s / jnp.maximum(cnt, 1.0)[:, None]
            return col_data.reshape(N, N_EDGE_TYPE * C) @ W

        def silu(x):
            return x * jax.nn.sigmoid(x)
        row, col = (edge_index[0], edge_index[1])
        h = dual_gn(x, batch_id, gn1_w, gn1_b)
        h = silu(h)
        h = graph_conv(h, row, col, edge_type, conv1_w)
        h = dual_gn(h, batch_id, gn2_w, gn2_b)
        h = silu(h)
        h = graph_conv(h, row, col, edge_type, conv2_w)
        return h + x

    def _L1_gnn_ref(x, edge_index, W1, att_src1, att_dst1, b1, W2, att_src2, att_dst2, b2):
        import jax, jax.numpy as jnp
        import numpy as np
        N = 50000
        NEG_SLOPE = 0.2

        def _gat_conv(x, src, dst, W, a_src, a_dst, b, heads, out_c):
            n = x.shape[0]
            h = (x @ W).reshape(n, heads, out_c)
            s = jnp.einsum('nhc,hc->nh', h, a_src)
            d = jnp.einsum('nhc,hc->nh', h, a_dst)
            e = jax.nn.leaky_relu(s[src] + d[dst], NEG_SLOPE)
            e_max = jax.ops.segment_max(e, dst, num_segments=n)
            e = jnp.exp(e - e_max[dst])
            denom = jax.ops.segment_sum(e, dst, num_segments=n)
            alpha = e / (denom[dst] + 1e-16)
            msg = h[src] * alpha[:, :, None]
            out = jax.ops.segment_sum(msg, dst, num_segments=n)
            return out.reshape(n, heads * out_c) + b
        n = x.shape[0]
        loop = jnp.arange(n, dtype=edge_index.dtype)
        src = jnp.concatenate([edge_index[0], loop])
        dst = jnp.concatenate([edge_index[1], loop])
        h = _gat_conv(x, src, dst, W1, att_src1, att_dst1, b1, heads=8, out_c=32)
        h = jax.nn.relu(h)
        out = _gat_conv(h, src, dst, W2, att_src2, att_dst2, b2, heads=1, out_c=256)
        return out
    edge_index = jnp.stack([src, dst])
    batch0 = jnp.zeros((3125,), jnp.int32)
    x = _layernorm(x + _L0_gnn_ref(x, L0_gnn_gn1_w, L0_gnn_gn1_b, L0_gnn_conv1_w, L0_gnn_gn2_w, L0_gnn_gn2_b, L0_gnn_conv2_w, edge_index, edge_type_7, batch0), axis=-1)
    x = _layernorm(x + _L1_gnn_ref(x, edge_index, L1_gnn_W1, L1_gnn_att_src1, L1_gnn_att_dst1, L1_gnn_b1, L1_gnn_W2, L1_gnn_att_src2, L1_gnn_att_dst2, L1_gnn_b2), axis=-1)
    return x

_drawn_inputs = setup_inputs


def setup_inputs(seed=0):
    import zlib

    import numpy as np

    out = dict(_drawn_inputs(seed))
    spreads = {'L0_gnn_gn1_w': (1.0, 0.2),
     'L0_gnn_gn1_b': (0.0, 0.1),
     'L0_gnn_gn2_w': (1.0, 0.2),
     'L0_gnn_gn2_b': (0.0, 0.289)}
    factors = {'L1_gnn_att_dst1': 8.0,
     'L1_gnn_b1': 5.48,
     'L1_gnn_att_src2': 8.0,
     'L1_gnn_att_dst2': 8.0,
     'L1_gnn_b2': 2.775}
    for name, (base, spread) in spreads.items():
        noise = np.random.default_rng([zlib.crc32(name.encode()), seed]).standard_normal(out[name].shape)
        drawn = base * np.exp(spread * noise) if base else spread * noise
        out[name] = jnp.asarray(drawn.astype(out[name].dtype))
    for name, factor in factors.items():
        out[name] = (out[name] * factor).astype(out[name].dtype)
    return out
```

```python
from contextlib import ExitStack

import concourse.bass as bass
from concourse import mybir

FP32 = mybir.dt.float32
BF16 = mybir.dt.bfloat16
FP16 = mybir.dt.float16
INT32 = mybir.dt.int32
ALU = mybir.AluOpType
ACT = mybir.ActivationFunctionType
AX = mybir.AxisListType

P = 128
NODES, CH = 3125, 256
EDGES, TYPES = 50000, 7
GROUPS = 32
HEADS = 8
HC = CH // HEADS
BLOCKS = -(-NODES // P)
LAST = NODES - (BLOCKS - 1) * P
COLS = -(-EDGES // P)
TAIL = EDGES - (P - 1) * COLS
CHUNKS = -(-(EDGES // P + BLOCKS) // 16) * 16
EXTRA = 8
TROWS = BLOCKS * P
TCODE = 4096
ACCW = CH + 3 * HEADS
HROW = CH + HEADS
EPS = 1e-5
SLOPE = 0.2
BIG = 2.0 ** 100
KC = CH // P


class Shared:
    pass


class Semaphores:

    def __init__(self, nc):
        self.nc, self.held = nc, []

    def __enter__(self):
        def sem(name):
            self.held.append(self.nc.alloc_semaphore(name=name))
            return self.held[-1]
        return sem

    def __exit__(self, *problem):
        if problem[0] is None:
            self.nc.clear_and_free_semaphores(self.held)
            self.nc.all_engine_barrier()


class Chain:

    def __init__(self, eng, sem):
        self.eng, self.sem, self.n = eng, sem, 0

    def __call__(self, ins):
        self.n += 1
        ins.then_inc(self.sem, 1)
        self.eng.wait_ge(self.sem, self.n)


def constants(nc, S, sem, src, dst, etype):
    loaded, ramps, padded, own = sem("c_loaded"), sem("c_ramps"), sem("c_padded"), sem("c_own")
    pad0, padc = 96, TAIL
    with nc.Block() as block:
        @block.sync
        def _(sp):
            sp.wait_ge(padded, 1)
            for tile, edges in ((S.src_i, src), (S.dst_i, dst), (S.type_i, etype)):
                sp.dma_start(tile[0:P - 1, :], edges[0:(P - 1) * COLS].rearrange("(p c) -> p c", c=COLS)).then_inc(loaded, 16)
                sp.dma_start(tile[P - 1:P, 0:TAIL], edges[(P - 1) * COLS:EDGES].rearrange("(a c) -> a c", a=1)).then_inc(loaded, 16)
            sp.wait_ge(loaded, 96)

        @block.gpsimd
        def _(pool):
            pool.iota(S.col_i[:, :], [[1, CHUNKS + EXTRA]], channel_multiplier=0).then_inc(ramps, 1)
            pool.iota(S.row_i[:, :], [[0, 1]], channel_multiplier=1).then_inc(ramps, 1)

        @block.vector
        def _(v):
            step = Chain(v, own)
            for n, tile in enumerate((S.src_i, S.dst_i, S.type_i)):
                ins = v.memset(tile[pad0:P, padc:COLS], 8191)
                if n == 2:
                    ins.then_inc(padded, 1)
            v.wait_ge(ramps, 2)
            v.tensor_copy(S.col_h[:, :], S.col_i[:, 0:CHUNKS])
            step(v.tensor_copy(S.row[:, :], S.row_i[:, :]))
            step(v.tensor_copy(S.col[:, :], S.col_i[:, :]))
            v.tensor_scalar(S.ident[:, :], S.col[:, 0:P], S.row[:, 0:1], None, ALU.is_equal)
            v.tensor_scalar(S.ident_b[:, :], S.col[:, 0:P], S.row[:, 0:1], None, ALU.is_equal)
            v.tensor_scalar(S.above[:, :], S.col[:, 0:P], S.row[:, 0:1], None, ALU.is_gt)
            v.tensor_scalar(S.down[:, :], S.col[:, 0:P], -float(HEADS), S.row[:, 0:1], ALU.add, ALU.is_equal)
            v.tensor_scalar(S.up[:, :], S.col[:, 0:P], float(HEADS), S.row[:, 0:1], ALU.add, ALU.is_equal)
            v.memset(S.ones[:, :], 1.0)


def place_edges(nc, S, sem, name, key_i, payload, pay_shift, decode):
    U = 17
    ITERS = COLS // U
    assert ITERS * U == COLS
    own, counted, summed = sem(name + "own"), sem(name + "counted"), sem(name + "summed")
    spread, moved = sem(name + "spread"), sem(name + "moved")
    with ExitStack() as ctx:
        def sb(n, shape, dt):
            return ctx.enter_context(nc.sbuf_tensor(name + n, shape, dt))

        def pb(n, shape):
            return ctx.enter_context(nc.psum_tensor(name + n, shape, FP32))
        ti, tj = sb("ti", [P, COLS], INT32), sb("tj", [P, COLS], INT32)
        blk, lo, hi = (sb(n, [P, COLS], FP32) for n in ("blk", "lo", "hi"))
        mask, run, pos = (sb(n, [P, COLS], FP32) for n in ("mask", "run", "pos"))
        lane, chunk = sb("lane", [P, COLS], FP32), sb("chunk", [P, COLS], FP32)
        cnt, base, tot, first, incl = (sb(n, [P, BLOCKS], FP32) for n in ("cnt", "base", "tot", "first", "incl"))
        nch_i = sb("nch_i", [P, BLOCKS], INT32)
        highs, lows = sb("highs", [P, U, P], FP16), sb("lows", [P, U, P], FP16)
        chunks = sb("chunks", [P, U, CHUNKS], FP16)
        ci, cj = sb("ci", [P, CHUNKS], INT32), sb("cj", [P, CHUNKS], INT32)
        cf, cg = sb("cf", [P, CHUNKS], FP32), sb("cg", [P, CHUNKS], FP32)
        p_cnt = pb("p_cnt", [P, 2 * BLOCKS])
        p_hi, p_lo = pb("p_hi", [P, CHUNKS]), pb("p_lo", [P, CHUNKS])
        with nc.Block() as block:
            @block.vector
            def _(v):
                step = Chain(v, own)
                step(v.tensor_scalar(ti[:, :], key_i[:, :], 7, None, ALU.logical_shift_right))
                step(v.tensor_copy(blk[:, :], ti[:, :]))
                step(v.tensor_scalar(ti[:, :], key_i[:, :], P - 1, None, ALU.bitwise_and))
                step(v.tensor_copy(lane[:, :], ti[:, :]))
                payload(v, step, lo)
                step(v.scalar_tensor_tensor(pos[:, :], lane[:, :], float(1 << pay_shift), lo[:, :], ALU.mult, ALU.add))
                step(v.tensor_copy(ti[:, :], pos[:, :]))
                step(v.tensor_scalar(tj[:, :], ti[:, :], 11, None, ALU.logical_shift_right))
                step(v.tensor_scalar(ti[:, :], ti[:, :], 2047, None, ALU.bitwise_and))
                v.tensor_copy(hi[:, :], tj[:, :])
                step(v.tensor_copy(lo[:, :], ti[:, :]))
                at = step.n
                with v.Fori(0, BLOCKS) as b:
                    v.tensor_scalar(mask[:, :], blk[:, :], S.col[:, bass.ds(b, 1)], 0.0, ALU.is_equal, ALU.add,
                                    accum_out=cnt[:, bass.ds(b, 1)]).then_inc(own, 1)
                    v.wait_ge(own, b + (at + 1))
                step.n += BLOCKS
                v.memset(pos[:, :], 0.0)
                v.memset(S.block_of[:, :], 0.0).then_inc(counted, 1)
                v.wait_ge(summed, 1)
                step(v.tensor_scalar(tot[:, :], p_cnt[:, 0:BLOCKS], float(P - 1), None, ALU.add))
                step(v.tensor_copy(nch_i[:, :], tot[:, :]))
                step(v.tensor_scalar(nch_i[:, :], nch_i[:, :], 7, None, ALU.logical_shift_right))
                step(v.tensor_copy(tot[:, :], nch_i[:, :]))
                step(v.tensor_tensor_scan(incl[:, :], tot[:, :], tot[:, :], 0.0, ALU.add, ALU.max))
                step(v.tensor_tensor(first[:, :], incl[:, :], tot[:, :], ALU.subtract))
                step(v.scalar_tensor_tensor(base[:, :], first[:, :], float(P), p_cnt[:, BLOCKS:2 * BLOCKS], ALU.mult, ALU.add))
                at = step.n
                with v.Fori(0, BLOCKS - 1) as b:
                    v.scalar_tensor_tensor(S.block_of[:, :], S.col[:, :], first[:, bass.ds(b + 1, 1)],
                                           S.block_of[:, :], ALU.is_ge, ALU.add).then_inc(own, 1)
                    v.wait_ge(own, b + (at + 1))
                step.n += BLOCKS - 1
                at = step.n
                with v.Fori(0, BLOCKS) as b:
                    v.tensor_scalar(mask[:, :], blk[:, :], S.col[:, bass.ds(b, 1)], None, ALU.is_equal).then_inc(own, 1)
                    v.wait_ge(own, b * 4 + (at + 1))
                    v.tensor_tensor_scan(run[:, :], mask[:, :], mask[:, :], base[:, bass.ds(b, 1)], ALU.add, ALU.max).then_inc(own, 1)
                    v.wait_ge(own, b * 4 + (at + 2))
                    v.tensor_tensor(run[:, :], run[:, :], mask[:, :], ALU.mult).then_inc(own, 1)
                    v.wait_ge(own, b * 4 + (at + 3))
                    v.tensor_tensor(pos[:, :], pos[:, :], run[:, :], ALU.add).then_inc(own, 1)
                    v.wait_ge(own, b * 4 + (at + 4))
                step.n += 4 * BLOCKS
                step(v.tensor_scalar(pos[:, :], pos[:, :], -1.0, None, ALU.add))
                step(v.tensor_copy(ti[:, :], pos[:, :]))
                step(v.tensor_scalar(tj[:, :], ti[:, :], P - 1, None, ALU.bitwise_and))
                step(v.tensor_scalar(ti[:, :], ti[:, :], 7, None, ALU.arith_shift_right))
                v.tensor_copy(lane[:, :], tj[:, :])
                step(v.tensor_copy(chunk[:, :], ti[:, :]))

                def column(c, u):
                    e = bass.ds(c, 1)
                    v.tensor_scalar(highs[:, u, :], S.col_h[:, 0:P], lane[:, e], hi[:, e], ALU.is_equal, ALU.mult)
                    v.tensor_scalar(lows[:, u, :], S.col_h[:, 0:P], lane[:, e], lo[:, e], ALU.is_equal, ALU.mult)
                    v.tensor_scalar(chunks[:, u, :], S.col_h[:, :], chunk[:, e], None, ALU.is_equal).then_inc(spread, 1)
                for u in range(U):
                    column(u, u)
                with v.Fori(1, ITERS) as i:
                    for u in range(U):
                        v.wait_ge(moved, i * U + (u + 1 - U))
                        column(i * U + u, u)
                v.wait_ge(moved, COLS)
                step(v.tensor_copy(cf[:, :], p_lo[:, :]))
                step(v.scalar_tensor_tensor(cf[:, :], p_hi[:, :], 2048.0, cf[:, :], ALU.mult, ALU.add))
                step(v.tensor_copy(ci[:, :], cf[:, :]))
                step(v.tensor_scalar(cj[:, :], ci[:, :], pay_shift, None, ALU.logical_shift_right))
                step(v.tensor_copy(cg[:, :], cj[:, :]))
                step(v.tensor_scalar(cf[:, :], cf[:, :], 0.0, None, ALU.is_gt))
                step(v.scalar_tensor_tensor(cg[:, :], cg[:, :], 1.0, cf[:, :], ALU.add, ALU.mult))
                v.memset(S.local[:, CHUNKS:], -1.0)
                step(v.tensor_scalar(S.local[:, 0:CHUNKS], cg[:, :], -1.0, None, ALU.add))
                v.memset(S.local_b[:, CHUNKS:], -1.0)
                v.tensor_copy(S.local_b[:, 0:CHUNKS], S.local[:, 0:CHUNKS])
                v.tensor_scalar(S.acc_at[0:1, :], S.block_of[0:1, :], float(ACCW), None, ALU.mult)
                v.tensor_scalar(S.block_hot[0:BLOCKS, :], S.block_of[0:BLOCKS, 0:CHUNKS], S.row[0:BLOCKS, 0:1], None, ALU.is_equal)
                decode(v, step, ci, cj, cf)

            @block.tensor
            def _(pe):
                pe.wait_ge(counted, 1)
                pe.matmul(p_cnt[:, 0:BLOCKS], S.ones[:, :], cnt[:, :], start=True, stop=True)
                pe.matmul(p_cnt[:, BLOCKS:2 * BLOCKS], S.above[:, :], cnt[:, :], start=True, stop=True).then_inc(summed, 1)

                def column(u, start, stop):
                    pe.matmul(p_hi[:, :], highs[:, u, :], chunks[:, u, :], start=start, stop=stop)
                    pe.matmul(p_lo[:, :], lows[:, u, :], chunks[:, u, :], start=start, stop=stop).then_inc(moved, 1)
                for u in range(U):
                    pe.wait_ge(spread, u + 1)
                    column(u, u == 0, False)
                with pe.Fori(1, ITERS - 1) as i:
                    for u in range(U):
                        pe.wait_ge(spread, i * U + (u + 1))
                        column(u, False, False)
                for u in range(U):
                    pe.wait_ge(spread, COLS - U + u + 1)
                    column(u, False, u == U - 1)


def place_by_src(nc, S, sem):
    def payload(v, step, out):
        step(v.tensor_copy(S.pay[:, :], S.type_i[:, :]))
        step(v.tensor_copy(out[:, :], S.dst_i[:, :]))
        step(v.tensor_scalar(out[:, :], out[:, :], 1.0, None, ALU.add))
        step(v.scalar_tensor_tensor(out[:, :], S.pay[:, :], float(TCODE), out[:, :], ALU.mult, ALU.add))

    def decode(v, step, code, ti, tf):
        step(v.tensor_scalar(ti[:, :], code[:, :], 12, 7, ALU.logical_shift_right, ALU.bitwise_and))
        step(v.tensor_copy(S.etype[:, :], ti[:, :]))
        step(v.tensor_scalar(code[:, :], code[:, :], (1 << 15) - 1, None, ALU.bitwise_and))
        step(v.tensor_copy(tf[:, :], code[:, :]))
        step(v.scalar_tensor_tensor(tf[:, :], S.etype[:, :], float(TROWS - TCODE), tf[:, :], ALU.mult, ALU.add))
        v.tensor_scalar(S.take[:, :], tf[:, :], -1.0, 0.0, ALU.add, ALU.max)
    place_edges(nc, S, sem, "ps_", S.src_i, payload, 15, decode)


def place_by_dst(nc, S, sem):
    def payload(v, step, out):
        step(v.tensor_copy(out[:, :], S.src_i[:, :]))
        step(v.tensor_scalar(out[:, :], out[:, :], 1.0, None, ALU.add))

    def decode(v, step, code, ti, tf):
        step(v.tensor_scalar(ti[:, :], code[:, :], 4095, None, ALU.bitwise_and))
        step(v.tensor_copy(tf[:, :], ti[:, :]))
        v.tensor_scalar(S.take[:, :], tf[:, :], -1.0, 0.0, ALU.add, ALU.max)
    place_edges(nc, S, sem, "pd_", S.dst_i, payload, 12, decode)



GRP = 8
PAIR = 2 * GRP


def hot_and_add(nc, S, v, own, hot, hot_dt_col, weight, acc, width, banks, hot_ready, added, done):
    regs = [v.alloc_register(f"{own}_at{u}") for u in range(GRP)]

    def onehot(c, slot):
        if weight is None:
            ins = v.tensor_scalar(hot[:, slot, :], hot_dt_col, S.local[:, bass.ds(c, 1)], None, ALU.is_equal)
        else:
            ins = v.tensor_scalar(hot[:, slot, :], hot_dt_col, S.local[:, bass.ds(c, 1)], weight[:, bass.ds(c, 1)],
                                  ALU.is_equal, ALU.mult)
        ins.then_inc(hot_ready, 1)
    v.sem_inc(added, GRP)
    for u in range(GRP):
        onehot(u, u)
    with v.Fori(0, CHUNKS // PAIR) as i:
        for h in range(2):
            first = i * PAIR + GRP * h
            v.load(regs, S.acc_at[0:1, bass.ds(first, GRP)])
            at = [v.snap(r, min_val=0, max_val=(BLOCKS - 1) * ACCW) for r in regs]
            v.wait_ge(done, first + PAIR)
            for u in range(GRP):
                onehot(first + (GRP + u), GRP * (1 - h) + u)
                v.wait_ge(done, first + (PAIR + u + 1))
                v.wait_ge(added, first + (GRP + u))
                part = acc[:, bass.ds(at[u], width)]
                v.tensor_tensor(part, part, banks[u][:, 0:width], ALU.add).then_inc(added, 1)


def count_types(nc, S, sem, acc, types):
    hot_ready, added, done, masks = sem("ct_hot"), sem("ct_added"), sem("ct_done"), sem("ct_masks")
    with ExitStack() as ctx:
        hot = ctx.enter_context(nc.sbuf_tensor("ct_hots", [P, PAIR, P], BF16))
        banks = [ctx.enter_context(nc.psum_tensor(f"ct_bank{u}", [P, 512], FP32)) for u in range(GRP)]
        with nc.Block() as block:
            @block.vector
            def _(v):
                for t in range(TYPES):
                    v.tensor_scalar(types[:, :, t], S.etype[:, :], float(t), None, ALU.is_equal)
                v.memset(acc[:, :], 0.0).then_inc(masks, 1)
                v.wait_ge(masks, 1)
                hot_and_add(nc, S, v, "ct", hot, S.col[:, 0:P], None, acc, TYPES, banks, hot_ready, added, done)

            @block.tensor
            def _(pe):
                pe.sem_inc(done, PAIR)
                pe.wait_ge(masks, 1)
                with pe.Fori(0, CHUNKS // PAIR) as i:
                    for u in range(PAIR):
                        pe.wait_ge(hot_ready, i * PAIR + (u + 1))
                        pe.wait_ge(added, i * PAIR + (u + 1))
                        pe.matmul(banks[u % GRP][:, 0:TYPES], hot[:, u, :], types[:, bass.ds(i * PAIR + u, 1), :].rearrange("p a t -> p (a t)"),
                                  start=True, stop=True).then_inc(done, 1)


def look_up(nc, S, sem, name, table, width, result):
    turned, turned_out = sem(name + "turned"), sem(name + "turned_out")
    spread, spread_out = sem(name + "spread"), sem(name + "spread_out")
    rows, hot_ready, found, stored = sem(name + "rows"), sem(name + "hot"), sem(name + "found"), sem(name + "stored")
    G4 = 4
    with ExitStack() as ctx:
        def sb(n, shape, dt):
            return ctx.enter_context(nc.sbuf_tensor(name + n, shape, dt))

        def pb(n, shape):
            return ctx.enter_context(nc.psum_tensor(name + n, shape, FP32))
        tt = sb("tt", [32, width, P], FP32)
        per_chunk = sb("per_chunk", [P, CHUNKS, width], FP32)
        hot = [sb(f"hot{n}", [P, G4 * P], FP32) for n in range(2)]
        p_a = [pb(f"a{n}", [P, 512]) for n in range(2)]
        p_row = [pb(f"row{n}", [P, 512]) for n in range(2)]
        p_out = [pb(f"out{n}", [P, 512]) for n in range(2)]
        with nc.Block() as block:
            @block.tensor
            def _(pe):
                for w in range(width):
                    if w >= 2:
                        pe.wait_ge(turned_out, w - 1)
                    pe.transpose(p_a[w % 2][0:BLOCKS, 0:P], table[:, :, w], S.ident[:, :]).then_inc(turned, 1)
                for w in range(width):
                    pe.wait_ge(turned_out, w + 1)
                    if w >= 2:
                        pe.wait_ge(spread_out, w - 1)
                    pe.matmul(p_row[w % 2][:, 0:CHUNKS], tt[0:BLOCKS, w, :], S.block_hot[0:BLOCKS, :], start=True, stop=True).then_inc(spread, 1)
                pe.wait_ge(spread_out, width)

                def rows_of(g, c):
                    for j in range(G4):
                        ins = pe.matmul(p_row[g % 2][:, j * P:(j + 1) * P], S.local_b[:, bass.ds(c + j, 1)].to_broadcast([P, P]),
                                        S.ident_b[:, :], start=True, stop=True)
                    ins.then_inc(rows, 1)
                rows_of(0, 0)
                pe.sem_inc(found, 2)
                with pe.Fori(0, CHUNKS // 32) as i:
                    for h in range(2):
                        pe.wait_ge(stored, i * 2 + (h + 1))
                        for q in range(4):
                            g = 4 * h + q
                            pe.wait_ge(hot_ready, i * 8 + (g + 1))
                            rows_of(g + 1, i * 32 + 4 * (g + 1))
                            pe.wait_ge(hot_ready, i * 8 + (g + 2))
                            for j in range(G4):
                                c = q * G4 + j
                                ins = pe.matmul(p_out[h][:, c * width:(c + 1) * width], hot[g % 2][:, j * P:(j + 1) * P],
                                                per_chunk[:, bass.ds(i * 32 + (h * 16 + c), 1), :].rearrange("p a t -> p (a t)"), start=True, stop=True)
                            ins.then_inc(found, 1)

            @block.vector
            def _(v):
                v.sem_inc(hot_ready, 1)
                with v.Fori(0, CHUNKS // 32) as i:
                    for g in range(8):
                        v.wait_ge(rows, i * 8 + (g + 1))
                        v.wait_ge(found, i * 8 + (g + 1))
                        v.tensor_scalar(hot[g % 2][:, :], p_row[g % 2][:, :], S.row[:, 0:1], None, ALU.is_equal).then_inc(hot_ready, 1)

            @block.scalar
            def _(act):
                for w in range(width):
                    act.wait_ge(turned, w + 1)
                    act.copy(tt[0:BLOCKS, w, :], p_a[w % 2][0:BLOCKS, 0:P]).then_inc(turned_out, 1)
                for w in range(width):
                    act.wait_ge(spread, w + 1)
                    act.copy(per_chunk[:, :, w], p_row[w % 2][:, 0:CHUNKS]).then_inc(spread_out, 1)
                act.sem_inc(stored, 2)
                with act.Fori(0, CHUNKS // 32) as i:
                    for h in range(2):
                        act.wait_ge(found, i * 8 + (4 * h + 6))
                        act.copy(result[:, bass.ds(i * 32 + 16 * h, 16), :],
                                 p_out[h][:, 0:16 * width].rearrange("p (c w) -> p c w", w=width)).then_inc(stored, 1)


def type_weights(nc, S, sem, acc):
    own = sem("tw_own")
    with ExitStack() as ctx:
        types = ctx.enter_context(nc.sbuf_tensor("types", [P, CHUNKS, TYPES], BF16))
        table = ctx.enter_context(nc.sbuf_tensor("tw_table", [P, BLOCKS, TYPES], FP32))
        each = ctx.enter_context(nc.sbuf_tensor("tw_each", [P, CHUNKS, TYPES], FP32))
        count_types(nc, S, sem, acc, types)
        with nc.Block() as block:
            @block.vector
            def _(v):
                step = Chain(v, own)
                counts = acc[:, :].rearrange("p (b w) -> p b w", w=ACCW)[:, :, 0:TYPES]
                step(v.tensor_scalar(table[:, :, :], counts, 1.0, None, ALU.max))
                step(v.reciprocal(table[:, :, :], table[:, :, :]))
        look_up(nc, S, sem, "tw_", table, TYPES, each)
        with nc.Block() as block:
            @block.vector
            def _(v):
                at = own
                v.tensor_tensor(each[:, :, :], each[:, :, :], types[:, :, :], ALU.mult).then_inc(at, 1)
                v.memset(S.weight[:, CHUNKS:], 0.0)
                v.wait_ge(at, 3)
                v.tensor_reduce(S.weight[:, 0:CHUNKS], each[:, :, :], AX.X, ALU.add)


def gather_and_add(nc, S, sem, name, table, acc, round_of_gathers):
    hot_ready, added, done, cleared = sem(name + "hot"), sem(name + "added"), sem(name + "done"), sem(name + "cleared")
    index_ready, passed = sem(name + "index"), sem(name + "passed")
    arrived, before = S.arrived, round_of_gathers * (CHUNKS // PAIR) * 16
    with ExitStack() as ctx:
        hot = ctx.enter_context(nc.sbuf_tensor(name + "hots", [P, PAIR, P], FP32))
        rows = ctx.enter_context(nc.sbuf_tensor(name + "rows", [P, PAIR, CH], FP32))
        index = ctx.enter_context(nc.sbuf_tensor(name + "indices", [P, PAIR], INT32))
        banks = [ctx.enter_context(nc.psum_tensor(f"{name}bank{u}", [P, 512], FP32)) for u in range(GRP)]
        with nc.Block() as block:
            @block.gpsimd
            def _(pool):
                with pool.Fori(0, CHUNKS // PAIR) as i:
                    for u in range(PAIR):
                        if u % GRP == 0:
                            pool.wait_ge(done, i * PAIR + (u + GRP))
                            pool.sem_inc(passed, 1)
                            pool.tensor_copy(index[:, u:u + GRP], S.take[:, bass.ds(i * PAIR + u, GRP)]).then_inc(index_ready, 1)
                            pool.wait_ge(index_ready, i * 2 + (u // GRP + 1))
                            pool.sem_inc(passed, 1)
                        pool.indirect_dma_start(rows[:, u, :], None, table, bass.IndirectOffsetOnAxis(ap=index[:, u:u + 1], axis=0)).then_inc(arrived[u], 16)

            @block.vector
            def _(v):
                v.memset(acc[:, :], 0.0).then_inc(cleared, 1)
                v.wait_ge(cleared, 1)
                hot_and_add(nc, S, v, name, hot, S.col[:, 0:P], S.weight, acc, CH, banks, hot_ready, added, done)

            @block.tensor
            def _(pe):
                pe.sem_inc(done, PAIR)
                with pe.Fori(0, CHUNKS // PAIR) as i:
                    for u in range(PAIR):
                        pe.wait_ge(hot_ready, i * PAIR + (u + 1))
                        pe.wait_ge(added, i * PAIR + (u + 1))
                        pe.wait_ge(arrived[u], i * 16 + (before + 16))
                        pe.matmul(banks[u % GRP][:, 0:CH], hot[:, u, :], rows[:, u, :], start=True, stop=True).then_inc(done, 1)


def blocks_of(tile):
    return tile[:, :].rearrange("p (b w) -> p b w", b=BLOCKS)


def over_blocks(row):
    return row.unsqueeze(1).to_broadcast([P, BLOCKS, row.shape[1]])


def group_norm(nc, S, sem, name, feat, norm, gn_w, gn_b):
    loaded, own, summed, centered, squared, rooted = (sem(name + n) for n in ("loaded", "own", "summed", "centered", "squared", "rooted"))
    with ExitStack() as ctx:
        sq = ctx.enter_context(nc.sbuf_tensor(name + "sq", [P, BLOCKS, CH], FP32))
        grp = ctx.enter_context(nc.sbuf_tensor(name + "grp", [P, GROUPS], FP32))
        eps = ctx.enter_context(nc.sbuf_tensor(name + "eps", [P, 1], FP32))
        scale = ctx.enter_context(nc.sbuf_tensor(name + "scale", [P, CH], FP32))
        bias = ctx.enter_context(nc.sbuf_tensor(name + "bias", [P, CH], FP32))
        sums = [ctx.enter_context(nc.psum_tensor(f"{name}sums{n}", [P, CH], FP32)) for n in range(2)]
        inv_count = 1.0 / (NODES * (CH // GROUPS) + EPS)
        with nc.Block() as block:
            @block.sync
            def _(sp):
                sp.dma_start(scale[:, :], gn_w[0, :].partition_broadcast(P)).then_inc(loaded, 16)
                sp.dma_start(bias[:, :], gn_b[0, :].partition_broadcast(P)).then_inc(loaded, 16)
                sp.wait_ge(loaded, 32)

            @block.tensor
            def _(pe):
                def column_sums(out, x):
                    pe.matmul(out, S.ones[:, :], x[:, 0, :], start=True, stop=False)
                    with pe.Fori(1, BLOCKS - 1) as b:
                        pe.matmul(out, S.ones[:, :], x[:, bass.ds(b, 1), :].rearrange("p a c -> p (a c)"), start=False, stop=False)
                    pe.matmul(out, S.ones[0:LAST, :], x[0:LAST, BLOCKS - 1, :], start=False, stop=True).then_inc(summed, 1)
                column_sums(sums[0][:, :], feat)
                pe.wait_ge(squared, 1)
                column_sums(sums[1][:, :], sq)

            @block.scalar
            def _(act):
                act.wait_ge(centered, 1)
                act.activation(sq[:, :, :], norm[:, :, :], ACT.Square).then_inc(squared, 1)
                act.wait_ge(centered, 2)
                act.activation(grp[:, :], grp[:, :], ACT.Sqrt, bias=eps[:, 0:1]).then_inc(rooted, 1)

            @block.vector
            def _(v):
                step = Chain(v, own)
                v.memset(eps[:, :], EPS)
                for n in range(2):
                    v.wait_ge(summed, n + 1)
                    step(v.tensor_reduce(grp[:, :], sums[n][:, :].rearrange("p (g c) -> p g c", g=GROUPS), AX.X, ALU.add))
                    if n == 0:
                        step(v.tensor_scalar(grp[:, :], grp[:, :], inv_count, None, ALU.mult))
                        mean = grp[:, :].unsqueeze(1).unsqueeze(3).to_broadcast([P, BLOCKS, GROUPS, CH // GROUPS])
                        v.tensor_tensor(norm[:, :, :].rearrange("p b (g c) -> p b g c", g=GROUPS),
                                        feat.rearrange("p b (g c) -> p b g c", g=GROUPS), mean, ALU.subtract).then_inc(centered, 1)
                        v.wait_ge(centered, 1)
                    else:
                        v.tensor_scalar(grp[:, :], grp[:, :], inv_count, None, ALU.mult).then_inc(centered, 1)
                v.wait_ge(rooted, 1)
                step(v.reciprocal(grp[:, :], grp[:, :]))
                v.wait_ge(loaded, 32)
                sc = scale[:, :].rearrange("p (g c) -> p g c", g=GROUPS)
                step(v.tensor_tensor(sc, sc, grp[:, :].unsqueeze(2).to_broadcast([P, GROUPS, CH // GROUPS]), ALU.mult))
                step(v.tensor_tensor(norm[:, :, :], norm[:, :, :], over_blocks(scale[:, :]), ALU.mult))
                v.tensor_tensor(norm[:, :, :], norm[:, :, :], over_blocks(bias[:, :]), ALU.add)


def typed_features(nc, S, sem, name, norm, conv_w, table):
    U = 5
    QUARTS = [(0, 512), (512, 512), (1024, 512), (1536, 256)]
    W = TYPES * CH
    loaded, acted, turned, turned_out, made = (sem(name + n) for n in ("loaded", "acted", "turned", "turned_out", "made"))
    out_v, out_a = sem(name + "out_v"), sem(name + "out_a")
    stored = [sem(f"{name}stored{n}") for n in range(U)]
    with ExitStack() as ctx:
        def sb(n, shape, dt=FP32):
            return ctx.enter_context(nc.sbuf_tensor(name + n, shape, dt))
        w_sb = sb("w", [P, KC, TYPES, CH])
        h = [sb(f"h{u}", [P, CH]) for u in range(U)]
        ht = [sb(f"ht{u}", [P, KC * P]) for u in range(U)]
        y = [sb(f"y{u}", [P, W]) for u in range(U)]
        p_t = [ctx.enter_context(nc.psum_tensor(f"{name}t{n}", [P, KC * P], FP32)) for n in range(2)]
        p_y = [ctx.enter_context(nc.psum_tensor(f"{name}py{n}", [P, 512], FP32)) for n in range(4)]
        out_rows = table.rearrange("(t n) c -> n t c", t=TYPES)
        with nc.Block() as block:
            @block.sync
            def _(sp):
                for k in range(KC):
                    sp.dma_start(w_sb[:, k, :, :], conv_w.rearrange("(t k p) n -> k p t n", t=TYPES, k=KC)[k]).then_inc(loaded, 16)
                for u in range(U):
                    sp.sem_inc(stored[u], 16)
                with sp.Fori(0, BLOCKS // U) as i:
                    for u in range(U):
                        sp.wait_ge(out_v, (i * U + (u + 2)) * 2)
                        sp.wait_ge(out_a, (i * U + (u + 2)) * 2)
                        sp.dma_start(out_rows[bass.ds((i * U + u) * P, P), :, :], y[u][:, :].rearrange("p (t c) -> p t c", t=TYPES)).then_inc(stored[u], 16)
                for u in range(U):
                    sp.wait_ge(stored[u], 16 * (BLOCKS // U + 1))

            @block.vector
            def _(v):
                v.sem_inc(out_v, 2)
                with v.Fori(0, BLOCKS // U) as i:
                    for u in range(U):
                        v.wait_ge(turned, i * U + (u + 1))
                        v.tensor_copy(ht[u][:, :], p_t[u % 2][:, :]).then_inc(turned_out, 1)
                        v.wait_ge(stored[u], i * 16 + 16)
                        for q in range(2):
                            v.wait_ge(made, (i * U + u) * 4 + (q + 1))
                            a, n = QUARTS[q]
                            v.tensor_copy(y[u][:, a:a + n], p_y[q][:, 0:n]).then_inc(out_v, 1)

            @block.scalar
            def _(act):
                def silu(b, u):
                    act.activation(h[u][:, :], norm[:, bass.ds(b, 1), :].rearrange("p a c -> p (a c)"), ACT.Silu).then_inc(acted, 1)

                def copy_out(i, u):
                    act.wait_ge(stored[u], i * 16 + 16)
                    for q in range(2, 4):
                        act.wait_ge(made, (i * U + u) * 4 + (q + 1))
                        a, n = QUARTS[q]
                        act.copy(y[u][:, a:a + n], p_y[q][:, 0:n]).then_inc(out_a, 1)
                act.sem_inc(out_a, 2)
                for u in range(U):
                    silu(u, u)
                with act.Fori(0, BLOCKS // U - 1) as i:
                    for u in range(U):
                        copy_out(i, u)
                        act.wait_ge(turned, i * U + (u + 1))
                        silu(i * U + (u + U), u)
                for u in range(U):
                    copy_out(BLOCKS // U - 1, u)

            @block.tensor
            def _(pe):
                pe.wait_ge(loaded, 16 * KC)
                with pe.Fori(0, BLOCKS // U) as i:
                    for u in range(U):
                        pe.wait_ge(acted, i * U + (u + 1))
                        for k in range(KC):
                            ins = pe.transpose(p_t[u % 2][:, k * P:(k + 1) * P], h[u][:, k * P:(k + 1) * P], S.ident[:, :])
                        ins.then_inc(turned, 1)
                        pe.wait_ge(turned_out, i * U + (u + 1))
                        for q, (a, n) in enumerate(QUARTS):
                            pe.wait_ge(out_v if q < 2 else out_a, (i * U + (u + 1)) * 2)
                            for k in range(KC):
                                ins = pe.matmul(p_y[q][:, 0:n], ht[u][:, k * P:(k + 1) * P],
                                                w_sb[:, k, :, :].rearrange("p t n -> p (t n)")[:, a:a + n], start=(k == 0), stop=(k == KC - 1))
                            ins.then_inc(made, 1)


def layer_norm(nc, S, sem, name, x):
    own, centered, squared, rooted = (sem(name + n) for n in ("own", "centered", "squared", "rooted"))
    with ExitStack() as ctx:
        sq = ctx.enter_context(nc.sbuf_tensor(name + "sq", [P, BLOCKS, CH], FP32))
        mean = ctx.enter_context(nc.sbuf_tensor(name + "mean", [P, BLOCKS], FP32))
        eps = ctx.enter_context(nc.sbuf_tensor(name + "eps", [P, 1], FP32))

        def wide(stat):
            return stat[:, :].unsqueeze(2).to_broadcast([P, BLOCKS, CH])
        with nc.Block() as block:
            @block.vector
            def _(v):
                step = Chain(v, own)
                v.memset(eps[:, :], EPS)
                step(v.tensor_reduce(mean[:, :], x[:, :, :], AX.X, ALU.add))
                step(v.tensor_scalar(mean[:, :], mean[:, :], 1.0 / CH, None, ALU.mult))
                v.tensor_tensor(x[:, :, :], x[:, :, :], wide(mean), ALU.subtract).then_inc(centered, 1)
                v.wait_ge(squared, 1)
                step(v.tensor_reduce(mean[:, :], sq[:, :, :], AX.X, ALU.add))
                v.tensor_scalar(mean[:, :], mean[:, :], 1.0 / CH, None, ALU.mult).then_inc(centered, 1)
                v.wait_ge(rooted, 1)
                step(v.reciprocal(mean[:, :], mean[:, :]))
                v.tensor_tensor(x[:, :, :], x[:, :, :], wide(mean), ALU.mult)

            @block.scalar
            def _(act):
                act.wait_ge(centered, 1)
                act.activation(sq[:, :, :], x[:, :, :], ACT.Square).then_inc(squared, 1)
                act.wait_ge(centered, 2)
                act.activation(mean[:, :], mean[:, :], ACT.Sqrt, bias=eps[:, 0:1]).then_inc(rooted, 1)


def attention_features(nc, S, sem, name, x, w, a_src, a_dst, heads, h, own_scores, table):
    U = 5
    loaded, copied, turned, turned_out, made, made_out, own, stored = (
        sem(name + n) for n in ("loaded", "copied", "turned", "turned_out", "made", "made_out", "own", "stored"))
    with ExitStack() as ctx:
        def sb(n, shape, dt=FP32):
            return ctx.enter_context(nc.sbuf_tensor(name + n, shape, dt))
        w_sb = sb("w", [P, KC, CH])
        a_sb = sb("a", [P, 2, CH])
        xs = [sb(f"x{u}", [P, CH]) for u in range(U)]
        xt = [sb(f"xt{u}", [P, KC * P]) for u in range(U)]
        prod = sb("prod", [P, BLOCKS, CH])
        p_t = [ctx.enter_context(nc.psum_tensor(f"{name}t{n}", [P, KC * P], FP32)) for n in range(2)]
        p_h = [ctx.enter_context(nc.psum_tensor(f"{name}h{n}", [P, CH], FP32)) for n in range(2)]
        with nc.Block() as block:
            @block.sync
            def _(sp):
                sp.dma_start(w_sb[:, :, :], w.rearrange("(k p) n -> p k n", k=KC)).then_inc(loaded, 16)
                for n, a in enumerate((a_src, a_dst)):
                    sp.dma_start(a_sb[:, n, :], a.rearrange("h c -> (h c)").partition_broadcast(P)).then_inc(loaded, 16)
                sp.wait_ge(own, 3 if heads == 1 else 2)
                sp.dma_start(table.rearrange("(b p) c -> p b c", p=P), h[:, :, :]).then_inc(stored, 16)
                sp.wait_ge(stored, 16)

            @block.scalar
            def _(act):
                def stage(b, u):
                    act.copy(xs[u][:, :], x[:, bass.ds(b, 1), :].rearrange("p a c -> p (a c)")).then_inc(copied, 1)

                def copy_out(b, n):
                    act.wait_ge(made, b + 1)
                    act.copy(h[:, bass.ds(b, 1), 0:CH].rearrange("p a c -> p (a c)"), p_h[n][:, :]).then_inc(made_out, 1)
                act.sem_inc(made_out, 1)
                for u in range(U):
                    stage(u, u)
                with act.Fori(0, BLOCKS // U - 1) as i:
                    for u in range(U):
                        copy_out(i * U + u, 0 if u % 2 else 1)
                        act.wait_ge(turned, i * U + (u + 1))
                        stage(i * U + (u + U), u)
                for u in range(U):
                    copy_out(BLOCKS - U + u, 0 if u % 2 else 1)

            @block.tensor
            def _(pe):
                pe.wait_ge(loaded, 48)
                with pe.Fori(0, BLOCKS // U) as i:
                    for u in range(U):
                        pe.wait_ge(copied, i * U + (u + 1))
                        for k in range(KC):
                            ins = pe.transpose(p_t[u % 2][:, k * P:(k + 1) * P], xs[u][:, k * P:(k + 1) * P], S.ident[:, :])
                        ins.then_inc(turned, 1)
                        pe.wait_ge(turned_out, i * U + (u + 1))
                        pe.wait_ge(made_out, i * U + (u + 1))
                        for k in range(KC):
                            ins = pe.matmul(p_h[0 if u % 2 else 1][:, :], xt[u][:, k * P:(k + 1) * P], w_sb[:, k, :], start=(k == 0), stop=(k == KC - 1))
                        ins.then_inc(made, 1)

            @block.vector
            def _(v):
                with v.Fori(0, BLOCKS // U) as i:
                    for u in range(U):
                        v.wait_ge(turned, i * U + (u + 1))
                        v.tensor_copy(xt[u][:, :], p_t[u % 2][:, :]).then_inc(turned_out, 1)
                step = Chain(v, own)
                v.wait_ge(loaded, 48)
                v.wait_ge(made_out, BLOCKS + 1)
                for n, out in ((0, h[:, :, CH:]), (1, own_scores[:, :, 0:HEADS])):
                    step(v.tensor_tensor(prod[:, :, :], h[:, :, 0:CH], over_blocks(a_sb[:, n, :]), ALU.mult))
                    if heads == 1:
                        step(v.tensor_reduce(own_scores[:, :, 2 * HEADS - 1], prod[:, :, :], AX.X, ALU.add))
                        step(v.tensor_copy(out, own_scores[:, :, 2 * HEADS - 1:].to_broadcast([P, BLOCKS, HEADS])))
                    else:
                        step(v.tensor_reduce(out, prod[:, :, :].rearrange("p b (h c) -> p b h c", h=heads), AX.X, ALU.add))
                own_logit = own_scores[:, :, HEADS:]
                step(v.tensor_tensor(own_logit, h[:, :, CH:], own_scores[:, :, 0:HEADS], ALU.add))
                v.scalar_tensor_tensor(own_logit, own_logit, SLOPE, own_logit, ALU.mult, ALU.max)


def gather_and_spill(nc, S, sem, name, table, edge, spill, round_of_gathers):
    index_ready, scores, passed = sem(name + "index"), sem(name + "scores"), sem(name + "passed")
    arrived, before = S.arrived, round_of_gathers * (CHUNKS // PAIR) * 16
    stored = [sem(f"{name}stored{h}") for h in range(2)]
    with ExitStack() as ctx:
        rows = ctx.enter_context(nc.sbuf_tensor(name + "rows", [P, PAIR, HROW], FP32))
        index = ctx.enter_context(nc.sbuf_tensor(name + "indices", [P, PAIR], INT32))
        with nc.Block() as block:
            @block.gpsimd
            def _(pool):
                with pool.Fori(0, CHUNKS // PAIR) as i:
                    for u in range(PAIR):
                        if u % GRP == 0:
                            pool.wait_ge(stored[u // GRP], i * 16 + 16)
                            pool.wait_ge(scores, i * 2 + (u // GRP + 1))
                            pool.sem_inc(passed, 1)
                            pool.tensor_copy(index[:, u:u + GRP], S.take[:, bass.ds(i * PAIR + u, GRP)]).then_inc(index_ready, 1)
                            pool.wait_ge(index_ready, i * 2 + (u // GRP + 1))
                            pool.sem_inc(passed, 1)
                        pool.indirect_dma_start(rows[:, u, :], None, table, bass.IndirectOffsetOnAxis(ap=index[:, u:u + 1], axis=0)).then_inc(arrived[u], 16)

            @block.vector
            def _(v):
                v.sem_inc(scores, 2)
                with v.Fori(0, CHUNKS // PAIR) as i:
                    for h in range(2):
                        for u in range(GRP):
                            v.wait_ge(arrived[h * GRP + u], i * 16 + (before + 16))
                        v.tensor_copy(edge[:, bass.ds(i * PAIR + h * GRP, GRP), 0:HEADS], rows[:, h * GRP:(h + 1) * GRP, CH:]).then_inc(scores, 1)

            @block.sync
            def _(sp):
                for h in range(2):
                    sp.sem_inc(stored[h], 16)
                with sp.Fori(0, CHUNKS // PAIR) as i:
                    for h in range(2):
                        for u in range(GRP):
                            sp.wait_ge(arrived[h * GRP + u], i * 16 + (before + 16))
                        sp.dma_start(spill[:, bass.ds(i * PAIR + h * GRP, GRP), :], rows[:, h * GRP:(h + 1) * GRP, 0:CH]).then_inc(stored[h], 16)
                for h in range(2):
                    sp.wait_ge(stored[h], 16 * (CHUNKS // PAIR + 1))


STRIPS = P // HEADS
SCH = CHUNKS // STRIPS
SLEN = SCH * P


def softmax_weights(nc, S, sem, name, edge):
    own, prepared, turned, turned_out, given, passed = (
        sem(name + n) for n in ("own", "prepared", "turned", "turned_out", "given", "passed"))
    weighed, nodes_staged, logits_staged = sem(name + "weighed"), sem(name + "nodes_staged"), sem(name + "logits_staged")
    QUADS = [(j, min(4, SCH - j)) for j in range(0, SCH, 4)]
    NQ = len(QUADS)
    with ExitStack() as ctx:
        def sb(n, shape, dt=FP32):
            return ctx.enter_context(nc.sbuf_tensor(name + n, shape, dt))
        peak = sb("peak", [P, SLEN])
        fwd = sb("fwd", [P, SLEN])
        reset = sb("reset", [P, SLEN + 1])
        node = sb("node", [P, CHUNKS])
        ends = sb("ends", [P, 2])
        row = sb("row", [1, 2 * P])
        carry = sb("carry", [1, P + HEADS])
        init = sb("init", [P, 1])
        p_b = [ctx.enter_context(nc.psum_tensor(f"{name}b{n}", [P, 512], FP32)) for n in range(4)]
        p_s = ctx.enter_context(nc.psum_tensor(name + "s", [P, 512], FP32))
        e0, e1, e2 = (edge[:, :, n * HEADS:(n + 1) * HEADS] for n in range(3))
        strips = [e.rearrange("p (i j) h -> p i j h", i=STRIPS) for e in (e0, e1, e2)]

        def staged(tile):
            return tile[:, 0:SLEN].rearrange("p (j i h) -> p j i h", j=SCH, i=STRIPS)

        with nc.Block() as block:
            @block.vector
            def _(v):
                step = Chain(v, own)
                give = Chain(v, given)
                step(v.tensor_tensor(e0, e0, e1, ALU.add))
                v.scalar_tensor_tensor(e0, e0, SLOPE, e0, ALU.mult, ALU.max).then_inc(prepared, 1)
                step(v.scalar_tensor_tensor(node[:, :], S.block_of[:, 0:CHUNKS], 256.0, S.local[:, 0:CHUNKS], ALU.mult, ALU.add))
                step(v.tensor_scalar(node[:, :], node[:, :], 2.0, None, ALU.add))
                v.tensor_copy(staged(reset), node[:, :].rearrange("p (i j) -> p j i", i=STRIPS).unsqueeze(3).to_broadcast([P, SCH, STRIPS, HEADS])).then_inc(nodes_staged, 1)
                n = 0
                for out in (peak, fwd):
                    for j, m in QUADS:
                        n += 1
                        v.wait_ge(turned, n)
                        v.tensor_copy(out[:, j * P:(j + m) * P], p_b[(n - 1) % 4][:, 0:m * P]).then_inc(turned_out, 1)
                v.wait_ge(turned_out, n)
                step(v.scalar_tensor_tensor(reset[:, 1:SLEN], fwd[:, 1:SLEN], 1.0, fwd[:, 0:SLEN - 1], ALU.mult, ALU.not_equal))
                give(v.tensor_copy(ends[:, 0:1], fwd[:, SLEN - 1:SLEN]))
                v.wait_ge(passed, 1)
                give(v.tensor_tensor(reset[:, 0:1], fwd[:, 0:1], p_s[:, 0:1], ALU.not_equal))
                v.wait_ge(passed, 2)
                step(v.tensor_copy(reset[:, SLEN:], p_s[:, 1:2]))
                step(v.tensor_scalar(reset[:, :], reset[:, :], -BIG, None, ALU.mult))

                def running_maximum(out, resets, x, last, back):
                    turn = (lambda ap: ap[:, ::-1]) if back else (lambda ap: ap)
                    step(v.tensor_tensor_scan(turn(out), turn(resets), turn(x), -BIG, ALU.add, ALU.max))
                    step(v.tensor_copy(ends[:, 0:1], out[:, last:last + 1]))
                    give(v.tensor_reduce(ends[:, 1:2], resets, AX.X, ALU.min))
                    step(v.memset(carry[:, :], -BIG))
                    v.wait_ge(passed, 5 if back else 3)
                    step(v.tensor_copy(row[:, :], p_s[0:1, P:3 * P]))
                    for h in range(HEADS):
                        state, hold = row[0:1, h:P:HEADS], row[0:1, P + h:2 * P:HEADS]
                        shifted = carry[0:1, h:P:HEADS] if back else carry[0:1, HEADS + h:HEADS + P:HEADS]
                        scan = v.tensor_tensor_scan(turn(shifted), turn(hold), turn(state), -BIG, ALU.add, ALU.max)
                        if h == HEADS - 1:
                            give(scan)
                    v.wait_ge(passed, 6 if back else 4)
                    step(v.tensor_copy(init[:, :], p_s[:, 2:3]))
                    return v.tensor_tensor_scan(turn(out), turn(resets), turn(x), init[:, 0:1], ALU.add, ALU.max)
                step(running_maximum(fwd[:, :], reset[:, 0:SLEN], peak[:, :], SLEN - 1, False))
                give(running_maximum(peak[:, :], reset[:, 1:], fwd[:, :], 0, True))
                give(v.tensor_scalar(fwd[:, :], reset[:, 1:], -1.0 / BIG, None, ALU.mult))
                for j, m in QUADS:
                    n += 1
                    v.wait_ge(turned, n)
                    part = strips[2][:, :, j:j + m, :].rearrange("p i j h -> p j i h")
                    out = strips[1][:, :, j:j + m, :].rearrange("p i j h -> p j i h")
                    src = p_b[(n - 1) % 4][:, 0:m * P].rearrange("p (j i h) -> p j i h", j=m, i=STRIPS)
                    v.tensor_tensor(out, src, part, ALU.max).then_inc(turned_out, 1)
                v.wait_ge(turned_out, n)
                v.tensor_tensor(e0, e0, e1, ALU.subtract).then_inc(weighed, 1)
                for j, m in QUADS:
                    n += 1
                    v.wait_ge(turned, n)
                    out = strips[2][:, :, j:j + m, :].rearrange("p i j h -> p j i h")
                    src = p_b[(n - 1) % 4][:, 0:m * P].rearrange("p (j i h) -> p j i h", j=m, i=STRIPS)
                    v.tensor_copy(out, src).then_inc(turned_out, 1)
                v.wait_ge(turned_out, n)
                v.tensor_tensor(e1, e1, e2, ALU.mult)

            @block.scalar
            def _(act):
                act.wait_ge(prepared, 1)
                act.copy(staged(fwd), strips[0].rearrange("p i j h -> p j i h")).then_inc(logits_staged, 1)
                act.wait_ge(weighed, 1)
                act.activation(e0, e0, ACT.Exp)

            @block.tensor
            def _(pe):
                n = 0

                def turn(j, m, view):
                    nonlocal n
                    if n >= 4:
                        pe.wait_ge(turned_out, n - 3)
                    for q in range(m):
                        ins = pe.transpose(p_b[n % 4][:, q * P:(q + 1) * P], view(j + q), S.ident[:, :])
                    ins.then_inc(turned, 1)
                    n += 1
                for ready, strip in ((logits_staged, fwd), (nodes_staged, reset)):
                    pe.wait_ge(ready, 1)
                    for j, m in QUADS:
                        turn(j, m, lambda c: strip[:, c * P:(c + 1) * P])
                pe.wait_ge(given, 1)
                pe.matmul(p_s[:, 0:1], S.down[:, :], ends[:, 0:1], start=True, stop=True).then_inc(passed, 1)
                pe.wait_ge(given, 2)
                pe.matmul(p_s[:, 1:2], S.up[:, :], reset[:, 0:1], start=True, stop=True).then_inc(passed, 1)
                for back in range(2):
                    pe.wait_ge(given, 3 + 2 * back)
                    pe.transpose(p_s[0:1, P:2 * P], ends[:, 0:1], S.ident[:, :])
                    pe.transpose(p_s[0:1, 2 * P:3 * P], ends[:, 1:2], S.ident[:, :]).then_inc(passed, 1)
                    pe.wait_ge(given, 4 + 2 * back)
                    pe.matmul(p_s[:, 2:3], carry[0:1, back * HEADS:back * HEADS + P], S.ones[0:1, 0:1], start=True, stop=True).then_inc(passed, 1)
                for w, strip in enumerate((peak, fwd)):
                    pe.wait_ge(given, 7 + w)
                    for j, m in QUADS:
                        turn(j, m, lambda c: strip[:, c * P:(c + 1) * P])


def weighted_sum(nc, S, sem, name, edge, spill, acc):
    hot_ready, added, done, cleared, mixed = (sem(name + n) for n in ("hot", "added", "done", "cleared", "mixed"))
    arrived = [sem(f"{name}row{h}") for h in range(2)]
    with ExitStack() as ctx:
        hot = ctx.enter_context(nc.sbuf_tensor(name + "hots", [P, PAIR, P], FP32))
        rows = ctx.enter_context(nc.sbuf_tensor(name + "rows", [P, PAIR, CH], FP32))
        banks = [ctx.enter_context(nc.psum_tensor(f"{name}bank{u}", [P, 512], FP32)) for u in range(GRP)]
        with nc.Block() as block:
            @block.sync
            def _(sp):
                with sp.Fori(0, CHUNKS // PAIR) as i:
                    for h in range(2):
                        sp.wait_ge(done, i * PAIR + GRP * (h + 1))
                        sp.dma_start(rows[:, h * GRP:(h + 1) * GRP, :], spill[:, bass.ds(i * PAIR + h * GRP, GRP), :]).then_inc(arrived[h], 16)

            @block.gpsimd
            def _(pool):
                with pool.Fori(0, CHUNKS // PAIR) as i:
                    for h in range(2):
                        pool.wait_ge(arrived[h], i * 16 + 16)
                        part = rows[:, h * GRP:(h + 1) * GRP, :].rearrange("p a (h c) -> p a h c", h=HEADS)
                        weight = edge[:, bass.ds(i * PAIR + h * GRP, GRP), 0:HEADS].unsqueeze(3).to_broadcast([P, GRP, HEADS, HC])
                        pool.tensor_tensor(part, part, weight, ALU.mult).then_inc(mixed, 1)

            @block.vector
            def _(v):
                v.memset(acc[:, :], 0.0).then_inc(cleared, 1)
                v.wait_ge(cleared, 1)
                hot_and_add(nc, S, v, name, hot, S.col[:, 0:P], None, acc, ACCW, banks, hot_ready, added, done)

            @block.tensor
            def _(pe):
                pe.sem_inc(done, PAIR)
                with pe.Fori(0, CHUNKS // PAIR) as i:
                    for u in range(PAIR):
                        pe.wait_ge(hot_ready, i * PAIR + (u + 1))
                        pe.wait_ge(added, i * PAIR + (u + 1))
                        if u % GRP == 0:
                            pe.wait_ge(mixed, i * 2 + (u // GRP + 1))
                        pe.matmul(banks[u % GRP][:, 0:CH], hot[:, u, :], rows[:, u, :], start=True, stop=True)
                        pe.matmul(banks[u % GRP][:, CH:ACCW], hot[:, u, :], edge[:, bass.ds(i * PAIR + u, 1), :].rearrange("p a w -> p (a w)"),
                                  start=True, stop=True).then_inc(done, 1)


def finish_attention(nc, S, sem, name, acc, h, own_scores, b, result, relu):
    own, loaded, lowered, weighed = (sem(name + n) for n in ("own", "loaded", "lowered", "weighed"))
    with ExitStack() as ctx:
        bias = ctx.enter_context(nc.sbuf_tensor(name + "bias", [P, CH], FP32))
        weight = ctx.enter_context(nc.sbuf_tensor(name + "weight", [P, BLOCKS, HEADS], FP32))
        total = ctx.enter_context(nc.sbuf_tensor(name + "total", [P, BLOCKS, HEADS], FP32))
        A = blocks_of(acc)
        own_logit = own_scores[:, :, HEADS:]

        def per_head(ap):
            return ap.rearrange("p b (h c) -> p b h c", h=HEADS)

        def wide(ap):
            return ap[:, :, :].unsqueeze(3).to_broadcast([P, BLOCKS, HEADS, HC])
        with nc.Block() as block:
            @block.sync
            def _(sp):
                sp.dma_start(bias[:, :], b.partition_broadcast(P)).then_inc(loaded, 16)
                sp.wait_ge(loaded, 16)

            @block.scalar
            def _(act):
                act.wait_ge(lowered, 1)
                act.activation(weight[:, :, :], weight[:, :, :], ACT.Exp).then_inc(weighed, 1)

            @block.vector
            def _(v):
                step = Chain(v, own)
                step(v.tensor_scalar(weight[:, :, :], A[:, :, CH + 2 * HEADS:], -1.0, 1.0, ALU.mult, ALU.add))
                step(v.tensor_tensor(weight[:, :, :], weight[:, :, :], own_logit, ALU.mult))
                step(v.tensor_tensor(weight[:, :, :], weight[:, :, :], A[:, :, CH + HEADS:CH + 2 * HEADS], ALU.add))
                v.tensor_tensor(weight[:, :, :], own_logit, weight[:, :, :], ALU.subtract).then_inc(lowered, 1)
                v.wait_ge(weighed, 1)
                step(v.scalar_tensor_tensor(total[:, :, :], A[:, :, CH:CH + HEADS], 1e-16, weight[:, :, :], ALU.add, ALU.add))
                step(v.reciprocal(total[:, :, :], total[:, :, :]))
                step(v.tensor_tensor(per_head(h[:, :, 0:CH]), per_head(h[:, :, 0:CH]), wide(weight), ALU.mult))
                step(v.tensor_tensor(result[:, :, :], h[:, :, 0:CH], A[:, :, 0:CH], ALU.add))
                step(v.tensor_tensor(per_head(result[:, :, :]), per_head(result[:, :, :]), wide(total), ALU.mult))
                v.wait_ge(loaded, 16)
                step(v.tensor_tensor(result[:, :, :], result[:, :, :], over_blocks(bias[:, :]), ALU.add))
                if relu:
                    v.tensor_scalar(result[:, :, :], result[:, :, :], 0.0, None, ALU.max)


def attention_layer(nc, S, name, x, w, a_src, a_dst, b, heads, acc, result, relu, node_table, spill, round_of_gathers):
    with ExitStack() as ctx:
        def sb(n, shape, dt=FP32):
            return ctx.enter_context(nc.sbuf_tensor(name + n, shape, dt))
        h = sb("h", [P, BLOCKS, HROW])
        own_scores = sb("own_scores", [P, BLOCKS, 2 * HEADS])
        with Semaphores(nc) as sem:
            attention_features(nc, S, sem, name + "f_", x, w, a_src, a_dst, heads, h, own_scores, node_table)
        with ExitStack() as inner:
            edge = inner.enter_context(nc.sbuf_tensor(name + "edge", [P, CHUNKS, 3 * HEADS], FP32))
            with Semaphores(nc) as sem:
                look_up(nc, S, sem, name + "l_", own_scores, 2 * HEADS, edge[:, :, HEADS:])
                gather_and_spill(nc, S, sem, name + "g_", node_table, edge, spill, round_of_gathers)
            with Semaphores(nc) as sem:
                softmax_weights(nc, S, sem, name + "s_", edge)
                weighted_sum(nc, S, sem, name + "w_", edge, spill, acc)
        with Semaphores(nc) as sem:
            finish_attention(nc, S, sem, name + "n_", acc, h, own_scores, b, result, relu)


def gnn(nc, x, src, dst, edge_type_7, L0_gnn_gn1_w, L0_gnn_gn1_b, L0_gnn_conv1_w, L0_gnn_gn2_w, L0_gnn_gn2_b, L0_gnn_conv2_w,
        L1_gnn_W1, L1_gnn_att_src1, L1_gnn_att_dst1, L1_gnn_b1, L1_gnn_W2, L1_gnn_att_src2, L1_gnn_att_dst2, L1_gnn_b2, out):
    WIDE = CHUNKS + EXTRA
    feature_table = nc.dram_tensor("feature_table", [TYPES * TROWS, CH], FP32).ap()
    node_table = nc.dram_tensor("node_table", [BLOCKS * P, HROW], FP32).ap()
    spill = nc.dram_tensor("spill", [P, CHUNKS, CH], FP32).ap()
    with ExitStack() as ctx:
        S = Shared()

        def keep(stack, n, shape, dt=FP32):
            return stack.enter_context(nc.sbuf_tensor(n, shape, dt))
        S.arrived = [ctx.enter_context(nc.semaphore(f"arrived{u}")) for u in range(PAIR)]
        S.col = keep(ctx, "col", [P, WIDE])
        S.col_h = keep(ctx, "col_h", [P, CHUNKS], FP16)
        S.row = keep(ctx, "row", [P, 1])
        S.ident = keep(ctx, "ident", [P, P])
        S.ident_b = keep(ctx, "ident_b", [P, P], BF16)
        S.above = keep(ctx, "above", [P, P])
        S.down = keep(ctx, "down", [P, P])
        S.up = keep(ctx, "up", [P, P])
        S.ones = keep(ctx, "ones", [P, P])
        S.block_of = keep(ctx, "block_of", [P, WIDE])
        S.block_hot = keep(ctx, "block_hot", [32, CHUNKS])
        S.acc_at = keep(ctx, "acc_at", [1, WIDE], INT32)
        S.local = keep(ctx, "local", [P, WIDE])
        S.local_b = keep(ctx, "local_b", [P, WIDE], BF16)
        S.take = keep(ctx, "take", [P, CHUNKS], INT32)
        x_sb = ctx.enter_context(nc.sbuf_tensor("x_sb", [P, BLOCKS, CH], FP32))
        acc = ctx.enter_context(nc.sbuf_tensor("acc", [P, BLOCKS * ACCW], FP32))
        sums = blocks_of(acc)[:, :, 0:CH]

        with ExitStack() as conv:
            S.col_i = keep(conv, "col_i", [P, WIDE], INT32)
            S.row_i = keep(conv, "row_i", [P, 1], INT32)
            S.src_i = keep(conv, "src_i", [P, COLS], INT32)
            S.dst_i = keep(conv, "dst_i", [P, COLS], INT32)
            S.type_i = keep(conv, "type_i", [P, COLS], INT32)
            S.pay = keep(conv, "pay", [P, COLS])
            S.weight = keep(conv, "weight", [P, WIDE])
            S.etype = keep(conv, "etype", [P, CHUNKS])
            with Semaphores(nc) as sem:
                constants(nc, S, sem, src, dst, edge_type_7)
                load_nodes(nc, S, sem, x, x_sb)
                place_by_src(nc, S, sem)
                type_weights(nc, S, sem, acc)
            for n, (gn_w, gn_b, conv_w) in enumerate(((L0_gnn_gn1_w, L0_gnn_gn1_b, L0_gnn_conv1_w),
                                                      (L0_gnn_gn2_w, L0_gnn_gn2_b, L0_gnn_conv2_w))):
                with Semaphores(nc) as sem:
                    with nc.sbuf_tensor(f"norm{n}", [P, BLOCKS, CH], FP32) as norm:
                        group_norm(nc, S, sem, f"n{n}_", sums if n else x_sb[:, :, :], norm, gn_w, gn_b)
                        typed_features(nc, S, sem, f"f{n}_", norm, conv_w, feature_table)
                    gather_and_add(nc, S, sem, f"a{n}_", feature_table, acc, n)
            with Semaphores(nc) as sem:
                place_by_dst(nc, S, sem)
        with Semaphores(nc) as sem:
            add_residual(nc, x_sb, sums, 2.0)
            layer_norm(nc, S, sem, "m0_", x_sb)
        attention_layer(nc, S, "g0_", x_sb, L1_gnn_W1, L1_gnn_att_src1, L1_gnn_att_dst1, L1_gnn_b1, HEADS, acc, sums, True,
                        node_table, spill, 2)
        attention_layer(nc, S, "g1_", sums, L1_gnn_W2, L1_gnn_att_src2, L1_gnn_att_dst2, L1_gnn_b2, 1, acc, sums, False,
                        node_table, spill, 3)
        with Semaphores(nc) as sem:
            add_residual(nc, x_sb, sums, 1.0)
            layer_norm(nc, S, sem, "m1_", x_sb)
            store_nodes(nc, S, sem, x_sb, out)


def load_nodes(nc, S, sem, x, x_sb):
    loaded, cleared = sem("x_loaded"), sem("x_cleared")
    with nc.Block() as block:
        @block.vector
        def _(v):
            v.memset(x_sb[:, BLOCKS - 1, :], 0.0).then_inc(cleared, 1)

        @block.sync
        def _(sp):
            sp.dma_start(x_sb[:, 0:BLOCKS - 1, :], x[0:(BLOCKS - 1) * P, :].rearrange("(b p) c -> p b c", p=P)).then_inc(loaded, 16)
            sp.wait_ge(cleared, 1)
            sp.dma_start(x_sb[0:LAST, BLOCKS - 1, :], x[(BLOCKS - 1) * P:, :]).then_inc(loaded, 16)
            sp.wait_ge(loaded, 32)


def store_nodes(nc, S, sem, x_sb, out):
    stored = sem("stored")
    with nc.Block() as block:
        @block.sync
        def _(sp):
            sp.dma_start(out[0:(BLOCKS - 1) * P, :].rearrange("(b p) c -> p b c", p=P), x_sb[:, 0:BLOCKS - 1, :]).then_inc(stored, 16)
            sp.dma_start(out[(BLOCKS - 1) * P:, :], x_sb[0:LAST, BLOCKS - 1, :]).then_inc(stored, 16)
            sp.wait_ge(stored, 32)


def add_residual(nc, x, y, times):
    with nc.Block() as block:
        @block.vector
        def _(v):
            v.scalar_tensor_tensor(x[:, :, :], x[:, :, :], times, y, ALU.mult, ALU.add)


_INS = ["x", "src", "dst", "edge_type_7", "L0_gnn_gn1_w", "L0_gnn_gn1_b", "L0_gnn_conv1_w", "L0_gnn_gn2_w", "L0_gnn_gn2_b",
        "L0_gnn_conv2_w", "L1_gnn_W1", "L1_gnn_att_src1", "L1_gnn_att_dst1", "L1_gnn_b1", "L1_gnn_W2", "L1_gnn_att_src2",
        "L1_gnn_att_dst2", "L1_gnn_b2"]


def kernel(**inputs):
    import numpy as np
    from concourse import bacc
    from concourse.bass_utils import run_bass_kernel_spmd

    nc = bacc.Bacc("TRN2", target_bir_lowering=False, num_devices=1)
    arrays, args = {}, []
    for name in _INS:
        a = np.ascontiguousarray(inputs[name])
        arrays[f"in_{name}"] = a
        args.append(nc.dram_tensor(f"in_{name}", a.shape, mybir.dt.from_np(a.dtype), kind="ExternalInput").ap())
    args.append(nc.dram_tensor("out", (NODES, CH), FP32, kind="ExternalOutput").ap())
    gnn(nc, *args)
    return run_bass_kernel_spmd(nc, [arrays], core_ids=[0]).results[0]["out"]
```

```python
from contextlib import ExitStack

import concourse.bass as bass
from concourse import mybir

FP32 = mybir.dt.float32
BF16 = mybir.dt.bfloat16
FP16 = mybir.dt.float16
INT32 = mybir.dt.int32
ALU = mybir.AluOpType
ACT = mybir.ActivationFunctionType
AX = mybir.AxisListType

P = 128
NODES, CH = 3125, 256
EDGES, TYPES = 50000, 7
GROUPS = 32
HEADS = 8
HC = CH // HEADS
BLOCKS = -(-NODES // P)
LAST = NODES - (BLOCKS - 1) * P
COLS = -(-EDGES // P)
TAIL = EDGES - (P - 1) * COLS
BINS = BLOCKS * TYPES
STEP = 16
CHUNKS = -(-(EDGES // P + BLOCKS) // 16) * 16
CPAD = CHUNKS
EXTRA = 8
TROWS = BLOCKS * P
TCODE = 4096
ACCW = CH + 3 * HEADS
HROW = CH + HEADS
EPS = 1e-5
SLOPE = 0.2
BIG = 2.0 ** 100
KC = CH // P


class Shared:
    pass


class Semaphores:

    def __init__(self, nc):
        self.nc, self.held = nc, []

    def __enter__(self):
        def sem(name):
            self.held.append(self.nc.alloc_semaphore(name=name))
            return self.held[-1]
        return sem

    def __exit__(self, *problem):
        if problem[0] is None:
            self.nc.clear_and_free_semaphores(self.held)
            self.nc.all_engine_barrier()


class Chain:

    def __init__(self, eng, sem):
        self.eng, self.sem, self.n = eng, sem, 0

    def __call__(self, ins):
        self.n += 1
        ins.then_inc(self.sem, 1)
        self.eng.wait_ge(self.sem, self.n)


def constants(nc, S, sem, src, dst, etype):
    loaded, ramps, padded, own = sem("c_loaded"), sem("c_ramps"), sem("c_padded"), sem("c_own")
    with nc.Block() as block:
        @block.sync
        def _(sp):
            sp.wait_ge(padded, 1)
            for tile, edges in ((S.src_i, src), (S.dst_i, dst), (S.type_i, etype)):
                sp.dma_start(tile[0:P - 1, 0:COLS], edges[0:(P - 1) * COLS].rearrange("(p c) -> p c", c=COLS)).then_inc(loaded, 16)
                sp.dma_start(tile[P - 1:P, 0:TAIL], edges[(P - 1) * COLS:EDGES].rearrange("(a c) -> a c", a=1)).then_inc(loaded, 16)
            sp.wait_ge(loaded, 96)

        @block.gpsimd
        def _(pool):
            pool.iota(S.col_i[:, :], [[1, CHUNKS + EXTRA]], channel_multiplier=0).then_inc(ramps, 1)
            pool.iota(S.row_i[:, :], [[0, 1]], channel_multiplier=1).then_inc(ramps, 1)

        @block.vector
        def _(v):
            step = Chain(v, own)
            for n, tile in enumerate((S.src_i, S.dst_i, S.type_i)):
                ins = v.memset(tile[:, :], 8191)
                if n == 2:
                    ins.then_inc(padded, 1)
            v.wait_ge(ramps, 2)
            v.tensor_copy(S.col_h[:, :], S.col_i[:, 0:CHUNKS])
            step(v.tensor_copy(S.row[:, :], S.row_i[:, :]))
            step(v.tensor_copy(S.col[:, :], S.col_i[:, :]))
            v.tensor_scalar(S.ident[:, :], S.col[:, 0:P], S.row[:, 0:1], None, ALU.is_equal)
            v.tensor_scalar(S.ident_b[:, :], S.col[:, 0:P], S.row[:, 0:1], None, ALU.is_equal)
            v.tensor_scalar(S.above[:, :], S.col[:, 0:P], S.row[:, 0:1], None, ALU.is_gt)
            v.tensor_scalar(S.down[:, :], S.col[:, 0:P], -float(HEADS), S.row[:, 0:1], ALU.add, ALU.is_equal)
            v.tensor_scalar(S.up[:, :], S.col[:, 0:P], float(HEADS), S.row[:, 0:1], ALU.add, ALU.is_equal)
            v.memset(S.ones[:, :], 1.0)
            v.memset(S.zeros[:, :], 0.0)


class Placement:

    def __init__(self, nc, ctx, sem, name, key_i, pay_shift):
        def sb(n, shape, dt=FP32):
            return ctx.enter_context(nc.sbuf_tensor(name + n, shape, dt))
        self.key_i, self.pay_shift = key_i, pay_shift
        self.own, self.counted, self.summed = sem(name + "own"), sem(name + "counted"), sem(name + "summed")
        self.spread, self.moved = sem(name + "spread"), sem(name + "moved")
        self.block_of = sb("block_of", [P, CHUNKS + EXTRA])
        self.block_hot = sb("block_hot", [32, CHUNKS])
        self.acc_at = sb("acc_at", [1, CHUNKS + EXTRA], INT32)
        self.local = sb("local", [P, CHUNKS + EXTRA])
        self.local_b = sb("local_b", [P, CHUNKS + EXTRA], BF16)
        self.take = sb("take", [P, CHUNKS], INT32)

    def scratch(self, nc, ctx, name):
        def sb(n, shape, dt=FP32):
            return ctx.enter_context(nc.sbuf_tensor(name + n, shape, dt))
        self.ti, self.tj = sb("ti", [P, CPAD], INT32), sb("tj", [P, CPAD], INT32)
        self.blk, self.lo, self.hi = sb("blk", [P, CPAD]), sb("lo", [P, CPAD]), sb("hi", [P, CPAD])
        self.pos, self.lane, self.chunk = sb("pos", [P, CPAD]), sb("lane", [P, CPAD]), sb("chunk", [P, CPAD])
        self.mask, self.run = [sb(f"mask{n}", [P, CPAD]) for n in range(2)], [sb(f"run{n}", [P, CPAD]) for n in range(2)]
        self.cnt, self.base, self.tot, self.first, self.incl = (sb(n, [P, BLOCKS]) for n in ("cnt", "base", "tot", "first", "incl"))
        self.nch_i = sb("nch_i", [P, BLOCKS], INT32)

    def buffers(self, nc, ctx, name):
        def sb(n, shape, dt=FP32):
            return ctx.enter_context(nc.sbuf_tensor(name + n, shape, dt))
        self.highs, self.lows = sb("highs", [P, STEP, P], FP16), sb("lows", [P, STEP, P], FP16)
        self.chunks = sb("chunks", [P, STEP, CHUNKS], FP16)
        self.p_hi, self.p_lo = (ctx.enter_context(nc.psum_tensor(name + n, [P, 512], FP32)) for n in ("p_hi", "p_lo"))

    def ranks(self, v, S, step, payload, p_cnt):
        T = self
        step(v.tensor_scalar(T.ti[:, :], T.key_i[:, :], 7, None, ALU.logical_shift_right))
        step(v.tensor_copy(T.blk[:, :], T.ti[:, :]))
        step(v.tensor_scalar(T.ti[:, :], T.key_i[:, :], P - 1, None, ALU.bitwise_and))
        step(v.tensor_copy(T.lane[:, :], T.ti[:, :]))
        payload(v, step, T.lo)
        if T.pay_shift == 15:
            v.tensor_copy(S.key_lane[:, :], T.lane[:, :])
            v.scalar_tensor_tensor(S.key_bin[:, :], T.blk[:, :], float(TYPES), S.pay[:, :], ALU.mult, ALU.add)
        step(v.scalar_tensor_tensor(T.pos[:, :], T.lane[:, :], float(1 << T.pay_shift), T.lo[:, :], ALU.mult, ALU.add))
        step(v.tensor_copy(T.ti[:, :], T.pos[:, :]))
        step(v.tensor_scalar(T.tj[:, :], T.ti[:, :], 11, None, ALU.logical_shift_right))
        step(v.tensor_scalar(T.ti[:, :], T.ti[:, :], 2047, None, ALU.bitwise_and))
        v.tensor_copy(T.hi[:, :], T.tj[:, :])
        step(v.tensor_copy(T.lo[:, :], T.ti[:, :]))
        spare = T.mask + T.run
        for b in range(BLOCKS):
            if b >= len(spare):
                v.wait_ge(T.counted, b - len(spare) + 1)
            v.tensor_scalar(spare[b % 4][:, :], T.blk[:, :], float(b), 0.0, ALU.is_equal, ALU.add, accum_out=T.cnt[:, b:b + 1]).then_inc(T.counted, 1)
        v.memset(T.pos[:, :], 0.0)
        v.memset(T.block_of[:, :], 0.0)
        v.wait_ge(T.summed, 1)
        step(v.tensor_scalar(T.tot[:, :], p_cnt[:, 0:BLOCKS], float(P - 1), None, ALU.add))
        step(v.tensor_copy(T.nch_i[:, :], T.tot[:, :]))
        step(v.tensor_scalar(T.nch_i[:, :], T.nch_i[:, :], 7, None, ALU.logical_shift_right))
        step(v.tensor_copy(T.tot[:, :], T.nch_i[:, :]))
        step(v.tensor_tensor_scan(T.incl[:, :], T.tot[:, :], T.tot[:, :], 0.0, ALU.add, ALU.max))
        step(v.tensor_tensor(T.first[:, :], T.incl[:, :], T.tot[:, :], ALU.subtract))
        step(v.scalar_tensor_tensor(T.base[:, :], T.first[:, :], float(P), p_cnt[:, BLOCKS:2 * BLOCKS], ALU.mult, ALU.add))
        mark = step.n
        v.tensor_scalar(T.mask[0][:, :], T.blk[:, :], 0.0, None, ALU.is_equal).then_inc(T.own, 1)
        for b in range(BLOCKS):
            m, r = T.mask[b % 2], T.run[b % 2]
            v.wait_ge(T.own, mark + 4 * b + 1)
            v.tensor_tensor_scan(r[:, :], m[:, :], m[:, :], T.base[:, b:b + 1], ALU.add, ALU.max).then_inc(T.own, 1)
            if b > 0:
                v.scalar_tensor_tensor(T.block_of[:, :], S.col[:, :], T.first[:, b:b + 1], T.block_of[:, :], ALU.is_ge, ALU.add)
            v.wait_ge(T.own, mark + 4 * b + 2)
            v.tensor_tensor(r[:, :], r[:, :], m[:, :], ALU.mult).then_inc(T.own, 1)
            n = T.mask[(b + 1) % 2]
            if b + 1 < BLOCKS:
                v.wait_ge(T.own, mark + 4 * b)
            v.tensor_scalar(n[:, :], T.blk[:, :], float(b + 1), None, ALU.is_equal).then_inc(T.own, 1)
            v.wait_ge(T.own, mark + 4 * b + 4)
            v.tensor_tensor(T.pos[:, :], T.pos[:, :], r[:, :], ALU.add).then_inc(T.own, 1)
        step.n = mark + 4 * BLOCKS + 1
        v.wait_ge(T.own, step.n)
        step(v.tensor_scalar(T.pos[:, :], T.pos[:, :], -1.0, None, ALU.add))
        step(v.tensor_copy(T.ti[:, :], T.pos[:, :]))
        step(v.tensor_scalar(T.tj[:, :], T.ti[:, :], P - 1, None, ALU.bitwise_and))
        step(v.tensor_scalar(T.ti[:, :], T.ti[:, :], 7, None, ALU.arith_shift_right))
        v.tensor_copy(T.lane[:, :], T.tj[:, :])
        step(v.tensor_copy(T.chunk[:, :], T.ti[:, :]))

    def totals(self, pe, S, p_cnt):
        pe.wait_ge(self.counted, BLOCKS)
        pe.matmul(p_cnt[:, 0:BLOCKS], S.ones[:, :], self.cnt[:, :], start=True, stop=True)
        pe.matmul(p_cnt[:, BLOCKS:2 * BLOCKS], S.above[:, :], self.cnt[:, :], start=True, stop=True).then_inc(self.summed, 1)

    def spread_column(self, v, S, c, slot):
        e = bass.ds(c, 1)
        v.tensor_scalar(self.highs[:, slot, :], S.col_h[:, 0:P], self.lane[:, e], self.hi[:, e], ALU.is_equal, ALU.mult)
        v.tensor_scalar(self.lows[:, slot, :], S.col_h[:, 0:P], self.lane[:, e], self.lo[:, e], ALU.is_equal, ALU.mult)
        return v.tensor_scalar(self.chunks[:, slot, :], S.col_h[:, :], self.chunk[:, e], None, ALU.is_equal)

    def move_column(self, pe, slot):
        pe.matmul(self.p_hi[:, 0:CHUNKS], self.highs[:, slot, :], self.chunks[:, slot, :], start=False, stop=False)
        return pe.matmul(self.p_lo[:, 0:CHUNKS], self.lows[:, slot, :], self.chunks[:, slot, :], start=False, stop=False)

    def open_sums(self, pe, S, start):
        for p in (self.p_hi, self.p_lo):
            ins = pe.matmul(p[:, 0:CHUNKS], S.zeros[:, 0:P], S.zeros[:, :], start=start, stop=not start)
        return ins

    def decode(self, v, S, step, rest):
        T = self
        ci, cj, cf, cg = T.ti[:, 0:CHUNKS], T.tj[:, 0:CHUNKS], T.lo[:, 0:CHUNKS], T.hi[:, 0:CHUNKS]
        step(v.tensor_copy(cf, T.p_lo[:, 0:CHUNKS]))
        step(v.scalar_tensor_tensor(cf, T.p_hi[:, 0:CHUNKS], 2048.0, cf, ALU.mult, ALU.add))
        step(v.tensor_copy(ci, cf))
        step(v.tensor_scalar(cj, ci, T.pay_shift, None, ALU.logical_shift_right))
        step(v.tensor_copy(cg, cj))
        step(v.tensor_scalar(cf, cf, 0.0, None, ALU.is_gt))
        step(v.scalar_tensor_tensor(cg, cg, 1.0, cf, ALU.add, ALU.mult))
        v.memset(T.local[:, CHUNKS:], -1.0)
        v.memset(T.local_b[:, CHUNKS:], -1.0)
        step(v.tensor_scalar(T.local[:, 0:CHUNKS], cg, -1.0, None, ALU.add))
        v.tensor_copy(T.local_b[:, 0:CHUNKS], T.local[:, 0:CHUNKS])
        v.tensor_scalar(T.acc_at[0:1, :], T.block_of[0:1, :], float(ACCW), None, ALU.mult)
        v.tensor_scalar(T.block_hot[0:BLOCKS, :], T.block_of[0:BLOCKS, 0:CHUNKS], S.row[0:BLOCKS, 0:1], None, ALU.is_equal)
        rest(v, step, ci, cj, cf)


def conv_payload(S):
    def payload(v, step, out):
        step(v.tensor_copy(S.pay[:, :], S.type_i[:, :]))
        step(v.tensor_copy(out[:, :], S.dst_i[:, :]))
        step(v.tensor_scalar(out[:, :], out[:, :], 1.0, None, ALU.add))
        step(v.scalar_tensor_tensor(out[:, :], S.pay[:, :], float(TCODE), out[:, :], ALU.mult, ALU.add))
    return payload


def conv_decode(S, E):
    def rest(v, step, code, ti, tf):
        step(v.tensor_scalar(ti, code, 12, 7, ALU.logical_shift_right, ALU.bitwise_and))
        step(v.tensor_copy(S.etype[:, :], ti))
        step(v.tensor_scalar(code, code, (1 << 15) - 1, None, ALU.bitwise_and))
        step(v.tensor_copy(tf, code))
        step(v.scalar_tensor_tensor(tf, S.etype[:, :], float(TROWS - TCODE), tf, ALU.mult, ALU.add))
        v.tensor_scalar(E.take[:, :], tf, -1.0, 0.0, ALU.add, ALU.max)
    return rest


def attention_payload(S):
    def payload(v, step, out):
        step(v.tensor_copy(out[:, :], S.src_i[:, :]))
        step(v.tensor_scalar(out[:, :], out[:, :], 1.0, None, ALU.add))
    return payload


def attention_decode(S, E):
    def rest(v, step, code, ti, tf):
        step(v.tensor_scalar(ti, code, 4095, None, ALU.bitwise_and))
        step(v.tensor_copy(tf, ti))
        v.tensor_scalar(E.take[:, :], tf, -1.0, 0.0, ALU.add, ALU.max)
    return rest


def rank_edges(nc, S, E, payload):
    with nc.psum_tensor("p_cnt", [P, 512], FP32) as p_cnt:
        with nc.Block() as block:
            @block.vector
            def _(v):
                step = Chain(v, E.own)
                E.ranks(v, S, step, payload, p_cnt)
                E.steps = step.n

            @block.tensor
            def _(pe):
                E.totals(pe, S, p_cnt)


GRP = 8
PAIR = 2 * GRP
RING = 4 * GRP


def hot_and_add(nc, S, E, v, own, hot, weight, acc, width, banks, hot_ready, added, done, beside=None):
    regs = [v.alloc_register(f"{own}_at{u}") for u in range(GRP)]

    def onehot(c, slot):
        if weight is None:
            ins = v.tensor_scalar(hot[:, slot, :], S.col[:, 0:P], E.local[:, bass.ds(c, 1)], None, ALU.is_equal)
        else:
            ins = v.tensor_scalar(hot[:, slot, :], S.col[:, 0:P], E.local[:, bass.ds(c, 1)], weight[:, bass.ds(c, 1)],
                                  ALU.is_equal, ALU.mult)
        ins.then_inc(hot_ready, 1)
    v.sem_inc(added, len(banks))
    for u in range(GRP):
        onehot(u, u)
    with v.Fori(0, CHUNKS // PAIR) as i:
        for h in range(2):
            first = i * PAIR + GRP * h
            v.load(regs, E.acc_at[0:1, bass.ds(first, GRP)])
            at = [v.snap(r, min_val=0, max_val=(BLOCKS - 1) * ACCW) for r in regs]
            v.wait_ge(done, first + RING)
            for u in range(GRP):
                onehot(first + (GRP + u), GRP * (1 - h) + u)
                if beside:
                    beside(first + u, GRP * h + u)
                v.wait_ge(done, first + (RING + u + 1))
                v.wait_ge(added, first + (len(banks) + u))
                part = acc[:, bass.ds(at[u], width)]
                v.tensor_tensor(part, part, banks[u % len(banks)][:, 0:width], ALU.add).then_inc(added, 1)


def look_up(nc, S, E, sem, name, table, width, result, gather=None):
    turned, turned_out = sem(name + "turned"), sem(name + "turned_out")
    spread, spread_out = sem(name + "spread"), sem(name + "spread_out")
    rows, hot_ready, found, stored = sem(name + "rows"), sem(name + "hot"), sem(name + "found"), sem(name + "stored")
    G4 = 4
    DEEP = 4
    if gather:
        node_table, edge, spill, round_of_gathers = gather
        index_ready, scores, passed = sem(name + "index"), sem(name + "scores"), sem(name + "passed")
        arrived, before = S.arrived, (2 * (CHUNKS // RING) + round_of_gathers * (CHUNKS // PAIR)) * 16
        spilled = [sem(f"{name}spilled{h}") for h in range(2)]
    with ExitStack() as ctx:
        def sb(n, shape, dt=FP32):
            return ctx.enter_context(nc.sbuf_tensor(name + n, shape, dt))

        def pb(n, shape):
            return ctx.enter_context(nc.psum_tensor(name + n, shape, FP32))
        tt = sb("tt", [32, width, P])
        per_chunk = sb("per_chunk", [P, CHUNKS, width])
        hot = [sb(f"hot{n}", [P, G4 * P]) for n in range(DEEP)]
        p_a = [pb(f"a{n}", [P, P]) for n in range(2)]
        p_row = [pb(f"row{n}", [P, 512]) for n in range(DEEP)]
        p_out = [pb(f"out{n}", [P, 512]) for n in range(2)]
        if gather:
            taken = sb("taken", [P, PAIR, HROW])
            index = sb("indices", [P, PAIR], INT32)
        with nc.Block() as block:
            @block.tensor
            def _(pe):
                for w in range(width):
                    if w >= 2:
                        pe.wait_ge(turned_out, w - 1)
                    pe.transpose(p_a[w % 2][0:BLOCKS, 0:P], table[:, :, w], S.ident[:, :]).then_inc(turned, 1)
                for w in range(width):
                    pe.wait_ge(turned_out, w + 1)
                    if w >= 2:
                        pe.wait_ge(spread_out, w - 1)
                    pe.matmul(p_row[w % 2][:, 0:CHUNKS], tt[0:BLOCKS, w, :], E.block_hot[0:BLOCKS, :], start=True, stop=True).then_inc(spread, 1)
                pe.wait_ge(spread_out, width)

                def rows_of(g, c):
                    for j in range(G4):
                        ins = pe.matmul(p_row[g % DEEP][:, j * P:(j + 1) * P], E.local_b[:, bass.ds(c + j, 1)].to_broadcast([P, P]),
                                        S.ident_b[:, :], start=True, stop=True)
                    ins.then_inc(rows, 1)
                rows_of(0, 0)
                rows_of(1, G4)
                pe.sem_inc(found, DEEP)
                with pe.Fori(0, CHUNKS // 32) as i:
                    for h in range(2):
                        pe.wait_ge(stored, i * 2 + (h + 1))
                        for q in range(4):
                            g = 4 * h + q
                            rows_of(g + 2, i * 32 + G4 * (g + 2))
                            pe.wait_ge(hot_ready, i * 8 + (g + 1))
                            for j in range(G4):
                                c = q * G4 + j
                                ins = pe.matmul(p_out[h][:, c * width:(c + 1) * width], hot[g % DEEP][:, j * P:(j + 1) * P],
                                                per_chunk[:, bass.ds(i * 32 + (h * 16 + c), 1), :].rearrange("p a t -> p (a t)"), start=True, stop=True)
                            ins.then_inc(found, 1)

            @block.vector
            def _(v):
                with v.Fori(0, CHUNKS // 32) as i:
                    for g in range(8):
                        v.wait_ge(rows, i * 8 + (g + 1))
                        v.wait_ge(found, i * 8 + (g + 1))
                        v.tensor_scalar(hot[g % DEEP][:, :], p_row[g % DEEP][:, :], S.row[:, 0:1], None, ALU.is_equal).then_inc(hot_ready, 1)

            @block.scalar
            def _(act):
                for w in range(width):
                    act.wait_ge(turned, w + 1)
                    act.copy(tt[0:BLOCKS, w, :], p_a[w % 2][0:BLOCKS, 0:P]).then_inc(turned_out, 1)
                for w in range(width):
                    act.wait_ge(spread, w + 1)
                    act.copy(per_chunk[:, :, w], p_row[w % 2][:, 0:CHUNKS]).then_inc(spread_out, 1)
                act.sem_inc(stored, 2)
                if gather:
                    act.sem_inc(scores, 2)
                with act.Fori(0, CHUNKS // 32) as i:
                    for h in range(2):
                        act.wait_ge(found, i * 8 + (4 * h + 4 + DEEP))
                        act.copy(result[:, bass.ds(i * 32 + 16 * h, 16), :],
                                 p_out[h][:, 0:16 * width].rearrange("p (c w) -> p c w", w=width)).then_inc(stored, 1)
                        if gather:
                            for q in range(2):
                                for u in range(GRP):
                                    act.wait_ge(arrived[q * GRP + u], i * 32 + (before + 16 * h + 16))
                                act.copy(edge[:, bass.ds(i * 32 + (16 * h + GRP * q), GRP), 0:HEADS],
                                         taken[:, q * GRP:(q + 1) * GRP, CH:]).then_inc(scores, 1)

            if gather:
                @block.gpsimd
                def _(pool):
                    with pool.Fori(0, CHUNKS // PAIR) as i:
                        for u in range(PAIR):
                            if u % GRP == 0:
                                pool.wait_ge(spilled[u // GRP], i * 16 + 16)
                                pool.wait_ge(scores, i * 2 + (u // GRP + 1))
                                pool.sem_inc(passed, 1)
                                pool.tensor_copy(index[:, u:u + GRP], E.take[:, bass.ds(i * PAIR + u, GRP)]).then_inc(index_ready, 1)
                                pool.wait_ge(index_ready, i * 2 + (u // GRP + 1))
                                pool.sem_inc(passed, 1)
                            pool.indirect_dma_start(taken[:, u, :], None, node_table,
                                                    bass.IndirectOffsetOnAxis(ap=index[:, u:u + 1], axis=0)).then_inc(arrived[u], 16)

                @block.sync
                def _(sp):
                    for h in range(2):
                        sp.sem_inc(spilled[h], 16)
                    with sp.Fori(0, CHUNKS // PAIR) as i:
                        for h in range(2):
                            for u in range(GRP):
                                sp.wait_ge(arrived[h * GRP + u], i * 16 + (before + 16))
                            sp.dma_start(spill[:, bass.ds(i * PAIR + h * GRP, GRP), :], taken[:, h * GRP:(h + 1) * GRP, 0:CH]).then_inc(spilled[h], 16)
                    for h in range(2):
                        sp.wait_ge(spilled[h], 16 * (CHUNKS // PAIR + 1))


def type_weights(nc, S, E, sem, table):
    own = sem("tw_own")
    with ExitStack() as ctx:
        types = ctx.enter_context(nc.sbuf_tensor("types", [P, CHUNKS, TYPES], BF16))
        each = ctx.enter_context(nc.sbuf_tensor("tw_each", [P, CHUNKS, TYPES], FP32))
        look_up(nc, S, E, sem, "tw_", table, TYPES, each)
        with nc.Block() as block:
            @block.vector
            def _(v):
                step = Chain(v, own)
                for t in range(TYPES):
                    ins = v.tensor_scalar(types[:, :, t], S.etype[:, :], float(t), None, ALU.is_equal)
                step(ins)
                v.memset(S.weight[:, CHUNKS:], 0.0)
                step(v.tensor_tensor(each[:, :, :], each[:, :, :], types[:, :, :], ALU.mult))
                v.tensor_reduce(S.weight[:, 0:CHUNKS], each[:, :, :], AX.X, ALU.add)


def gather_and_add(nc, S, E, sem, name, table, acc, round_of_gathers, other=None):
    hot_ready, added, done, cleared = sem(name + "hot"), sem(name + "added"), sem(name + "done"), sem(name + "cleared")
    index_ready, passed = sem(name + "index"), sem(name + "passed")
    arrived, before = S.arrived, round_of_gathers * (CHUNKS // RING) * 16
    with ExitStack() as ctx:
        hot = ctx.enter_context(nc.sbuf_tensor(name + "hots", [P, PAIR, P], FP32))
        rows = ctx.enter_context(nc.sbuf_tensor(name + "rows", [P, RING, CH], FP32))
        index = ctx.enter_context(nc.sbuf_tensor(name + "indices", [P, RING], INT32))
        if other:
            other.buffers(nc, ctx, name)
        banks = [ctx.enter_context(nc.psum_tensor(f"{name}bank{u}", [P, 512], FP32)) for u in range(GRP // 2 if other else GRP)]
        with nc.Block() as block:
            @block.gpsimd
            def _(pool):
                with pool.Fori(0, CHUNKS // RING) as i:
                    for u in range(RING):
                        if u % GRP == 0:
                            pool.wait_ge(done, i * RING + (u + GRP))
                            pool.sem_inc(passed, 1)
                            pool.tensor_copy(index[:, u:u + GRP], E.take[:, bass.ds(i * RING + u, GRP)]).then_inc(index_ready, 1)
                            pool.wait_ge(index_ready, i * 4 + (u // GRP + 1))
                            pool.sem_inc(passed, 1)
                        pool.indirect_dma_start(rows[:, u, :], None, table,
                                                bass.IndirectOffsetOnAxis(ap=index[:, u:u + 1], axis=0)).then_inc(arrived[u], 16)

            @block.vector
            def _(v):
                v.memset(acc[:, :], 0.0).then_inc(cleared, 1)
                v.wait_ge(cleared, 1)

                def column(c, u):
                    v.wait_ge(other.moved, c + 1)
                    other.spread_column(v, S, c, u).then_inc(other.spread, 1)
                hot_and_add(nc, S, E, v, name, hot, S.weight, acc, CH, banks, hot_ready, added, done, column if other else None)
                if other:
                    v.wait_ge(other.moved, CPAD + STEP + 1)
                    step = Chain(v, other.own)
                    step.n = other.steps
                    other.decode(v, S, step, attention_decode(S, other))

            @block.tensor
            def _(pe):
                pe.sem_inc(done, RING)
                if other:
                    pe.sem_inc(other.moved, STEP)
                    other.open_sums(pe, S, True)
                with pe.Fori(0, CHUNKS // RING) as i:
                    for u in range(RING):
                        pe.wait_ge(hot_ready, i * RING + (u + 1))
                        pe.wait_ge(added, i * RING + (u + 1))
                        pe.wait_ge(arrived[u], i * 16 + (before + 16))
                        pe.matmul(banks[u % len(banks)][:, 0:CH], hot[:, u % PAIR, :], rows[:, u, :], start=True, stop=True).then_inc(done, 1)
                        if other:
                            pe.wait_ge(other.spread, i * RING + (u + 1))
                            other.move_column(pe, u % STEP).then_inc(other.moved, 1)
                if other:
                    other.open_sums(pe, S, False).then_inc(other.moved, 1)


def blocks_of(tile):
    return tile[:, :].rearrange("p (b w) -> p b w", b=BLOCKS)


def over_blocks(row):
    return row.unsqueeze(1).to_broadcast([P, BLOCKS, row.shape[1]])


def group_norm(nc, S, sem, name, feat, norm, gn_w, gn_b):
    loaded, own, summed, centered, squared, rooted = (sem(name + n) for n in ("loaded", "own", "summed", "centered", "squared", "rooted"))
    with ExitStack() as ctx:
        sq = ctx.enter_context(nc.sbuf_tensor(name + "sq", [P, BLOCKS, CH], FP32))
        grp = ctx.enter_context(nc.sbuf_tensor(name + "grp", [P, GROUPS], FP32))
        eps = ctx.enter_context(nc.sbuf_tensor(name + "eps", [P, 1], FP32))
        scale = ctx.enter_context(nc.sbuf_tensor(name + "scale", [P, CH], FP32))
        bias = ctx.enter_context(nc.sbuf_tensor(name + "bias", [P, CH], FP32))
        sums = [ctx.enter_context(nc.psum_tensor(f"{name}sums{n}", [P, CH], FP32)) for n in range(2)]
        inv_count = 1.0 / (NODES * (CH // GROUPS) + EPS)
        with nc.Block() as block:
            @block.sync
            def _(sp):
                sp.dma_start(scale[:, :], gn_w[0, :].partition_broadcast(P)).then_inc(loaded, 16)
                sp.dma_start(bias[:, :], gn_b[0, :].partition_broadcast(P)).then_inc(loaded, 16)
                sp.wait_ge(loaded, 32)

            @block.tensor
            def _(pe):
                def column_sums(out, x):
                    pe.matmul(out, S.ones[:, :], x[:, 0, :], start=True, stop=False)
                    with pe.Fori(1, BLOCKS - 1) as b:
                        pe.matmul(out, S.ones[:, :], x[:, bass.ds(b, 1), :].rearrange("p a c -> p (a c)"), start=False, stop=False)
                    pe.matmul(out, S.ones[0:LAST, :], x[0:LAST, BLOCKS - 1, :], start=False, stop=True).then_inc(summed, 1)
                column_sums(sums[0][:, :], feat)
                pe.wait_ge(squared, 1)
                column_sums(sums[1][:, :], sq)

            @block.scalar
            def _(act):
                act.wait_ge(centered, 1)
                act.activation(sq[:, :, :], norm[:, :, :], ACT.Square).then_inc(squared, 1)
                act.wait_ge(centered, 2)
                act.activation(grp[:, :], grp[:, :], ACT.Sqrt, bias=eps[:, 0:1]).then_inc(rooted, 1)

            @block.vector
            def _(v):
                step = Chain(v, own)
                v.memset(eps[:, :], EPS)
                for n in range(2):
                    v.wait_ge(summed, n + 1)
                    step(v.tensor_reduce(grp[:, :], sums[n][:, :].rearrange("p (g c) -> p g c", g=GROUPS), AX.X, ALU.add))
                    if n == 0:
                        step(v.tensor_scalar(grp[:, :], grp[:, :], inv_count, None, ALU.mult))
                        mean = grp[:, :].unsqueeze(1).unsqueeze(3).to_broadcast([P, BLOCKS, GROUPS, CH // GROUPS])
                        v.tensor_tensor(norm[:, :, :].rearrange("p b (g c) -> p b g c", g=GROUPS),
                                        feat.rearrange("p b (g c) -> p b g c", g=GROUPS), mean, ALU.subtract).then_inc(centered, 1)
                        v.wait_ge(centered, 1)
                    else:
                        v.tensor_scalar(grp[:, :], grp[:, :], inv_count, None, ALU.mult).then_inc(centered, 1)
                v.wait_ge(rooted, 1)
                step(v.reciprocal(grp[:, :], grp[:, :]))
                v.wait_ge(loaded, 32)
                sc = scale[:, :].rearrange("p (g c) -> p g c", g=GROUPS)
                step(v.tensor_tensor(sc, sc, grp[:, :].unsqueeze(2).to_broadcast([P, GROUPS, CH // GROUPS]), ALU.mult))
                step(v.tensor_tensor(norm[:, :, :], norm[:, :, :], over_blocks(scale[:, :]), ALU.mult))
                v.tensor_tensor(norm[:, :, :], norm[:, :, :], over_blocks(bias[:, :]), ALU.add)


def typed_features(nc, S, sem, name, norm, conv_w, table, move=None, rank=None):
    U = 5
    QUARTS = [(0, 512), (512, 512), (1024, 512), (1536, 256)]
    NQ = len(QUARTS)
    W = TYPES * CH
    loaded, acted, turned, turned_out, made, out = (sem(name + n) for n in ("loaded", "acted", "turned", "turned_out", "made", "out"))
    stored = [sem(f"{name}stored{n}") for n in range(U)]
    with ExitStack() as ctx:
        def sb(n, shape, dt=FP32):
            return ctx.enter_context(nc.sbuf_tensor(name + n, shape, dt))

        def pb(n):
            return ctx.enter_context(nc.psum_tensor(name + n, [P, 512], FP32))
        w_sb = sb("w", [P, KC, TYPES, CH])
        h = [sb(f"h{u}", [P, CH]) for u in range(U)]
        ht = [sb(f"ht{u}", [P, KC * P]) for u in range(U)]
        y = [sb(f"y{n}", [P, W]) for n in range(U)]
        p_t = pb("p_t")
        p_y = [pb(f"py{n}") for n in range(NQ)]
        if move:
            E, counts = move
            E.buffers(nc, ctx, name)
            nodes, bins = sb("nodes", [P, STEP, P], FP16), sb("bins", [P, STEP, BINS + 1], FP16)
            p_bins = pb("bins_p")
        if rank:
            R, payload = rank
            p_cnt = pb("p_cnt")
        out_rows = table.rearrange("(t n) c -> n t c", t=TYPES)
        with nc.Block() as block:
            @block.sync
            def _(sp):
                for k in range(KC):
                    sp.dma_start(w_sb[:, k, :, :], conv_w.rearrange("(t k p) n -> k p t n", t=TYPES, k=KC)[k]).then_inc(loaded, 16)
                for u in range(U):
                    sp.sem_inc(stored[u], 16)
                with sp.Fori(0, BLOCKS // U) as i:
                    for u in range(U):
                        sp.wait_ge(out, (i * U + (u + 2)) * NQ)
                        sp.dma_start(out_rows[bass.ds((i * U + u) * P, P), :, :], y[u][:, :].rearrange("p (t c) -> p t c", t=TYPES)).then_inc(stored[u], 16)
                for u in range(U):
                    sp.wait_ge(stored[u], 16 * (BLOCKS // U + 1))

            @block.scalar
            def _(act):
                def silu(b, u):
                    act.activation(h[u][:, :], norm[:, bass.ds(b, 1), :].rearrange("p a c -> p (a c)"), ACT.Silu).then_inc(acted, 1)

                def turn_out(b, u):
                    act.wait_ge(turned, b + 1)
                    act.copy(ht[u][:, :], p_t[:, 0:KC * P]).then_inc(turned_out, 1)

                def copy_out(i, u):
                    act.wait_ge(stored[u], i * 16 + 16)
                    for q, (a, n) in enumerate(QUARTS):
                        act.wait_ge(made, (i * U + u) * NQ + (q + 1))
                        act.copy(y[u][:, a:a + n], p_y[q][:, 0:n]).then_inc(out, 1)
                act.sem_inc(out, NQ)
                for u in range(U):
                    silu(u, u)
                turn_out(0, 0)
                with act.Fori(0, BLOCKS // U - 1) as i:
                    for u in range(U):
                        turn_out(i * U + (u + 1), (u + 1) % U)
                        copy_out(i, u)
                        silu(i * U + (u + U), u)
                for u in range(U):
                    if u + 1 < U:
                        turn_out(BLOCKS - U + u + 1, u + 1)
                    copy_out(BLOCKS // U - 1, u)

            @block.tensor
            def _(pe):
                pe.wait_ge(loaded, 16 * KC)

                def turn(b, u):
                    pe.wait_ge(acted, b + 1)
                    for k in range(KC):
                        ins = pe.transpose(p_t[:, k * P:(k + 1) * P], h[u][:, k * P:(k + 1) * P], S.ident[:, :])
                    ins.then_inc(turned, 1)

                def multiply(b, u, more):
                    pe.wait_ge(turned_out, b + 1)
                    if more:
                        turn(b + 1, (u + 1) % U)
                    for q, (a, n) in enumerate(QUARTS):
                        pe.wait_ge(out, b * NQ + (q + 1))
                        for k in range(KC):
                            ins = pe.matmul(p_y[q][:, 0:n], ht[u][:, k * P:(k + 1) * P],
                                            w_sb[:, k, :, :].rearrange("p t n -> p (t n)")[:, a:a + n], start=(k == 0), stop=(k == KC - 1))
                        ins.then_inc(made, 1)

                def columns(b):
                    for s in range(STEP):
                        pe.wait_ge(E.spread, b * STEP + (s + 1))
                        pe.matmul(p_bins[:, 0:BINS], nodes[:, s, :], bins[:, s, 0:BINS], start=False, stop=False)
                        E.move_column(pe, s).then_inc(E.moved, 1)
                if move:
                    pe.sem_inc(E.moved, STEP)
                    pe.matmul(p_bins[:, 0:BINS], S.zeros[:, 0:P], S.zeros[:, 0:BINS], start=True, stop=False)
                    E.open_sums(pe, S, True)
                if rank:
                    R.totals(pe, S, p_cnt)
                turn(0, 0)
                with pe.Fori(0, BLOCKS // U - 1) as i:
                    for u in range(U):
                        multiply(i * U + u, u, True)
                        if move:
                            columns(i * U + u)
                for u in range(U):
                    multiply(BLOCKS - U + u, u, u + 1 < U)
                    if move:
                        columns(BLOCKS - U + u)
                if move:
                    pe.matmul(p_bins[:, 0:BINS], S.zeros[:, 0:P], S.zeros[:, 0:BINS], start=False, stop=True)
                    E.open_sums(pe, S, False).then_inc(E.moved, 1)

            @block.vector
            def _(v):
                if move:
                    with v.Fori(0, BLOCKS) as i:
                        for s in range(STEP):
                            c = i * STEP + s
                            v.wait_ge(E.moved, c + 1)
                            v.tensor_scalar(nodes[:, s, :], S.col_h[:, 0:P], S.key_lane[:, bass.ds(c, 1)], None, ALU.is_equal)
                            v.tensor_scalar(bins[:, s, :], S.col_h[:, 0:BINS + 1], S.key_bin[:, bass.ds(c, 1)], None, ALU.is_equal)
                            E.spread_column(v, S, c, s).then_inc(E.spread, 1)
                    v.wait_ge(E.moved, BLOCKS * STEP + STEP + 1)
                    step = Chain(v, E.own)
                    step.n = E.steps
                    step(v.tensor_scalar(counts[:, :, :], p_bins[:, 0:BINS].rearrange("p (b t) -> p b t", t=TYPES), 1.0, None, ALU.max))
                    v.reciprocal(counts[:, :, :], counts[:, :, :])
                    E.decode(v, S, step, conv_decode(S, E))
                if rank:
                    step = Chain(v, R.own)
                    R.ranks(v, S, step, payload, p_cnt)
                    R.steps = step.n


def layer_norm(nc, S, sem, name, x):
    own, centered, squared, rooted = (sem(name + n) for n in ("own", "centered", "squared", "rooted"))
    with ExitStack() as ctx:
        sq = ctx.enter_context(nc.sbuf_tensor(name + "sq", [P, BLOCKS, CH], FP32))
        mean = ctx.enter_context(nc.sbuf_tensor(name + "mean", [P, BLOCKS], FP32))
        eps = ctx.enter_context(nc.sbuf_tensor(name + "eps", [P, 1], FP32))

        def wide(stat):
            return stat[:, :].unsqueeze(2).to_broadcast([P, BLOCKS, CH])
        with nc.Block() as block:
            @block.vector
            def _(v):
                step = Chain(v, own)
                v.memset(eps[:, :], EPS)
                step(v.tensor_reduce(mean[:, :], x[:, :, :], AX.X, ALU.add))
                step(v.tensor_scalar(mean[:, :], mean[:, :], 1.0 / CH, None, ALU.mult))
                v.tensor_tensor(x[:, :, :], x[:, :, :], wide(mean), ALU.subtract).then_inc(centered, 1)
                v.wait_ge(squared, 1)
                step(v.tensor_reduce(mean[:, :], sq[:, :, :], AX.X, ALU.add))
                v.tensor_scalar(mean[:, :], mean[:, :], 1.0 / CH, None, ALU.mult).then_inc(centered, 1)
                v.wait_ge(rooted, 1)
                step(v.reciprocal(mean[:, :], mean[:, :]))
                v.tensor_tensor(x[:, :, :], x[:, :, :], wide(mean), ALU.mult)

            @block.scalar
            def _(act):
                act.wait_ge(centered, 1)
                act.activation(sq[:, :, :], x[:, :, :], ACT.Square).then_inc(squared, 1)
                act.wait_ge(centered, 2)
                act.activation(mean[:, :], mean[:, :], ACT.Sqrt, bias=eps[:, 0:1]).then_inc(rooted, 1)


def attention_features(nc, S, sem, name, x, w, a_src, a_dst, heads, h, own_scores, table):
    U = 5
    loaded, copied, turned, turned_out, made, made_out, own, stored = (
        sem(name + n) for n in ("loaded", "copied", "turned", "turned_out", "made", "made_out", "own", "stored"))
    with ExitStack() as ctx:
        def sb(n, shape, dt=FP32):
            return ctx.enter_context(nc.sbuf_tensor(name + n, shape, dt))
        w_sb = sb("w", [P, KC, CH])
        a_sb = sb("a", [P, 2, CH])
        xs = [sb(f"x{u}", [P, CH]) for u in range(U)]
        xt = [sb(f"xt{u}", [P, KC * P]) for u in range(U)]
        prod = sb("prod", [P, BLOCKS, CH])
        p_t = [ctx.enter_context(nc.psum_tensor(f"{name}t{n}", [P, KC * P], FP32)) for n in range(2)]
        p_h = [ctx.enter_context(nc.psum_tensor(f"{name}h{n}", [P, CH], FP32)) for n in range(2)]
        with nc.Block() as block:
            @block.sync
            def _(sp):
                sp.dma_start(w_sb[:, :, :], w.rearrange("(k p) n -> p k n", k=KC)).then_inc(loaded, 16)
                for n, a in enumerate((a_src, a_dst)):
                    sp.dma_start(a_sb[:, n, :], a.rearrange("h c -> (h c)").partition_broadcast(P)).then_inc(loaded, 16)
                sp.wait_ge(own, 3 if heads == 1 else 2)
                sp.dma_start(table.rearrange("(b p) c -> p b c", p=P), h[:, :, :]).then_inc(stored, 16)
                sp.wait_ge(stored, 16)

            @block.scalar
            def _(act):
                def stage(b, u):
                    act.copy(xs[u][:, :], x[:, bass.ds(b, 1), :].rearrange("p a c -> p (a c)")).then_inc(copied, 1)

                def copy_out(b, n):
                    act.wait_ge(made, b + 1)
                    act.copy(h[:, bass.ds(b, 1), 0:CH].rearrange("p a c -> p (a c)"), p_h[n][:, :]).then_inc(made_out, 1)
                act.sem_inc(made_out, 1)
                for u in range(U):
                    stage(u, u)
                with act.Fori(0, BLOCKS // U - 1) as i:
                    for u in range(U):
                        copy_out(i * U + u, 0 if u % 2 else 1)
                        act.wait_ge(turned, i * U + (u + 1))
                        stage(i * U + (u + U), u)
                for u in range(U):
                    copy_out(BLOCKS - U + u, 0 if u % 2 else 1)

            @block.tensor
            def _(pe):
                pe.wait_ge(loaded, 48)
                with pe.Fori(0, BLOCKS // U) as i:
                    for u in range(U):
                        pe.wait_ge(copied, i * U + (u + 1))
                        for k in range(KC):
                            ins = pe.transpose(p_t[u % 2][:, k * P:(k + 1) * P], xs[u][:, k * P:(k + 1) * P], S.ident[:, :])
                        ins.then_inc(turned, 1)
                        pe.wait_ge(turned_out, i * U + (u + 1))
                        pe.wait_ge(made_out, i * U + (u + 1))
                        for k in range(KC):
                            ins = pe.matmul(p_h[0 if u % 2 else 1][:, :], xt[u][:, k * P:(k + 1) * P], w_sb[:, k, :], start=(k == 0), stop=(k == KC - 1))
                        ins.then_inc(made, 1)

            @block.vector
            def _(v):
                with v.Fori(0, BLOCKS // U) as i:
                    for u in range(U):
                        v.wait_ge(turned, i * U + (u + 1))
                        v.tensor_copy(xt[u][:, :], p_t[u % 2][:, :]).then_inc(turned_out, 1)
                step = Chain(v, own)
                v.wait_ge(loaded, 48)
                v.wait_ge(made_out, BLOCKS + 1)
                for n, out in ((0, h[:, :, CH:]), (1, own_scores[:, :, 0:HEADS])):
                    step(v.tensor_tensor(prod[:, :, :], h[:, :, 0:CH], over_blocks(a_sb[:, n, :]), ALU.mult))
                    if heads == 1:
                        step(v.tensor_reduce(own_scores[:, :, 2 * HEADS - 1], prod[:, :, :], AX.X, ALU.add))
                        step(v.tensor_copy(out, own_scores[:, :, 2 * HEADS - 1:].to_broadcast([P, BLOCKS, HEADS])))
                    else:
                        step(v.tensor_reduce(out, prod[:, :, :].rearrange("p b (h c) -> p b h c", h=heads), AX.X, ALU.add))
                own_logit = own_scores[:, :, HEADS:]
                step(v.tensor_tensor(own_logit, h[:, :, CH:], own_scores[:, :, 0:HEADS], ALU.add))
                v.scalar_tensor_tensor(own_logit, own_logit, SLOPE, own_logit, ALU.mult, ALU.max)


STRIPS = P // HEADS
SCH = CHUNKS // STRIPS
SLEN = SCH * P


def softmax_weights(nc, S, E, sem, name, edge):
    own, prepared, turned, turned_out, given, passed = (
        sem(name + n) for n in ("own", "prepared", "turned", "turned_out", "given", "passed"))
    weighed, nodes_staged, logits_staged = sem(name + "weighed"), sem(name + "nodes_staged"), sem(name + "logits_staged")
    QUADS = [(j, min(4, SCH - j)) for j in range(0, SCH, 4)]
    NQ = len(QUADS)
    with ExitStack() as ctx:
        def sb(n, shape, dt=FP32):
            return ctx.enter_context(nc.sbuf_tensor(name + n, shape, dt))
        peak = sb("peak", [P, SLEN])
        fwd = sb("fwd", [P, SLEN])
        reset = sb("reset", [P, SLEN + 1])
        node = sb("node", [P, CHUNKS])
        ends = sb("ends", [P, 2])
        row = sb("row", [1, 2 * P])
        carry = sb("carry", [1, P + HEADS])
        init = sb("init", [P, 1])
        p_b = [ctx.enter_context(nc.psum_tensor(f"{name}b{n}", [P, 512], FP32)) for n in range(4)]
        p_s = ctx.enter_context(nc.psum_tensor(name + "s", [P, 512], FP32))
        e0, e1, e2 = (edge[:, :, n * HEADS:(n + 1) * HEADS] for n in range(3))
        strips = [e.rearrange("p (i j) h -> p i j h", i=STRIPS) for e in (e0, e1, e2)]

        def staged(tile):
            return tile[:, 0:SLEN].rearrange("p (j i h) -> p j i h", j=SCH, i=STRIPS)

        with nc.Block() as block:
            @block.vector
            def _(v):
                step = Chain(v, own)
                give = Chain(v, given)
                step(v.tensor_tensor(e0, e0, e1, ALU.add))
                v.scalar_tensor_tensor(e0, e0, SLOPE, e0, ALU.mult, ALU.max).then_inc(prepared, 1)
                step(v.scalar_tensor_tensor(node[:, :], E.block_of[:, 0:CHUNKS], 256.0, E.local[:, 0:CHUNKS], ALU.mult, ALU.add))
                step(v.tensor_scalar(node[:, :], node[:, :], 2.0, None, ALU.add))
                v.tensor_copy(staged(reset), node[:, :].rearrange("p (i j) -> p j i", i=STRIPS).unsqueeze(3).to_broadcast([P, SCH, STRIPS, HEADS])).then_inc(nodes_staged, 1)
                n = 0
                for out in (peak, fwd):
                    for j, m in QUADS:
                        n += 1
                        v.wait_ge(turned, n)
                        v.tensor_copy(out[:, j * P:(j + m) * P], p_b[(n - 1) % 4][:, 0:m * P]).then_inc(turned_out, 1)
                v.wait_ge(turned_out, n)
                step(v.scalar_tensor_tensor(reset[:, 1:SLEN], fwd[:, 1:SLEN], 1.0, fwd[:, 0:SLEN - 1], ALU.mult, ALU.not_equal))
                give(v.tensor_copy(ends[:, 0:1], fwd[:, SLEN - 1:SLEN]))
                v.wait_ge(passed, 1)
                give(v.tensor_tensor(reset[:, 0:1], fwd[:, 0:1], p_s[:, 0:1], ALU.not_equal))
                v.wait_ge(passed, 2)
                step(v.tensor_copy(reset[:, SLEN:], p_s[:, 1:2]))
                step(v.tensor_scalar(reset[:, :], reset[:, :], -BIG, None, ALU.mult))

                def running_maximum(out, resets, x, last, back):
                    turn = (lambda ap: ap[:, ::-1]) if back else (lambda ap: ap)
                    step(v.tensor_tensor_scan(turn(out), turn(resets), turn(x), -BIG, ALU.add, ALU.max))
                    step(v.tensor_copy(ends[:, 0:1], out[:, last:last + 1]))
                    give(v.tensor_reduce(ends[:, 1:2], resets, AX.X, ALU.min))
                    step(v.memset(carry[:, :], -BIG))
                    v.wait_ge(passed, 5 if back else 3)
                    step(v.tensor_copy(row[:, :], p_s[0:1, P:3 * P]))
                    for h in range(HEADS):
                        state, hold = row[0:1, h:P:HEADS], row[0:1, P + h:2 * P:HEADS]
                        shifted = carry[0:1, h:P:HEADS] if back else carry[0:1, HEADS + h:HEADS + P:HEADS]
                        scan = v.tensor_tensor_scan(turn(shifted), turn(hold), turn(state), -BIG, ALU.add, ALU.max)
                        if h == HEADS - 1:
                            give(scan)
                    v.wait_ge(passed, 6 if back else 4)
                    step(v.tensor_copy(init[:, :], p_s[:, 2:3]))
                    return v.tensor_tensor_scan(turn(out), turn(resets), turn(x), init[:, 0:1], ALU.add, ALU.max)
                step(running_maximum(fwd[:, :], reset[:, 0:SLEN], peak[:, :], SLEN - 1, False))
                give(running_maximum(peak[:, :], reset[:, 1:], fwd[:, :], 0, True))
                give(v.tensor_scalar(fwd[:, :], reset[:, 1:], -1.0 / BIG, None, ALU.mult))
                for j, m in QUADS:
                    n += 1
                    v.wait_ge(turned, n)
                    part = strips[2][:, :, j:j + m, :].rearrange("p i j h -> p j i h")
                    out = strips[1][:, :, j:j + m, :].rearrange("p i j h -> p j i h")
                    src = p_b[(n - 1) % 4][:, 0:m * P].rearrange("p (j i h) -> p j i h", j=m, i=STRIPS)
                    v.tensor_tensor(out, src, part, ALU.max).then_inc(turned_out, 1)
                v.wait_ge(turned_out, n)
                v.tensor_tensor(e0, e0, e1, ALU.subtract).then_inc(weighed, 1)
                for j, m in QUADS:
                    n += 1
                    v.wait_ge(turned, n)
                    out = strips[2][:, :, j:j + m, :].rearrange("p i j h -> p j i h")
                    src = p_b[(n - 1) % 4][:, 0:m * P].rearrange("p (j i h) -> p j i h", j=m, i=STRIPS)
                    v.tensor_copy(out, src).then_inc(turned_out, 1)
                v.wait_ge(turned_out, n)
                v.tensor_tensor(e1, e1, e2, ALU.mult)

            @block.scalar
            def _(act):
                act.wait_ge(prepared, 1)
                act.copy(staged(fwd), strips[0].rearrange("p i j h -> p j i h")).then_inc(logits_staged, 1)
                act.wait_ge(weighed, 1)
                act.activation(e0, e0, ACT.Exp)

            @block.tensor
            def _(pe):
                n = 0

                def turn(j, m, view):
                    nonlocal n
                    if n >= 4:
                        pe.wait_ge(turned_out, n - 3)
                    for q in range(m):
                        ins = pe.transpose(p_b[n % 4][:, q * P:(q + 1) * P], view(j + q), S.ident[:, :])
                    ins.then_inc(turned, 1)
                    n += 1
                for ready, strip in ((logits_staged, fwd), (nodes_staged, reset)):
                    pe.wait_ge(ready, 1)
                    for j, m in QUADS:
                        turn(j, m, lambda c: strip[:, c * P:(c + 1) * P])
                pe.wait_ge(given, 1)
                pe.matmul(p_s[:, 0:1], S.down[:, :], ends[:, 0:1], start=True, stop=True).then_inc(passed, 1)
                pe.wait_ge(given, 2)
                pe.matmul(p_s[:, 1:2], S.up[:, :], reset[:, 0:1], start=True, stop=True).then_inc(passed, 1)
                for back in range(2):
                    pe.wait_ge(given, 3 + 2 * back)
                    pe.transpose(p_s[0:1, P:2 * P], ends[:, 0:1], S.ident[:, :])
                    pe.transpose(p_s[0:1, 2 * P:3 * P], ends[:, 1:2], S.ident[:, :]).then_inc(passed, 1)
                    pe.wait_ge(given, 4 + 2 * back)
                    pe.matmul(p_s[:, 2:3], carry[0:1, back * HEADS:back * HEADS + P], S.ones[0:1, 0:1], start=True, stop=True).then_inc(passed, 1)
                for w, strip in enumerate((peak, fwd)):
                    pe.wait_ge(given, 7 + w)
                    for j, m in QUADS:
                        turn(j, m, lambda c: strip[:, c * P:(c + 1) * P])


def weighted_sum(nc, S, E, sem, name, edge, spill, acc):
    hot_ready, added, done, cleared, mixed, beside = (sem(name + n) for n in ("hot", "added", "done", "cleared", "mixed", "beside"))
    QUARTS = RING // GRP
    arrived = [sem(f"{name}row{q}") for q in range(QUARTS)]
    with ExitStack() as ctx:
        hot = ctx.enter_context(nc.sbuf_tensor(name + "hots", [P, PAIR, P], FP32))
        rows = ctx.enter_context(nc.sbuf_tensor(name + "rows", [P, RING, ACCW], FP32))
        banks = [ctx.enter_context(nc.psum_tensor(f"{name}bank{u}", [P, 512], FP32)) for u in range(GRP)]

        def quarter(q):
            return rows[:, q * GRP:(q + 1) * GRP, :]
        with nc.Block() as block:
            @block.sync
            def _(sp):
                with sp.Fori(0, CHUNKS // RING) as i:
                    for q in range(QUARTS):
                        sp.wait_ge(done, i * RING + GRP * (q + 1))
                        sp.dma_start(quarter(q)[:, :, 0:CH], spill[:, bass.ds(i * RING + q * GRP, GRP), :]).then_inc(arrived[q], 16)

            @block.gpsimd
            def _(pool):
                with pool.Fori(0, CHUNKS // RING) as i:
                    for q in range(QUARTS):
                        pool.wait_ge(arrived[q], i * 16 + 16)
                        part = quarter(q)[:, :, 0:CH].rearrange("p a (h c) -> p a h c", h=HEADS)
                        weight = edge[:, bass.ds(i * RING + q * GRP, GRP), 0:HEADS].unsqueeze(3).to_broadcast([P, GRP, HEADS, HC])
                        pool.tensor_tensor(part, part, weight, ALU.mult).then_inc(mixed, 1)

            @block.scalar
            def _(act):
                with act.Fori(0, CHUNKS // RING) as i:
                    for q in range(QUARTS):
                        act.wait_ge(done, i * RING + GRP * (q + 1))
                        act.copy(quarter(q)[:, :, CH:], edge[:, bass.ds(i * RING + q * GRP, GRP), :]).then_inc(beside, 1)

            @block.vector
            def _(v):
                v.memset(acc[:, :], 0.0).then_inc(cleared, 1)
                v.wait_ge(cleared, 1)
                hot_and_add(nc, S, E, v, name, hot, None, acc, ACCW, banks, hot_ready, added, done)

            @block.tensor
            def _(pe):
                pe.sem_inc(done, RING)
                with pe.Fori(0, CHUNKS // RING) as i:
                    for u in range(RING):
                        pe.wait_ge(hot_ready, i * RING + (u + 1))
                        pe.wait_ge(added, i * RING + (u + 1))
                        if u % GRP == 0:
                            pe.wait_ge(mixed, i * QUARTS + (u // GRP + 1))
                            pe.wait_ge(beside, i * QUARTS + (u // GRP + 1))
                        pe.matmul(banks[u % GRP][:, 0:ACCW], hot[:, u % PAIR, :], rows[:, u, :], start=True, stop=True).then_inc(done, 1)


def finish_attention(nc, S, sem, name, acc, h, own_scores, b, result, relu):
    own, loaded, lowered, weighed = (sem(name + n) for n in ("own", "loaded", "lowered", "weighed"))
    with ExitStack() as ctx:
        bias = ctx.enter_context(nc.sbuf_tensor(name + "bias", [P, CH], FP32))
        weight = ctx.enter_context(nc.sbuf_tensor(name + "weight", [P, BLOCKS, HEADS], FP32))
        total = ctx.enter_context(nc.sbuf_tensor(name + "total", [P, BLOCKS, HEADS], FP32))
        A = blocks_of(acc)
        own_logit = own_scores[:, :, HEADS:]

        def per_head(ap):
            return ap.rearrange("p b (h c) -> p b h c", h=HEADS)

        def wide(ap):
            return ap[:, :, :].unsqueeze(3).to_broadcast([P, BLOCKS, HEADS, HC])
        with nc.Block() as block:
            @block.sync
            def _(sp):
                sp.dma_start(bias[:, :], b.partition_broadcast(P)).then_inc(loaded, 16)
                sp.wait_ge(loaded, 16)

            @block.scalar
            def _(act):
                act.wait_ge(lowered, 1)
                act.activation(weight[:, :, :], weight[:, :, :], ACT.Exp).then_inc(weighed, 1)

            @block.vector
            def _(v):
                step = Chain(v, own)
                step(v.tensor_scalar(weight[:, :, :], A[:, :, CH + 2 * HEADS:], -1.0, 1.0, ALU.mult, ALU.add))
                step(v.tensor_tensor(weight[:, :, :], weight[:, :, :], own_logit, ALU.mult))
                step(v.tensor_tensor(weight[:, :, :], weight[:, :, :], A[:, :, CH + HEADS:CH + 2 * HEADS], ALU.add))
                v.tensor_tensor(weight[:, :, :], own_logit, weight[:, :, :], ALU.subtract).then_inc(lowered, 1)
                v.wait_ge(weighed, 1)
                step(v.scalar_tensor_tensor(total[:, :, :], A[:, :, CH:CH + HEADS], 1e-16, weight[:, :, :], ALU.add, ALU.add))
                step(v.reciprocal(total[:, :, :], total[:, :, :]))
                step(v.tensor_tensor(per_head(h[:, :, 0:CH]), per_head(h[:, :, 0:CH]), wide(weight), ALU.mult))
                step(v.tensor_tensor(result[:, :, :], h[:, :, 0:CH], A[:, :, 0:CH], ALU.add))
                step(v.tensor_tensor(per_head(result[:, :, :]), per_head(result[:, :, :]), wide(total), ALU.mult))
                v.wait_ge(loaded, 16)
                step(v.tensor_tensor(result[:, :, :], result[:, :, :], over_blocks(bias[:, :]), ALU.add))
                if relu:
                    v.tensor_scalar(result[:, :, :], result[:, :, :], 0.0, None, ALU.max)


def attention_layer(nc, S, E, name, x, w, a_src, a_dst, b, heads, acc, result, relu, node_table, spill, round_of_gathers):
    with ExitStack() as ctx:
        def sb(n, shape, dt=FP32):
            return ctx.enter_context(nc.sbuf_tensor(name + n, shape, dt))
        h = sb("h", [P, BLOCKS, HROW])
        own_scores = sb("own_scores", [P, BLOCKS, 2 * HEADS])
        with Semaphores(nc) as sem:
            attention_features(nc, S, sem, name + "f_", x, w, a_src, a_dst, heads, h, own_scores, node_table)
        with ExitStack() as inner:
            edge = inner.enter_context(nc.sbuf_tensor(name + "edge", [P, CHUNKS, 3 * HEADS], FP32))
            with Semaphores(nc) as sem:
                look_up(nc, S, E, sem, name + "l_", own_scores, 2 * HEADS, edge[:, :, HEADS:], (node_table, edge, spill, round_of_gathers))
            with Semaphores(nc) as sem:
                softmax_weights(nc, S, E, sem, name + "s_", edge)
                weighted_sum(nc, S, E, sem, name + "w_", edge, spill, acc)
        with Semaphores(nc) as sem:
            finish_attention(nc, S, sem, name + "n_", acc, h, own_scores, b, result, relu)


def gnn(nc, x, src, dst, edge_type_7, L0_gnn_gn1_w, L0_gnn_gn1_b, L0_gnn_conv1_w, L0_gnn_gn2_w, L0_gnn_gn2_b, L0_gnn_conv2_w,
        L1_gnn_W1, L1_gnn_att_src1, L1_gnn_att_dst1, L1_gnn_b1, L1_gnn_W2, L1_gnn_att_src2, L1_gnn_att_dst2, L1_gnn_b2, out):
    WIDE = CHUNKS + EXTRA
    feature_table = nc.dram_tensor("feature_table", [TYPES * TROWS, CH], FP32).ap()
    node_table = nc.dram_tensor("node_table", [BLOCKS * P, HROW], FP32).ap()
    spill = nc.dram_tensor("spill", [P, CHUNKS, CH], FP32).ap()
    with ExitStack() as ctx:
        S = Shared()

        def keep(stack, n, shape, dt=FP32):
            return stack.enter_context(nc.sbuf_tensor(n, shape, dt))
        S.arrived = [ctx.enter_context(nc.semaphore(f"arrived{u}")) for u in range(RING)]
        S.col = keep(ctx, "col", [P, WIDE])
        S.col_h = keep(ctx, "col_h", [P, CHUNKS], FP16)
        S.row = keep(ctx, "row", [P, 1])
        S.ident = keep(ctx, "ident", [P, P])
        S.ident_b = keep(ctx, "ident_b", [P, P], BF16)
        S.above = keep(ctx, "above", [P, P])
        S.down = keep(ctx, "down", [P, P])
        S.up = keep(ctx, "up", [P, P])
        S.ones = keep(ctx, "ones", [P, P])
        S.zeros = keep(ctx, "zeros", [P, CHUNKS], FP16)
        x_sb = ctx.enter_context(nc.sbuf_tensor("x_sb", [P, BLOCKS, CH], FP32))
        acc = ctx.enter_context(nc.sbuf_tensor("acc", [P, BLOCKS * ACCW], FP32))
        sums = blocks_of(acc)[:, :, 0:CH]

        def lasting(name):
            return ctx.enter_context(nc.semaphore(name))
        by_dst = Placement(nc, ctx, lasting, "by_dst_", None, 12)
        with ExitStack() as conv:
            by_src = Placement(nc, conv, lasting, "by_src_", None, 15)
            S.col_i = keep(conv, "col_i", [P, WIDE], INT32)
            S.row_i = keep(conv, "row_i", [P, 1], INT32)
            S.weight = keep(conv, "weight", [P, WIDE])
            S.etype = keep(conv, "etype", [P, CHUNKS])
            counts = keep(conv, "counts", [P, BLOCKS, TYPES])
            with ExitStack() as lists:
                S.src_i = keep(lists, "src_i", [P, CPAD], INT32)
                S.dst_i = keep(lists, "dst_i", [P, CPAD], INT32)
                by_src.key_i, by_dst.key_i = S.src_i, S.dst_i
                with ExitStack() as types:
                    S.type_i = keep(types, "type_i", [P, CPAD], INT32)
                    S.pay = keep(types, "pay", [P, CPAD])
                    S.key_lane = keep(types, "key_lane", [P, CPAD])
                    S.key_bin = keep(types, "key_bin", [P, CPAD])
                    by_src.scratch(nc, types, "s_")
                    with Semaphores(nc) as sem:
                        constants(nc, S, sem, src, dst, edge_type_7)
                        load_nodes(nc, S, sem, x, x_sb)
                        rank_edges(nc, S, by_src, conv_payload(S))
                        group_norm(nc, S, sem, "n0_", x_sb[:, :, :], sums, L0_gnn_gn1_w, L0_gnn_gn1_b)
                        typed_features(nc, S, sem, "f0_", sums, L0_gnn_conv1_w, feature_table, move=(by_src, counts))
                with Semaphores(nc) as sem:
                    type_weights(nc, S, by_src, sem, counts)
                    gather_and_add(nc, S, by_src, sem, "a0_", feature_table, acc, 0)
                by_dst.scratch(nc, lists, "d_")
                with Semaphores(nc) as sem:
                    group_norm(nc, S, sem, "n1_", sums, sums, L0_gnn_gn2_w, L0_gnn_gn2_b)
                    typed_features(nc, S, sem, "f1_", sums, L0_gnn_conv2_w, feature_table, rank=(by_dst, attention_payload(S)))
                    gather_and_add(nc, S, by_src, sem, "a1_", feature_table, acc, 1, other=by_dst)
        with Semaphores(nc) as sem:
            add_residual(nc, x_sb, sums, 2.0)
            layer_norm(nc, S, sem, "m0_", x_sb)
        attention_layer(nc, S, by_dst, "g0_", x_sb, L1_gnn_W1, L1_gnn_att_src1, L1_gnn_att_dst1, L1_gnn_b1, HEADS, acc, sums, True,
                        node_table, spill, 0)
        attention_layer(nc, S, by_dst, "g1_", sums, L1_gnn_W2, L1_gnn_att_src2, L1_gnn_att_dst2, L1_gnn_b2, 1, acc, sums, False,
                        node_table, spill, 1)
        with Semaphores(nc) as sem:
            add_residual(nc, x_sb, sums, 1.0)
            layer_norm(nc, S, sem, "m1_", x_sb)
            store_nodes(nc, S, sem, x_sb, out)


def load_nodes(nc, S, sem, x, x_sb):
    loaded, cleared = sem("x_loaded"), sem("x_cleared")
    with nc.Block() as block:
        @block.vector
        def _(v):
            v.memset(x_sb[:, BLOCKS - 1, :], 0.0).then_inc(cleared, 1)

        @block.sync
        def _(sp):
            sp.dma_start(x_sb[:, 0:BLOCKS - 1, :], x[0:(BLOCKS - 1) * P, :].rearrange("(b p) c -> p b c", p=P)).then_inc(loaded, 16)
            sp.wait_ge(cleared, 1)
            sp.dma_start(x_sb[0:LAST, BLOCKS - 1, :], x[(BLOCKS - 1) * P:, :]).then_inc(loaded, 16)
            sp.wait_ge(loaded, 32)


def store_nodes(nc, S, sem, x_sb, out):
    stored = sem("stored")
    with nc.Block() as block:
        @block.sync
        def _(sp):
            sp.dma_start(out[0:(BLOCKS - 1) * P, :].rearrange("(b p) c -> p b c", p=P), x_sb[:, 0:BLOCKS - 1, :]).then_inc(stored, 16)
            sp.dma_start(out[(BLOCKS - 1) * P:, :], x_sb[0:LAST, BLOCKS - 1, :]).then_inc(stored, 16)
            sp.wait_ge(stored, 32)


def add_residual(nc, x, y, times):
    with nc.Block() as block:
        @block.vector
        def _(v):
            v.scalar_tensor_tensor(x[:, :, :], x[:, :, :], times, y, ALU.mult, ALU.add)


_INS = ["x", "src", "dst", "edge_type_7", "L0_gnn_gn1_w", "L0_gnn_gn1_b", "L0_gnn_conv1_w", "L0_gnn_gn2_w", "L0_gnn_gn2_b",
        "L0_gnn_conv2_w", "L1_gnn_W1", "L1_gnn_att_src1", "L1_gnn_att_dst1", "L1_gnn_b1", "L1_gnn_W2", "L1_gnn_att_src2",
        "L1_gnn_att_dst2", "L1_gnn_b2"]


def kernel(**inputs):
    import numpy as np
    from concourse import bacc
    from concourse.bass_utils import run_bass_kernel_spmd

    nc = bacc.Bacc("TRN2", target_bir_lowering=False, num_devices=1)
    arrays, args = {}, []
    for name in _INS:
        a = np.ascontiguousarray(inputs[name])
        arrays[f"in_{name}"] = a
        args.append(nc.dram_tensor(f"in_{name}", a.shape, mybir.dt.from_np(a.dtype), kind="ExternalInput").ap())
    args.append(nc.dram_tensor("out", (NODES, CH), FP32, kind="ExternalOutput").ap())
    gnn(nc, *args)
    return run_bass_kernel_spmd(nc, [arrays], core_ids=[0]).results[0]["out"]
```

```python
from contextlib import ExitStack

import concourse.bass as bass
from concourse import mybir

FP32 = mybir.dt.float32
BF16 = mybir.dt.bfloat16
FP16 = mybir.dt.float16
INT32 = mybir.dt.int32
ALU = mybir.AluOpType
ACT = mybir.ActivationFunctionType
AX = mybir.AxisListType

P = 128
NODES, CH = 3125, 256
EDGES, TYPES = 50000, 7
GROUPS = 32
HEADS = 8
HC = CH // HEADS
BLOCKS = -(-NODES // P)
LAST = NODES - (BLOCKS - 1) * P
COLS = -(-EDGES // P)
TAIL = EDGES - (P - 1) * COLS
BINS = BLOCKS * TYPES
STEP = 16
CHUNKS = -(-(EDGES // P + BLOCKS) // 16) * 16
CPAD = CHUNKS
LAG = 4
EXTRA = 48
TROWS = BLOCKS * P
TCODE = 4096
ACCW = CH + 3 * HEADS
HROW = CH + HEADS
EPS = 1e-5
SLOPE = 0.2
BIG = 2.0 ** 100
KC = CH // P


class Shared:
    pass


class Semaphores:

    def __init__(self, nc):
        self.nc, self.held = nc, []

    def __enter__(self):
        def sem(name):
            self.held.append(self.nc.alloc_semaphore(name=name))
            return self.held[-1]
        return sem

    def __exit__(self, *problem):
        if problem[0] is None:
            self.nc.clear_and_free_semaphores(self.held)
            self.nc.all_engine_barrier()


class Chain:

    def __init__(self, eng, sem):
        self.eng, self.sem, self.n = eng, sem, 0

    def __call__(self, ins):
        self.n += 1
        ins.then_inc(self.sem, 1)
        self.eng.wait_ge(self.sem, self.n)


def constants(nc, S, sem, src, dst, etype):
    loaded, ramps, padded, own = sem("c_loaded"), sem("c_ramps"), sem("c_padded"), sem("c_own")
    with nc.Block() as block:
        @block.sync
        def _(sp):
            sp.wait_ge(padded, 1)
            for tile, edges in ((S.src_i, src), (S.dst_i, dst), (S.type_i, etype)):
                sp.dma_start(tile[0:P - 1, 0:COLS], edges[0:(P - 1) * COLS].rearrange("(p c) -> p c", c=COLS)).then_inc(loaded, 16)
                sp.dma_start(tile[P - 1:P, 0:TAIL], edges[(P - 1) * COLS:EDGES].rearrange("(a c) -> a c", a=1)).then_inc(loaded, 16)
            sp.wait_ge(loaded, 96)

        @block.gpsimd
        def _(pool):
            pool.iota(S.col_i[:, :], [[1, CHUNKS + EXTRA]], channel_multiplier=0).then_inc(ramps, 1)
            pool.iota(S.row_i[:, :], [[0, 1]], channel_multiplier=1).then_inc(ramps, 1)

        @block.vector
        def _(v):
            step = Chain(v, own)
            for n, tile in enumerate((S.src_i, S.dst_i, S.type_i)):
                ins = v.memset(tile[:, :], 8191)
                if n == 2:
                    ins.then_inc(padded, 1)
            v.wait_ge(ramps, 2)
            v.tensor_copy(S.col_h[:, :], S.col_i[:, 0:CHUNKS])
            step(v.tensor_copy(S.row[:, :], S.row_i[:, :]))
            step(v.tensor_copy(S.col[:, :], S.col_i[:, :]))
            v.tensor_scalar(S.ident[:, :], S.col[:, 0:P], S.row[:, 0:1], None, ALU.is_equal)
            v.tensor_scalar(S.ident_b[:, :], S.col[:, 0:P], S.row[:, 0:1], None, ALU.is_equal)
            v.tensor_scalar(S.above[:, :], S.col[:, 0:P], S.row[:, 0:1], None, ALU.is_gt)
            v.tensor_scalar(S.down[:, :], S.col[:, 0:P], -float(HEADS), S.row[:, 0:1], ALU.add, ALU.is_equal)
            v.tensor_scalar(S.up[:, :], S.col[:, 0:P], float(HEADS), S.row[:, 0:1], ALU.add, ALU.is_equal)
            v.memset(S.ones[:, :], 1.0)
            v.memset(S.zeros[:, :], 0.0)


class Placement:

    def __init__(self, nc, ctx, sem, name, pay_shift, table_dt):
        def sb(n, shape, dt=FP32):
            return ctx.enter_context(nc.sbuf_tensor(name + n, shape, dt))
        self.pay_shift, self.table_dt = pay_shift, table_dt
        self.own, self.counted, self.summed = sem(name + "own"), sem(name + "counted"), sem(name + "summed")
        self.spread, self.scaled, self.moved = sem(name + "spread"), sem(name + "scaled"), sem(name + "moved")
        self.block_of = sb("block_of", [P, CHUNKS + EXTRA])
        self.block_hot = sb("block_hot", [32, CHUNKS], table_dt)
        self.acc_at = sb("acc_at", [1, CHUNKS + EXTRA], INT32)
        self.local = sb("local", [P, CHUNKS + EXTRA])
        self.local_b = sb("local_b", [P, CHUNKS + EXTRA], BF16)
        self.take = sb("take", [P, CHUNKS], INT32)

    def scratch(self, nc, ctx, name):
        def sb(n, shape, dt=FP32):
            return ctx.enter_context(nc.sbuf_tensor(name + n, shape, dt))
        self.ti, self.tj = sb("ti", [P, CPAD], INT32), sb("tj", [P, CPAD], INT32)
        self.blk, self.lo, self.hi = sb("blk", [P, CPAD]), sb("lo", [P, CPAD]), sb("hi", [P, CPAD])
        self.pos = sb("pos", [P, CPAD])
        self.lane, self.chunk = (sb(n, [P, CPAD + LAG]) for n in ("lane", "chunk"))
        self.mask, self.run = [sb(f"mask{n}", [P, CPAD]) for n in range(2)], [sb(f"run{n}", [P, CPAD]) for n in range(2)]
        self.cnt, self.base, self.tot, self.first, self.incl = (sb(n, [P, BLOCKS]) for n in ("cnt", "base", "tot", "first", "incl"))
        self.nch_i = sb("nch_i", [P, BLOCKS], INT32)

    def buffers(self, nc, ctx, name):
        def sb(n, shape, dt=FP32):
            return ctx.enter_context(nc.sbuf_tensor(name + n, shape, dt))
        self.lanes, self.highs, self.lows = (sb(n, [P, STEP, P], FP16) for n in ("lanes", "highs", "lows"))
        self.chunks = sb("chunks", [P, STEP, CHUNKS], FP16)
        self.p_hi, self.p_lo = (ctx.enter_context(nc.psum_tensor(name + n, [P, 512], FP32)) for n in ("p_hi", "p_lo"))

    def ranks(self, v, S, step, payload, p_cnt):
        T = self
        step(v.tensor_scalar(T.ti[:, :], T.key_i[:, :], 7, None, ALU.logical_shift_right))
        step(v.tensor_copy(T.blk[:, :], T.ti[:, :]))
        step(v.tensor_scalar(T.ti[:, :], T.key_i[:, :], P - 1, None, ALU.bitwise_and))
        step(v.tensor_copy(T.lane[:, 0:CPAD], T.ti[:, :]))
        payload(v, step, T.lo)
        if T.pay_shift == 15:
            v.tensor_copy(S.key_lane[:, :], T.lane[:, 0:CPAD])
            v.scalar_tensor_tensor(S.key_bin[:, :], T.blk[:, :], float(TYPES), S.pay[:, :], ALU.mult, ALU.add)
        step(v.scalar_tensor_tensor(T.pos[:, :], T.lane[:, 0:CPAD], float(1 << T.pay_shift), T.lo[:, :], ALU.mult, ALU.add))
        step(v.tensor_copy(T.ti[:, :], T.pos[:, :]))
        step(v.tensor_scalar(T.tj[:, :], T.ti[:, :], 11, None, ALU.logical_shift_right))
        step(v.tensor_scalar(T.ti[:, :], T.ti[:, :], 2047, None, ALU.bitwise_and))
        v.tensor_copy(T.hi[:, :], T.tj[:, :])
        step(v.tensor_copy(T.lo[:, :], T.ti[:, :]))
        spare = T.mask + T.run
        for b in range(BLOCKS):
            if b >= len(spare):
                v.wait_ge(T.counted, b - len(spare) + 1)
            v.tensor_scalar(spare[b % 4][:, :], T.blk[:, :], float(b), 0.0, ALU.is_equal, ALU.add, accum_out=T.cnt[:, b:b + 1]).then_inc(T.counted, 1)
        v.memset(T.pos[:, :], 0.0)
        v.memset(T.block_of[:, :], 0.0)
        v.memset(T.lane[:, CPAD:], -1.0)
        v.memset(T.chunk[:, CPAD:], -1.0)
        v.wait_ge(T.summed, 1)
        step(v.tensor_scalar(T.tot[:, :], p_cnt[:, 0:BLOCKS], float(P - 1), None, ALU.add))
        step(v.tensor_copy(T.nch_i[:, :], T.tot[:, :]))
        step(v.tensor_scalar(T.nch_i[:, :], T.nch_i[:, :], 7, None, ALU.logical_shift_right))
        step(v.tensor_copy(T.tot[:, :], T.nch_i[:, :]))
        step(v.tensor_tensor_scan(T.incl[:, :], T.tot[:, :], T.tot[:, :], 0.0, ALU.add, ALU.max))
        step(v.tensor_tensor(T.first[:, :], T.incl[:, :], T.tot[:, :], ALU.subtract))
        step(v.scalar_tensor_tensor(T.base[:, :], T.first[:, :], float(P), p_cnt[:, BLOCKS:2 * BLOCKS], ALU.mult, ALU.add))
        mark = step.n
        v.tensor_scalar(T.mask[0][:, :], T.blk[:, :], 0.0, None, ALU.is_equal).then_inc(T.own, 1)
        for b in range(BLOCKS):
            m, r = T.mask[b % 2], T.run[b % 2]
            v.wait_ge(T.own, mark + 4 * b + 1)
            v.tensor_tensor_scan(r[:, :], m[:, :], m[:, :], T.base[:, b:b + 1], ALU.add, ALU.max).then_inc(T.own, 1)
            if b > 0:
                v.scalar_tensor_tensor(T.block_of[:, :], S.col[:, :], T.first[:, b:b + 1], T.block_of[:, :], ALU.is_ge, ALU.add)
            v.wait_ge(T.own, mark + 4 * b + 2)
            v.tensor_tensor(r[:, :], r[:, :], m[:, :], ALU.mult).then_inc(T.own, 1)
            n = T.mask[(b + 1) % 2]
            if b + 1 < BLOCKS:
                v.wait_ge(T.own, mark + 4 * b)
            v.tensor_scalar(n[:, :], T.blk[:, :], float(b + 1), None, ALU.is_equal).then_inc(T.own, 1)
            v.wait_ge(T.own, mark + 4 * b + 4)
            v.tensor_tensor(T.pos[:, :], T.pos[:, :], r[:, :], ALU.add).then_inc(T.own, 1)
        step.n = mark + 4 * BLOCKS + 1
        v.wait_ge(T.own, step.n)
        step(v.tensor_scalar(T.pos[:, :], T.pos[:, :], -1.0, None, ALU.add))
        step(v.tensor_copy(T.ti[:, :], T.pos[:, :]))
        step(v.tensor_scalar(T.tj[:, :], T.ti[:, :], P - 1, None, ALU.bitwise_and))
        step(v.tensor_scalar(T.ti[:, :], T.ti[:, :], 7, None, ALU.arith_shift_right))
        v.tensor_copy(T.lane[:, 0:CPAD], T.tj[:, :])
        step(v.tensor_copy(T.chunk[:, 0:CPAD], T.ti[:, :]))

    def totals(self, pe, S, p_cnt):
        pe.wait_ge(self.counted, BLOCKS)
        pe.matmul(p_cnt[:, 0:BLOCKS], S.ones[:, :], self.cnt[:, :], start=True, stop=True)
        pe.matmul(p_cnt[:, BLOCKS:2 * BLOCKS], S.above[:, :], self.cnt[:, :], start=True, stop=True).then_inc(self.summed, 1)

    def spread_column(self, v, S, c, slot):
        e = bass.ds(c, 1)
        v.tensor_scalar(self.lanes[:, slot, :], S.col_h[:, 0:P], self.lane[:, e], None, ALU.is_equal)
        return v.tensor_scalar(self.chunks[:, slot, :], S.col_h[:, :], self.chunk[:, e], None, ALU.is_equal)

    def scale_column(self, act, c, slot):
        e = bass.ds(c, 1)
        act.wait_ge(self.spread, c + 1)
        act.mul(self.highs[:, slot, :], self.lanes[:, slot, :], self.hi[:, e])
        act.mul(self.lows[:, slot, :], self.lanes[:, slot, :], self.lo[:, e]).then_inc(self.scaled, 1)

    def move_column(self, pe, slot):
        pe.matmul(self.p_hi[:, 0:CHUNKS], self.highs[:, slot, :], self.chunks[:, slot, :], start=False, stop=False)
        return pe.matmul(self.p_lo[:, 0:CHUNKS], self.lows[:, slot, :], self.chunks[:, slot, :], start=False, stop=False)

    def open_sums(self, pe, S, start):
        for p in (self.p_hi, self.p_lo):
            ins = pe.matmul(p[:, 0:CHUNKS], S.zeros[:, 0:P], S.zeros[:, :], start=start, stop=not start)
        return ins

    def decode(self, v, S, step, rest):
        T = self
        ci, cj, cf, cg = T.ti[:, 0:CHUNKS], T.tj[:, 0:CHUNKS], T.lo[:, 0:CHUNKS], T.hi[:, 0:CHUNKS]
        step(v.tensor_copy(cf, T.p_lo[:, 0:CHUNKS]))
        step(v.scalar_tensor_tensor(cf, T.p_hi[:, 0:CHUNKS], 2048.0, cf, ALU.mult, ALU.add))
        step(v.tensor_copy(ci, cf))
        step(v.tensor_scalar(cj, ci, T.pay_shift, None, ALU.logical_shift_right))
        step(v.tensor_copy(cg, cj))
        step(v.tensor_scalar(cf, cf, 0.0, None, ALU.is_gt))
        step(v.scalar_tensor_tensor(cg, cg, 1.0, cf, ALU.add, ALU.mult))
        v.memset(T.local[:, CHUNKS:], -1.0)
        v.memset(T.local_b[:, CHUNKS:], -1.0)
        step(v.tensor_scalar(T.local[:, 0:CHUNKS], cg, -1.0, None, ALU.add))
        v.tensor_copy(T.local_b[:, 0:CHUNKS], T.local[:, 0:CHUNKS])
        v.tensor_scalar(T.acc_at[0:1, :], T.block_of[0:1, :], float(ACCW), None, ALU.mult)
        v.tensor_scalar(T.block_hot[0:BLOCKS, :], T.block_of[0:BLOCKS, 0:CHUNKS], S.row[0:BLOCKS, 0:1], None, ALU.is_equal)
        rest(v, step, ci, cj, cf)


def conv_payload(S):
    def payload(v, step, out):
        step(v.tensor_copy(S.pay[:, :], S.type_i[:, :]))
        step(v.tensor_copy(out[:, :], S.dst_i[:, :]))
        step(v.tensor_scalar(out[:, :], out[:, :], 1.0, None, ALU.add))
        step(v.scalar_tensor_tensor(out[:, :], S.pay[:, :], float(TCODE), out[:, :], ALU.mult, ALU.add))
    return payload


def conv_decode(S, E):
    def rest(v, step, code, ti, tf):
        step(v.tensor_scalar(ti, code, 12, 7, ALU.logical_shift_right, ALU.bitwise_and))
        step(v.tensor_copy(S.etype[:, :], ti))
        step(v.tensor_scalar(code, code, (1 << 15) - 1, None, ALU.bitwise_and))
        step(v.tensor_copy(tf, code))
        step(v.scalar_tensor_tensor(tf, S.etype[:, :], float(TROWS - TCODE), tf, ALU.mult, ALU.add))
        v.tensor_scalar(E.take[:, :], tf, -1.0, 0.0, ALU.add, ALU.max)
    return rest


def attention_payload(S):
    def payload(v, step, out):
        step(v.tensor_copy(out[:, :], S.src_i[:, :]))
        step(v.tensor_scalar(out[:, :], out[:, :], 1.0, None, ALU.add))
    return payload


def attention_decode(S, E):
    def rest(v, step, code, ti, tf):
        step(v.tensor_scalar(ti, code, 4095, None, ALU.bitwise_and))
        step(v.tensor_copy(tf, ti))
        v.tensor_scalar(E.take[:, :], tf, -1.0, 0.0, ALU.add, ALU.max)
    return rest


def rank_edges(nc, S, E, payload):
    with nc.psum_tensor("p_cnt", [P, 512], FP32) as p_cnt:
        with nc.Block() as block:
            @block.vector
            def _(v):
                step = Chain(v, E.own)
                E.ranks(v, S, step, payload, p_cnt)
                E.steps = step.n

            @block.tensor
            def _(pe):
                E.totals(pe, S, p_cnt)


GRP = 8
PAIR = 2 * GRP
RING = 4 * GRP


def hot_and_add(nc, S, E, v, own, hot, weight, accs, width, banks, hot_ready, added, done, beside=None):
    regs = [v.alloc_register(f"{own}_at{u}") for u in range(PAIR)]

    def onehot(c, slot):
        v.tensor_scalar(hot[:, slot, :], S.col[:, 0:P], E.local[:, bass.ds(c, 1)], weight[:, bass.ds(c, 1)],
                        ALU.is_equal, ALU.mult).then_inc(hot_ready, 1)
    v.sem_inc(added, len(banks))
    if hot:
        for u in range(GRP):
            onehot(u, u)
    with v.Fori(0, CHUNKS // PAIR) as i:
        for h in range(2):
            first = i * PAIR + GRP * h
            if hot:
                v.wait_ge(done, first + RING)
            if h == 0:
                v.load(regs, E.acc_at[0:1, bass.ds(i * PAIR, PAIR)])
                at = [v.snap(r, min_val=0, max_val=(BLOCKS - 1) * ACCW) for r in regs]
            for u in range(GRP):
                if hot:
                    onehot(first + (GRP + u), GRP * (1 - h) + u)
                if beside:
                    beside(i, GRP * h + u)
                v.wait_ge(done, first + (RING + u + 1))
                v.wait_ge(added, first + (len(banks) + u + 1 - len(accs)))
                part = accs[u % len(accs)][:, bass.ds(at[GRP * h + u], width)]
                v.tensor_tensor(part, part, banks[u % len(banks)][:, 0:width], ALU.add).then_inc(added, 1)


G4 = 4
HALF = 16


class LookUp:

    def __init__(self, nc, ctx, sem, name, E, table, width, deep):
        def sb(n, shape, dt=FP32):
            return ctx.enter_context(nc.sbuf_tensor(name + n, shape, dt))

        def pb(n):
            return ctx.enter_context(nc.psum_tensor(name + n, [P, 512], FP32))
        self.E, self.table, self.width, self.deep = E, table, width, deep
        self.turned, self.turned_out, self.spread, self.spread_out, self.tail = (
            sem(name + n) for n in ("turned", "turned_out", "spread", "spread_out", "tail"))
        self.staged, self.rows, self.hot_ready, self.found, self.stored = (
            sem(name + n) for n in ("staged", "rows", "hot_ready", "found", "stored"))
        self.tt = sb("tt", [32, width, P], E.table_dt)
        self.per_chunk = sb("per_chunk", [P, CHUNKS + EXTRA, width], E.table_dt)
        self.now_local = [sb(f"now_local{h}", [P, HALF], BF16) for h in range(2)]
        self.now_rows = [sb(f"now_rows{h}", [P, HALF, width], E.table_dt) for h in range(2)]
        self.hot = [sb(f"hot{n}", [P, G4 * P], E.table_dt) for n in range(deep)]
        self.p_row = [pb(f"row{n}") for n in range(deep)]
        self.p_out = [pb(f"out{n}") for n in range(2)]

    def spread_table(self, pe, S):
        for w in range(self.width + 1):
            if w < self.width:
                if w >= 2:
                    pe.wait_ge(self.turned_out, w - 1)
                pe.transpose(self.p_out[w % 2][0:BLOCKS, 0:P], self.table[:, :, w], S.ident[:, :]).then_inc(self.turned, 1)
            if w == 0:
                continue
            w -= 1
            pe.wait_ge(self.turned_out, w + 1)
            if w >= self.deep:
                pe.wait_ge(self.spread_out, w - self.deep + 1)
            pe.matmul(self.p_row[w % self.deep][:, 0:CHUNKS], self.tt[0:BLOCKS, w, :], self.E.block_hot[0:BLOCKS, :],
                      start=True, stop=True).then_inc(self.spread, 1)
        pe.sem_inc(self.found, self.deep)
        pe.wait_ge(self.spread_out, self.width)

    def keep_table(self, act):
        for w in range(self.width):
            act.wait_ge(self.spread, w + 1)
            act.copy(self.per_chunk[:, 0:CHUNKS, w], self.p_row[w % self.deep][:, 0:CHUNKS]).then_inc(self.spread_out, 1)
        act.sem_inc(self.stored, 2)
        act.wait_ge(self.tail, 1)
        act.wait_ge(self.spread_out, self.width)
        for h in range(2):
            self.stage(act, HALF * h, h)

    def turn_table(self, v):
        for w in range(self.width):
            v.wait_ge(self.turned, w + 1)
            v.tensor_copy(self.tt[0:BLOCKS, w, :], self.p_out[w % 2][0:BLOCKS, 0:P]).then_inc(self.turned_out, 1)
        v.memset(self.per_chunk[:, CHUNKS:, :], 0.0).then_inc(self.tail, 1)

    def stage(self, act, c, h):
        at = bass.ds(c, HALF)
        act.copy(self.now_local[h][:, :], self.E.local_b[:, at])
        act.copy(self.now_rows[h][:, :, :], self.per_chunk[:, at, :]).then_inc(self.staged, 1)

    def rows_of(self, pe, S, g):
        for j in range(G4):
            c = g % 4 * G4 + j
            ins = pe.matmul(self.p_row[g % self.deep][:, j * P:(j + 1) * P], self.now_local[g // 4 % 2][:, c:c + 1].to_broadcast([P, P]),
                            S.ident_b[:, :], start=True, stop=True)
        ins.then_inc(self.rows, 1)

    def compare(self, v, S, g):
        return v.tensor_scalar(self.hot[g % self.deep][:, :], self.p_row[g % self.deep][:, :], S.row[:, 0:1], None,
                               ALU.is_equal).then_inc(self.hot_ready, 1)

    def find(self, pe, g):
        h, w = g // 4 % 2, self.width
        for j in range(G4):
            c = g % 4 * G4 + j
            ins = pe.matmul(self.p_out[h][:, c * w:(c + 1) * w], self.hot[g % self.deep][:, j * P:(j + 1) * P],
                            self.now_rows[h][:, c, :], start=True, stop=True)
        ins.then_inc(self.found, 1)

    def store(self, act, result, c, h):
        act.copy(result[:, bass.ds(c, HALF), :], self.p_out[h][:, 0:HALF * self.width].rearrange("p (c w) -> p c w", w=self.width)).then_inc(self.stored, 1)


def look_up_and_gather(nc, S, E, sem, name, table, width, result, node_table, edge, spill, round_of_gathers):
    DEEP = 4
    index_ready, scores, passed = sem(name + "index"), sem(name + "scores"), sem(name + "passed")
    arrived, before = S.arrived, (2 * (CHUNKS // RING) + round_of_gathers * (CHUNKS // PAIR)) * 16
    spilled = [sem(f"{name}spilled{h}") for h in range(2)]
    with ExitStack() as ctx:
        L = LookUp(nc, ctx, sem, name, E, table, width, DEEP)
        taken = ctx.enter_context(nc.sbuf_tensor(name + "taken", [P, PAIR, HROW], FP32))
        index = ctx.enter_context(nc.sbuf_tensor(name + "indices", [P, RING], INT32))
        with nc.Block() as block:
            @block.tensor
            def _(pe):
                L.spread_table(pe, S)
                pe.wait_ge(L.staged, 1)
                L.rows_of(pe, S, 0)
                L.rows_of(pe, S, 1)
                with pe.Fori(0, CHUNKS // 32) as i:
                    for h in range(2):
                        pe.wait_ge(L.stored, i * 2 + (h + 1))
                        for q in range(4):
                            g = 4 * h + q
                            if q == 2:
                                pe.wait_ge(L.staged, i * 2 + (h + 2))
                            L.rows_of(pe, S, g + 2)
                            pe.wait_ge(L.hot_ready, i * 8 + (g + 1))
                            L.find(pe, g)

            @block.vector
            def _(v):
                L.turn_table(v)
                with v.Fori(0, CHUNKS // 32) as i:
                    for g in range(8):
                        v.wait_ge(L.rows, i * 8 + (g + 1))
                        v.wait_ge(L.found, i * 8 + (g + 1))
                        L.compare(v, S, g)

            @block.scalar
            def _(act):
                act.sem_inc(scores, 2)
                L.keep_table(act)
                with act.Fori(0, CHUNKS // 32) as i:
                    for h in range(2):
                        for q in range(2):
                            for u in range(GRP):
                                act.wait_ge(arrived[q * GRP + u], i * 32 + (before + 16 * h + 16))
                            act.copy(edge[:, bass.ds(i * 32 + (HALF * h + GRP * q), GRP), 0:HEADS],
                                     taken[:, q * GRP:(q + 1) * GRP, CH:]).then_inc(scores, 1)
                        act.wait_ge(L.found, i * 8 + (4 * h + 4 + DEEP))
                        L.store(act, result, i * 32 + HALF * h, h)
                        L.stage(act, i * 32 + (HALF * h + 32), h)

            @block.gpsimd
            def _(pool):
                with pool.Fori(0, CHUNKS // RING) as i:
                    for u in range(RING):
                        if u % GRP == 0:
                            pool.wait_ge(spilled[u // GRP % 2], i * 32 + (16 + u // PAIR * 16))
                            pool.wait_ge(scores, i * 4 + (u // GRP + 1))
                            pool.sem_inc(passed, 1)
                        if u % PAIR == 0:
                            pool.tensor_copy(index[:, u:u + PAIR], E.take[:, bass.ds(i * RING + u, PAIR)]).then_inc(index_ready, 1)
                            pool.wait_ge(index_ready, i * 2 + (u // PAIR + 1))
                            pool.sem_inc(passed, 1)
                        pool.indirect_dma_start(taken[:, u % PAIR, :], None, node_table,
                                                bass.IndirectOffsetOnAxis(ap=index[:, u:u + 1], axis=0)).then_inc(arrived[u % PAIR], 16)

            @block.sync
            def _(sp):
                for h in range(2):
                    sp.sem_inc(spilled[h], 16)
                with sp.Fori(0, CHUNKS // PAIR) as i:
                    for h in range(2):
                        for u in range(GRP):
                            sp.wait_ge(arrived[h * GRP + u], i * 16 + (before + 16))
                        sp.dma_start(spill[:, bass.ds(i * PAIR + h * GRP, GRP), :], taken[:, h * GRP:(h + 1) * GRP, 0:CH]).then_inc(spilled[h], 16)
                for h in range(2):
                    sp.wait_ge(spilled[h], 16 * (CHUNKS // PAIR + 1))


class TypeWeights:
    DEEP = 2
    STEPS = 5

    def __init__(self, nc, ctx, sem, name, E, counts):
        def sb(n, shape, dt=FP32):
            return ctx.enter_context(nc.sbuf_tensor(name + n, shape, dt))
        self.counts, self.own, self.cut, self.passed = counts, sem(name + "own"), sem(name + "cut"), sem(name + "passed")
        self.type_hot = sb("types", [P, CHUNKS + HALF, TYPES], BF16)
        self.each = sb("each", [P, CHUNKS + EXTRA, 2 * TYPES])
        self.digits = sb("digits", [P, BLOCKS, 2 * TYPES])
        self.whole, self.digit = (sb(n, [P, BLOCKS, TYPES], INT32) for n in ("whole", "digit"))
        self.look = LookUp(nc, ctx, sem, name, E, self.digits, 2 * TYPES, self.DEEP)

    def begin_vector(self, v, S):
        cut = Chain(v, self.cut)
        cut(v.tensor_copy(self.whole[:, :, :], self.counts[:, :, :]))
        cut(v.tensor_scalar(self.digit[:, :, :], self.whole[:, :, :], 8, None, ALU.logical_shift_right))
        cut(v.tensor_copy(self.digits[:, :, 0:TYPES], self.digit[:, :, :]))
        cut(v.tensor_scalar(self.digit[:, :, :], self.whole[:, :, :], 255, None, ALU.bitwise_and))
        cut(v.tensor_copy(self.digits[:, :, TYPES:], self.digit[:, :, :]))
        self.look.turn_table(v)
        v.memset(self.type_hot[:, CHUNKS:, :], 0.0)
        for t in range(TYPES):
            ins = v.tensor_scalar(self.type_hot[:, 0:CHUNKS, t], S.etype[:, :], float(t), None, ALU.is_equal)
        cut(ins)
        for g in range(8):
            self.compare(v, S, g, g)
        self.weigh(v, S, 0)

    def compare(self, v, S, before, g):
        v.wait_ge(self.look.rows, before + 1)
        v.wait_ge(self.look.found, before + 1)
        self.look.compare(v, S, g)

    def weigh(self, v, S, half):
        at = bass.ds(half * HALF, HALF)
        count, weight = self.each[:, at, TYPES:], S.weight[:, at]
        v.wait_ge(self.look.stored, half + 3)
        for n, ins in enumerate((
                lambda: v.scalar_tensor_tensor(count, self.each[:, at, 0:TYPES], 256.0, count, ALU.mult, ALU.add),
                lambda: v.tensor_tensor(count, count, self.type_hot[:, at, :], ALU.mult),
                lambda: v.tensor_reduce(weight, count, AX.X, ALU.add),
                lambda: v.tensor_scalar(weight, weight, 1.0, None, ALU.max),
                lambda: v.reciprocal(weight, weight))):
            ins().then_inc(self.own, 1)
            v.wait_ge(self.own, half * self.STEPS + (n + 1))
            if n == 3:
                v.sem_inc(self.passed, 1)

    def begin_tensor(self, pe, S):
        pe.wait_ge(self.cut, 5)
        self.look.spread_table(pe, S)
        self.tensor(pe, S, 0, 0, 0, True)
        for g in range(8):
            if g + 1 < 8:
                self.tensor(pe, S, g + 1, (g + 1) // 4, g + 1, True)
            self.tensor(pe, S, g, g // 4, g, False)

    def tensor(self, pe, S, before, half, g, first):
        L = self.look
        if first:
            if g % 4 == 0:
                pe.wait_ge(L.staged, half + 1)
            L.rows_of(pe, S, g)
        else:
            if g % 4 == 0:
                pe.wait_ge(L.stored, half + 1)
            pe.wait_ge(L.hot_ready, before + 1)
            L.find(pe, g)

    def scalar(self, act, meanwhile):
        L = self.look
        L.keep_table(act)
        meanwhile()
        for half in range(2):
            act.wait_ge(L.found, 4 * half + 4 + self.DEEP)
            L.store(act, self.each, HALF * half, half)
            if half == 0:
                L.stage(act, 2 * HALF, 0)
        with act.Fori(0, CHUNKS // RING) as i:
            for h in range(2):
                L.stage(act, i * RING + HALF * (h + 3), 1 - h)
                act.wait_ge(L.found, i * 8 + (4 * h + 12 + self.DEEP))
                L.store(act, self.each, i * RING + HALF * (h + 2), h)


def clear_accumulator(act, S, acc, cleared):
    act.copy(blocks_of(acc), S.zeros[:, 0:ACCW].unsqueeze(1).to_broadcast([P, BLOCKS, ACCW])).then_inc(cleared, 1)


def gather_and_add(nc, S, E, sem, name, table, acc, round_of_gathers, counts=None, other=None):
    hot_ready, added, done, cleared = sem(name + "hot"), sem(name + "added"), sem(name + "done"), sem(name + "cleared")
    index_ready, passed = sem(name + "index"), sem(name + "passed")
    arrived, before = S.arrived, round_of_gathers * (CHUNKS // RING) * 16
    with ExitStack() as ctx:
        hot = ctx.enter_context(nc.sbuf_tensor(name + "hots", [P, PAIR, P], FP32))
        rows = ctx.enter_context(nc.sbuf_tensor(name + "rows", [P, RING, CH], FP32))
        index = ctx.enter_context(nc.sbuf_tensor(name + "indices", [P, RING], INT32))
        if other:
            other.buffers(nc, ctx, name)
        if counts:
            T = TypeWeights(nc, ctx, sem, name + "t_", E, counts)
        banks = [ctx.enter_context(nc.psum_tensor(f"{name}bank{u}", [P, 512], FP32)) for u in range(GRP // 2)]
        with nc.Block() as block:
            @block.gpsimd
            def _(pool):
                with pool.Fori(0, CHUNKS // RING) as i:
                    for u in range(RING):
                        if u % PAIR == 0:
                            pool.wait_ge(done, i * RING + (u + PAIR))
                            pool.sem_inc(passed, 1)
                            pool.tensor_copy(index[:, u:u + PAIR], E.take[:, bass.ds(i * RING + u, PAIR)]).then_inc(index_ready, 1)
                            pool.wait_ge(index_ready, i * 2 + (u // PAIR + 1))
                            pool.sem_inc(passed, 1)
                        pool.indirect_dma_start(rows[:, u, :], None, table,
                                                bass.IndirectOffsetOnAxis(ap=index[:, u:u + 1], axis=0)).then_inc(arrived[u], 16)

            @block.vector
            def _(v):
                def column(i, u):
                    v.wait_ge(other.moved, i * PAIR + (u + LAG + 1))
                    other.spread_column(v, S, i * PAIR + (u + LAG), (u + LAG) % STEP).then_inc(other.spread, 1)

                def weights(i, u):
                    if u == 0:
                        T.weigh(v, S, i + 1)
                    if u % G4 == 1:
                        T.compare(v, S, i * 4 + (8 + u // G4), u // G4)
                if counts:
                    T.begin_vector(v, S)
                v.wait_ge(cleared, 1)
                if other:
                    for u in range(LAG):
                        other.spread_column(v, S, u, u).then_inc(other.spread, 1)
                hot_and_add(nc, S, E, v, name, hot, S.weight, [acc], CH, banks, hot_ready, added, done, column if other else weights)
                if other:
                    v.wait_ge(other.moved, CPAD + STEP + 1)
                    step = Chain(v, other.own)
                    step.n = other.steps
                    other.decode(v, S, step, attention_decode(S, other))

            @block.scalar
            def _(act):
                def clear():
                    clear_accumulator(act, S, acc, cleared)
                if counts:
                    T.scalar(act, clear)
                else:
                    clear()
                if other:
                    with act.Fori(0, CPAD // STEP) as i:
                        for u in range(STEP):
                            other.scale_column(act, i * STEP + u, u)

            @block.tensor
            def _(pe):
                pe.sem_inc(done, RING)
                if counts:
                    T.begin_tensor(pe, S)
                if other:
                    pe.sem_inc(other.moved, STEP)
                    other.open_sums(pe, S, True)
                with pe.Fori(0, CHUNKS // RING) as i:
                    for u in range(RING):
                        g = u // G4
                        if counts and u % G4 == 0:
                            T.tensor(pe, S, None, i * 2 + (u // HALF + 2), g, True)
                        pe.wait_ge(hot_ready, i * RING + (u + 1))
                        pe.wait_ge(added, i * RING + (u + 1))
                        pe.wait_ge(arrived[u], i * 16 + (before + 16))
                        pe.matmul(banks[u % len(banks)][:, 0:CH], hot[:, u % PAIR, :], rows[:, u, :], start=True, stop=True).then_inc(done, 1)
                        if counts and u % G4 == G4 - 1:
                            T.tensor(pe, S, i * 8 + (g + 8), i * 2 + (u // HALF + 2), g, False)
                        if other:
                            pe.wait_ge(other.scaled, i * RING + (u + 1))
                            other.move_column(pe, u % STEP).then_inc(other.moved, 1)
                if other:
                    other.open_sums(pe, S, False).then_inc(other.moved, 1)


def blocks_of(tile):
    return tile[:, :].rearrange("p (b w) -> p b w", b=BLOCKS)


def over_blocks(row):
    return row.unsqueeze(1).to_broadcast([P, BLOCKS, row.shape[1]])


def group_norm(nc, S, sem, name, feat, norm, gn_w, gn_b, feat_loaded=None):
    loaded, own, summed, centered, squared, rooted = (sem(name + n) for n in ("loaded", "own", "summed", "centered", "squared", "rooted"))
    with ExitStack() as ctx:
        sq = ctx.enter_context(nc.sbuf_tensor(name + "sq", [P, BLOCKS, CH], FP32))
        grp = ctx.enter_context(nc.sbuf_tensor(name + "grp", [P, GROUPS], FP32))
        eps = ctx.enter_context(nc.sbuf_tensor(name + "eps", [P, 1], FP32))
        scale = ctx.enter_context(nc.sbuf_tensor(name + "scale", [P, CH], FP32))
        bias = ctx.enter_context(nc.sbuf_tensor(name + "bias", [P, CH], FP32))
        sums = [ctx.enter_context(nc.psum_tensor(f"{name}sums{n}", [P, CH], FP32)) for n in range(2)]
        inv_count = 1.0 / (NODES * (CH // GROUPS) + EPS)
        with nc.Block() as block:
            @block.sync
            def _(sp):
                sp.dma_start(scale[:, :], gn_w[0, :].partition_broadcast(P)).then_inc(loaded, 16)
                sp.dma_start(bias[:, :], gn_b[0, :].partition_broadcast(P)).then_inc(loaded, 16)
                sp.wait_ge(loaded, 32)

            @block.tensor
            def _(pe):
                def column_sums(out, x):
                    pe.matmul(out, S.ones[:, :], x[:, 0, :], start=True, stop=False)
                    with pe.Fori(1, BLOCKS - 1) as b:
                        pe.matmul(out, S.ones[:, :], x[:, bass.ds(b, 1), :].rearrange("p a c -> p (a c)"), start=False, stop=False)
                    pe.matmul(out, S.ones[0:LAST, :], x[0:LAST, BLOCKS - 1, :], start=False, stop=True).then_inc(summed, 1)
                if feat_loaded:
                    pe.wait_ge(feat_loaded, 32)
                column_sums(sums[0][:, :], feat)
                pe.wait_ge(squared, 1)
                column_sums(sums[1][:, :], sq)

            @block.scalar
            def _(act):
                act.wait_ge(centered, 1)
                act.activation(sq[:, :, :], norm[:, :, :], ACT.Square).then_inc(squared, 1)
                act.wait_ge(centered, 2)
                act.activation(grp[:, :], grp[:, :], ACT.Sqrt, bias=eps[:, 0:1]).then_inc(rooted, 1)

            @block.vector
            def _(v):
                step = Chain(v, own)
                v.memset(eps[:, :], EPS)
                for n in range(2):
                    v.wait_ge(summed, n + 1)
                    step(v.tensor_reduce(grp[:, :], sums[n][:, :].rearrange("p (g c) -> p g c", g=GROUPS), AX.X, ALU.add))
                    if n == 0:
                        step(v.tensor_scalar(grp[:, :], grp[:, :], inv_count, None, ALU.mult))
                        mean = grp[:, :].unsqueeze(1).unsqueeze(3).to_broadcast([P, BLOCKS, GROUPS, CH // GROUPS])
                        v.tensor_tensor(norm[:, :, :].rearrange("p b (g c) -> p b g c", g=GROUPS),
                                        feat.rearrange("p b (g c) -> p b g c", g=GROUPS), mean, ALU.subtract).then_inc(centered, 1)
                        v.wait_ge(centered, 1)
                    else:
                        v.tensor_scalar(grp[:, :], grp[:, :], inv_count, None, ALU.mult).then_inc(centered, 1)
                v.wait_ge(rooted, 1)
                step(v.reciprocal(grp[:, :], grp[:, :]))
                v.wait_ge(loaded, 32)
                sc = scale[:, :].rearrange("p (g c) -> p g c", g=GROUPS)
                step(v.tensor_tensor(sc, sc, grp[:, :].unsqueeze(2).to_broadcast([P, GROUPS, CH // GROUPS]), ALU.mult))
                step(v.tensor_tensor(norm[:, :, :], norm[:, :, :], over_blocks(scale[:, :]), ALU.mult))
                v.tensor_tensor(norm[:, :, :], norm[:, :, :], over_blocks(bias[:, :]), ALU.add)


def typed_features(nc, S, sem, name, norm, conv_w, table, move=None, rank=None):
    U = 5
    QUARTS = [(0, 512), (512, 512), (1024, 512), (1536, 256)]
    NQ = len(QUARTS)
    PART = STEP // NQ
    W = TYPES * CH
    loaded, acted, turned, turned_out, made, out = (sem(name + n) for n in ("loaded", "acted", "turned", "turned_out", "made", "out"))
    stored = [sem(f"{name}stored{n}") for n in range(U)]
    with ExitStack() as ctx:
        def sb(n, shape, dt=FP32):
            return ctx.enter_context(nc.sbuf_tensor(name + n, shape, dt))

        def pb(n):
            return ctx.enter_context(nc.psum_tensor(name + n, [P, 512], FP32))
        w_sb = sb("w", [P, KC, TYPES, CH])
        h = [sb(f"h{u}", [P, CH]) for u in range(U)]
        ht = [sb(f"ht{u}", [P, KC * P]) for u in range(U)]
        y = [sb(f"y{n}", [P, W]) for n in range(U)]
        p_t = pb("p_t")
        p_y = [pb(f"py{n}") for n in range(NQ)]
        if move:
            E, counts = move
            E.buffers(nc, ctx, name)
            nodes, bins = sb("nodes", [P, STEP, P], FP16), sb("bins", [P, STEP, BINS + 1], FP16)
            p_bins = pb("bins_p")
        if rank:
            R, payload = rank
            p_cnt = pb("p_cnt")
        out_rows = table.rearrange("(t n) c -> n t c", t=TYPES)
        with nc.Block() as block:
            @block.sync
            def _(sp):
                for k in range(KC):
                    sp.dma_start(w_sb[:, k, :, :], conv_w.rearrange("(t k p) n -> k p t n", t=TYPES, k=KC)[k]).then_inc(loaded, 16)
                for u in range(U):
                    sp.sem_inc(stored[u], 16)
                with sp.Fori(0, BLOCKS // U) as i:
                    for u in range(U):
                        sp.wait_ge(out, (i * U + (u + 2)) * NQ)
                        sp.dma_start(out_rows[bass.ds((i * U + u) * P, P), :, :], y[u][:, :].rearrange("p (t c) -> p t c", t=TYPES)).then_inc(stored[u], 16)
                for u in range(U):
                    sp.wait_ge(stored[u], 16 * (BLOCKS // U + 1))

            @block.scalar
            def _(act):
                def silu(b, u):
                    act.activation(h[u][:, :], norm[:, bass.ds(b, 1), :].rearrange("p a c -> p (a c)"), ACT.Silu).then_inc(acted, 1)

                def turn_out(b, u):
                    act.wait_ge(turned, b + 1)
                    act.copy(ht[u][:, :], p_t[:, 0:KC * P]).then_inc(turned_out, 1)

                def copy_out(i, u):
                    act.wait_ge(stored[u], i * 16 + 16)
                    for q, (a, n) in enumerate(QUARTS):
                        if move:
                            for s in range(q * PART, (q + 1) * PART):
                                E.scale_column(act, (i * U + u) * STEP + s, s)
                        act.wait_ge(made, (i * U + u) * NQ + (q + 1))
                        act.copy(y[u][:, a:a + n], p_y[q][:, 0:n]).then_inc(out, 1)
                act.sem_inc(out, NQ)
                for u in range(U):
                    silu(u, u)
                turn_out(0, 0)
                with act.Fori(0, BLOCKS // U - 1) as i:
                    for u in range(U):
                        turn_out(i * U + (u + 1), (u + 1) % U)
                        copy_out(i, u)
                        silu(i * U + (u + U), u)
                for u in range(U):
                    if u + 1 < U:
                        turn_out(BLOCKS - U + u + 1, u + 1)
                    copy_out(BLOCKS // U - 1, u)

            @block.tensor
            def _(pe):
                pe.wait_ge(loaded, 16 * KC)

                def turn(b, u):
                    pe.wait_ge(acted, b + 1)
                    for k in range(KC):
                        ins = pe.transpose(p_t[:, k * P:(k + 1) * P], h[u][:, k * P:(k + 1) * P], S.ident[:, :])
                    ins.then_inc(turned, 1)

                def multiply(b, u, more):
                    pe.wait_ge(turned_out, b + 1)
                    if more:
                        turn(b + 1, (u + 1) % U)
                    for q, (a, n) in enumerate(QUARTS):
                        pe.wait_ge(out, b * NQ + (q + 1))
                        for k in range(KC):
                            ins = pe.matmul(p_y[q][:, 0:n], ht[u][:, k * P:(k + 1) * P],
                                            w_sb[:, k, :, :].rearrange("p t n -> p (t n)")[:, a:a + n], start=(k == 0), stop=(k == KC - 1))
                        ins.then_inc(made, 1)
                        if move:
                            columns(b, q)

                def columns(b, q):
                    for s in range(q * PART, (q + 1) * PART):
                        pe.wait_ge(E.scaled, b * STEP + (s + 1))
                        pe.matmul(p_bins[:, 0:BINS], nodes[:, s, :], bins[:, s, 0:BINS], start=False, stop=False)
                        E.move_column(pe, s).then_inc(E.moved, 1)
                if move:
                    pe.sem_inc(E.moved, STEP)
                    pe.matmul(p_bins[:, 0:BINS], S.zeros[:, 0:P], S.zeros[:, 0:BINS], start=True, stop=False)
                    E.open_sums(pe, S, True)
                turn(0, 0)
                if rank:
                    for u in range(U):
                        multiply(u, u, True)
                    R.totals(pe, S, p_cnt)
                with pe.Fori(1 if rank else 0, BLOCKS // U - 1) as i:
                    for u in range(U):
                        multiply(i * U + u, u, True)
                for u in range(U):
                    multiply(BLOCKS - U + u, u, u + 1 < U)
                if move:
                    pe.matmul(p_bins[:, 0:BINS], S.zeros[:, 0:P], S.zeros[:, 0:BINS], start=False, stop=True)
                    E.open_sums(pe, S, False).then_inc(E.moved, 1)

            @block.vector
            def _(v):
                if move:
                    with v.Fori(0, BLOCKS) as i:
                        for s in range(STEP):
                            c = i * STEP + s
                            v.wait_ge(E.moved, c + 1)
                            v.tensor_scalar(nodes[:, s, :], S.col_h[:, 0:P], S.key_lane[:, bass.ds(c, 1)], None, ALU.is_equal)
                            v.tensor_scalar(bins[:, s, :], S.col_h[:, 0:BINS + 1], S.key_bin[:, bass.ds(c, 1)], None, ALU.is_equal)
                            E.spread_column(v, S, c, s).then_inc(E.spread, 1)
                    v.wait_ge(E.moved, BLOCKS * STEP + STEP + 1)
                    step = Chain(v, E.own)
                    step.n = E.steps
                    v.tensor_copy(counts[:, :, :], p_bins[:, 0:BINS].rearrange("p (b t) -> p b t", t=TYPES))
                    E.decode(v, S, step, conv_decode(S, E))
                if rank:
                    step = Chain(v, R.own)
                    R.ranks(v, S, step, payload, p_cnt)
                    R.steps = step.n


def add_and_norm(nc, S, sem, name, x, y, times, out=None):
    U = 5
    own, set_up, centered, squared, rooted, normed, stored = (sem(name + n) for n in ("own", "set_up", "centered", "squared", "rooted", "normed", "stored"))
    with ExitStack() as ctx:
        sq = ctx.enter_context(nc.sbuf_tensor(name + "sq", [P, BLOCKS, CH], FP32))
        mean, var = (ctx.enter_context(nc.sbuf_tensor(name + n, [P, BLOCKS], FP32)) for n in ("mean", "var"))
        eps = ctx.enter_context(nc.sbuf_tensor(name + "eps", [P, 1], FP32))

        def one(tile, b):
            return tile[:, bass.ds(b, 1), :].rearrange("p a c -> p (a c)")
        with nc.Block() as block:
            @block.vector
            def _(v):
                v.memset(eps[:, :], EPS).then_inc(set_up, 1)
                with v.Fori(0, BLOCKS // U) as i:
                    part = bass.ds(i * U, U)
                    v.scalar_tensor_tensor(x[:, part, :], x[:, part, :], times, y[:, part, :], ALU.mult, ALU.add).then_inc(own, 1)
                    v.wait_ge(own, i * 2 + 1)
                    v.tensor_reduce(mean[:, part], x[:, part, :], AX.X, ALU.add).then_inc(own, 1)
                    v.wait_ge(own, i * 2 + 2)
                    v.tensor_scalar(mean[:, part], mean[:, part], -1.0 / CH, None, ALU.mult).then_inc(centered, 1)
                v.wait_ge(rooted, 1)
                v.reciprocal(var[:, :], var[:, :]).then_inc(own, 1)
                v.wait_ge(own, 2 * BLOCKS // U + 1)
                with v.Fori(0, BLOCKS // U) as i:
                    for u in range(U):
                        b = i * U + u
                        ins = v.tensor_scalar(one(x, b), one(x, b), mean[:, bass.ds(b, 1)], var[:, bass.ds(b, 1)], ALU.add, ALU.mult)
                    ins.then_inc(normed, 1)

            @block.scalar
            def _(act):
                act.wait_ge(set_up, 1)
                with act.Fori(0, BLOCKS // U) as i:
                    act.wait_ge(centered, i + 1)
                    for u in range(U):
                        b = i * U + u
                        ins = act.activation(one(sq, b), one(x, b), ACT.Square, bias=mean[:, bass.ds(b, 1)], accum_out=var[:, bass.ds(b, 1)])
                    ins.then_inc(squared, 1)
                act.wait_ge(squared, BLOCKS // U)
                act.activation(var[:, :], var[:, :], ACT.Sqrt, bias=eps[:, 0:1], scale=1.0 / CH).then_inc(rooted, 1)

            if out is not None:
                @block.sync
                def _(sp):
                    rows = out[0:(BLOCKS - 1) * P, :].rearrange("(b p) c -> p b c", p=P)
                    with sp.Fori(0, BLOCKS // U - 1) as i:
                        sp.wait_ge(normed, i + 1)
                        part = bass.ds(i * U, U)
                        sp.dma_start(rows[:, part, :], x[:, part, :]).then_inc(stored, 16)
                    sp.wait_ge(normed, BLOCKS // U)
                    sp.dma_start(rows[:, BLOCKS - U:, :], x[:, BLOCKS - U:BLOCKS - 1, :]).then_inc(stored, 16)
                    sp.dma_start(out[(BLOCKS - 1) * P:, :], x[0:LAST, BLOCKS - 1, :]).then_inc(stored, 16)
                    sp.wait_ge(stored, 16 * (BLOCKS // U + 1))


def attention_features(nc, S, sem, name, x, w, a_src, a_dst, heads, h, own_scores, table):
    U, BANKS = 5, 3
    W = CH + 2 * HEADS
    loaded, copied, turned, turned_out, made, made_out, own, extended, stored = (
        sem(name + n) for n in ("loaded", "copied", "turned", "turned_out", "made", "made_out", "own", "extended", "stored"))
    with ExitStack() as ctx:
        def sb(n, shape, dt=FP32):
            return ctx.enter_context(nc.sbuf_tensor(name + n, shape, dt))
        w_sb = sb("w", [P, KC, W])
        a_sb = sb("a", [P, 2, CH])
        prod = sb("prod", [P, KC, 2, CH])
        score = sb("score", [P, KC, 2, heads])
        xs = [sb(f"x{u}", [P, CH]) for u in range(U)]
        xt = [sb(f"xt{u}", [P, KC * P]) for u in range(U)]
        p_t = [ctx.enter_context(nc.psum_tensor(f"{name}t{n}", [P, KC * P], FP32)) for n in range(U)]
        p_h = [ctx.enter_context(nc.psum_tensor(f"{name}h{n}", [P, W], FP32)) for n in range(BANKS)]
        with nc.Block() as block:
            @block.sync
            def _(sp):
                sp.dma_start(w_sb[:, :, 0:CH], w.rearrange("(k p) n -> p k n", k=KC)).then_inc(loaded, 16)
                for n, a in enumerate((a_src, a_dst)):
                    sp.dma_start(a_sb[:, n, :], a.rearrange("h c -> (h c)").partition_broadcast(P)).then_inc(loaded, 16)
                rows = table.rearrange("(b p) c -> p b c", p=P)
                with sp.Fori(0, BLOCKS // U) as i:
                    part = bass.ds(i * U, U)
                    sp.wait_ge(made_out, i * U + (U + BANKS - 1))
                    sp.dma_start(rows[:, part, :], h[:, part, :]).then_inc(stored, 16)
                sp.wait_ge(stored, 16 * (BLOCKS // U))

            @block.scalar
            def _(act):
                def stage(b, u):
                    act.copy(xs[u][:, :], x[:, bass.ds(b, 1), :].rearrange("p a c -> p (a c)")).then_inc(copied, 1)

                def copy_out(b, u):
                    act.wait_ge(made, b + 1)
                    act.copy(own_scores[:, bass.ds(b, 1), 0:HEADS].rearrange("p a c -> p (a c)"), p_h[u % BANKS][:, HROW:])
                    act.copy(h[:, bass.ds(b, 1), :].rearrange("p a c -> p (a c)"), p_h[u % BANKS][:, 0:HROW]).then_inc(made_out, 1)
                for u in range(U):
                    stage(u, u)
                with act.Fori(0, BLOCKS // U - 1) as i:
                    for u in range(U):
                        copy_out(i * U + u, u)
                        stage(i * U + (u + U), u)
                for u in range(U):
                    copy_out(BLOCKS - U + u, u)

            @block.tensor
            def _(pe):
                pe.sem_inc(made_out, BANKS - 1)

                def turn(b, u):
                    pe.wait_ge(copied, b + 1)
                    for k in range(KC):
                        ins = pe.transpose(p_t[u][:, k * P:(k + 1) * P], xs[u][:, k * P:(k + 1) * P], S.ident[:, :])
                    ins.then_inc(turned, 1)

                def multiply(b, u, more):
                    if more:
                        turn(b + 1, (u + 1) % U)
                    pe.wait_ge(turned_out, b + 1)
                    pe.wait_ge(made_out, b + 1)
                    for k in range(KC):
                        ins = pe.matmul(p_h[u % BANKS][:, :], xt[u][:, k * P:(k + 1) * P], w_sb[:, k, :], start=(k == 0), stop=(k == KC - 1))
                    ins.then_inc(made, 1)
                turn(0, 0)
                pe.wait_ge(loaded, 48)
                pe.wait_ge(extended, 1)
                with pe.Fori(0, BLOCKS // U - 1) as i:
                    for u in range(U):
                        multiply(i * U + u, u, True)
                for u in range(U):
                    multiply(BLOCKS - U + u, u, u + 1 < U)

            @block.vector
            def _(v):
                step = Chain(v, own)
                v.wait_ge(loaded, 48)
                for k in range(KC):
                    ins = v.tensor_tensor(prod[:, k, :, :], w_sb[:, k, 0:CH].unsqueeze(1).to_broadcast([P, 2, CH]), a_sb[:, :, :], ALU.mult)
                step(ins)
                step(v.tensor_reduce(score[:, :, :, :], prod[:, :, :, :].rearrange("p k n (h c) -> p k n h c", h=heads), AX.X, ALU.add))
                for n in range(2):
                    extra = score[:, :, n, :]
                    ins = v.tensor_copy(w_sb[:, :, CH + n * HEADS:CH + (n + 1) * HEADS],
                                        extra.to_broadcast([P, KC, HEADS]) if heads == 1 else extra)
                ins.then_inc(extended, 1)
                with v.Fori(0, BLOCKS // U) as i:
                    for u in range(U):
                        v.wait_ge(turned, i * U + (u + 1))
                        v.tensor_copy(xt[u][:, :], p_t[u][:, :]).then_inc(turned_out, 1)
                v.wait_ge(made_out, BLOCKS + BANKS - 1)
                own_logit = own_scores[:, :, HEADS:]
                step(v.tensor_tensor(own_logit, h[:, :, CH:], own_scores[:, :, 0:HEADS], ALU.add))
                v.scalar_tensor_tensor(own_logit, own_logit, SLOPE, own_logit, ALU.mult, ALU.max)


STRIPS = P // HEADS
SCH = CHUNKS // STRIPS
SLEN = SCH * P


def softmax_weights(nc, S, E, sem, name, edge):
    own, prepared, turned, turned_out, given, passed = (
        sem(name + n) for n in ("own", "prepared", "turned", "turned_out", "given", "passed"))
    weighed, nodes_staged, logits_staged = sem(name + "weighed"), sem(name + "nodes_staged"), sem(name + "logits_staged")
    QUADS = [(j, min(4, SCH - j)) for j in range(0, SCH, 4)]
    NQ = len(QUADS)
    with ExitStack() as ctx:
        def sb(n, shape, dt=FP32):
            return ctx.enter_context(nc.sbuf_tensor(name + n, shape, dt))
        peak = sb("peak", [P, SLEN])
        fwd = sb("fwd", [P, SLEN])
        reset = sb("reset", [P, SLEN + 1])
        node = sb("node", [P, CHUNKS])
        ends = sb("ends", [P, 2])
        row = sb("row", [1, 2 * P])
        carry = sb("carry", [1, P + HEADS])
        init = sb("init", [P, 1])
        p_b = [ctx.enter_context(nc.psum_tensor(f"{name}b{n}", [P, 512], FP32)) for n in range(4)]
        p_s = ctx.enter_context(nc.psum_tensor(name + "s", [P, 512], FP32))
        e0, e1, e2 = (edge[:, :, n * HEADS:(n + 1) * HEADS] for n in range(3))
        strips = [e.rearrange("p (i j) h -> p i j h", i=STRIPS) for e in (e0, e1, e2)]

        def staged(tile):
            return tile[:, 0:SLEN].rearrange("p (j i h) -> p j i h", j=SCH, i=STRIPS)

        with nc.Block() as block:
            @block.vector
            def _(v):
                step = Chain(v, own)
                give = Chain(v, given)
                step(v.tensor_tensor(e0, e0, e1, ALU.add))
                v.scalar_tensor_tensor(e0, e0, SLOPE, e0, ALU.mult, ALU.max).then_inc(prepared, 1)
                step(v.scalar_tensor_tensor(node[:, :], E.block_of[:, 0:CHUNKS], 256.0, E.local[:, 0:CHUNKS], ALU.mult, ALU.add))
                step(v.tensor_scalar(node[:, :], node[:, :], 2.0, None, ALU.add))
                v.tensor_copy(staged(reset), node[:, :].rearrange("p (i j) -> p j i", i=STRIPS).unsqueeze(3).to_broadcast([P, SCH, STRIPS, HEADS])).then_inc(nodes_staged, 1)
                n = 0
                for out in (peak, fwd):
                    for j, m in QUADS:
                        n += 1
                        v.wait_ge(turned, n)
                        v.tensor_copy(out[:, j * P:(j + m) * P], p_b[(n - 1) % 4][:, 0:m * P]).then_inc(turned_out, 1)
                v.wait_ge(turned_out, n)
                step(v.scalar_tensor_tensor(reset[:, 1:SLEN], fwd[:, 1:SLEN], 1.0, fwd[:, 0:SLEN - 1], ALU.mult, ALU.not_equal))
                give(v.tensor_copy(ends[:, 0:1], fwd[:, SLEN - 1:SLEN]))
                v.wait_ge(passed, 1)
                give(v.tensor_tensor(reset[:, 0:1], fwd[:, 0:1], p_s[:, 0:1], ALU.not_equal))
                v.wait_ge(passed, 2)
                step(v.tensor_copy(reset[:, SLEN:], p_s[:, 1:2]))
                step(v.tensor_scalar(reset[:, :], reset[:, :], -BIG, None, ALU.mult))

                def running_maximum(out, resets, x, last, back):
                    turn = (lambda ap: ap[:, ::-1]) if back else (lambda ap: ap)
                    step(v.tensor_tensor_scan(turn(out), turn(resets), turn(x), -BIG, ALU.add, ALU.max))
                    step(v.tensor_copy(ends[:, 0:1], out[:, last:last + 1]))
                    give(v.tensor_reduce(ends[:, 1:2], resets, AX.X, ALU.min))
                    step(v.memset(carry[:, :], -BIG))
                    v.wait_ge(passed, 5 if back else 3)
                    step(v.tensor_copy(row[:, :], p_s[0:1, P:3 * P]))
                    for h in range(HEADS):
                        state, hold = row[0:1, h:P:HEADS], row[0:1, P + h:2 * P:HEADS]
                        shifted = carry[0:1, h:P:HEADS] if back else carry[0:1, HEADS + h:HEADS + P:HEADS]
                        scan = v.tensor_tensor_scan(turn(shifted), turn(hold), turn(state), -BIG, ALU.add, ALU.max)
                        if h == HEADS - 1:
                            give(scan)
                    v.wait_ge(passed, 6 if back else 4)
                    step(v.tensor_copy(init[:, :], p_s[:, 2:3]))
                    return v.tensor_tensor_scan(turn(out), turn(resets), turn(x), init[:, 0:1], ALU.add, ALU.max)
                step(running_maximum(fwd[:, :], reset[:, 0:SLEN], peak[:, :], SLEN - 1, False))
                give(running_maximum(peak[:, :], reset[:, 1:], fwd[:, :], 0, True))
                give(v.tensor_scalar(fwd[:, :], reset[:, 1:], -1.0 / BIG, None, ALU.mult))
                for j, m in QUADS:
                    n += 1
                    v.wait_ge(turned, n)
                    part = strips[2][:, :, j:j + m, :].rearrange("p i j h -> p j i h")
                    out = strips[1][:, :, j:j + m, :].rearrange("p i j h -> p j i h")
                    src = p_b[(n - 1) % 4][:, 0:m * P].rearrange("p (j i h) -> p j i h", j=m, i=STRIPS)
                    v.tensor_tensor(out, src, part, ALU.max).then_inc(turned_out, 1)
                v.wait_ge(turned_out, n)
                v.tensor_tensor(e0, e0, e1, ALU.subtract).then_inc(weighed, 1)
                for j, m in QUADS:
                    n += 1
                    v.wait_ge(turned, n)
                    out = strips[2][:, :, j:j + m, :].rearrange("p i j h -> p j i h")
                    src = p_b[(n - 1) % 4][:, 0:m * P].rearrange("p (j i h) -> p j i h", j=m, i=STRIPS)
                    v.tensor_copy(out, src).then_inc(turned_out, 1)
                v.wait_ge(turned_out, n)
                v.tensor_tensor(e1, e1, e2, ALU.mult)

            @block.scalar
            def _(act):
                act.wait_ge(prepared, 1)
                act.copy(staged(fwd), strips[0].rearrange("p i j h -> p j i h")).then_inc(logits_staged, 1)
                act.wait_ge(weighed, 1)
                act.activation(e0, e0, ACT.Exp)

            @block.tensor
            def _(pe):
                n = 0

                def turn(j, m, view):
                    nonlocal n
                    if n >= 4:
                        pe.wait_ge(turned_out, n - 3)
                    for q in range(m):
                        ins = pe.transpose(p_b[n % 4][:, q * P:(q + 1) * P], view(j + q), S.ident[:, :])
                    ins.then_inc(turned, 1)
                    n += 1
                for ready, strip in ((logits_staged, fwd), (nodes_staged, reset)):
                    pe.wait_ge(ready, 1)
                    for j, m in QUADS:
                        turn(j, m, lambda c: strip[:, c * P:(c + 1) * P])
                pe.wait_ge(given, 1)
                pe.matmul(p_s[:, 0:1], S.down[:, :], ends[:, 0:1], start=True, stop=True).then_inc(passed, 1)
                pe.wait_ge(given, 2)
                pe.matmul(p_s[:, 1:2], S.up[:, :], reset[:, 0:1], start=True, stop=True).then_inc(passed, 1)
                for back in range(2):
                    pe.wait_ge(given, 3 + 2 * back)
                    pe.transpose(p_s[0:1, P:2 * P], ends[:, 0:1], S.ident[:, :])
                    pe.transpose(p_s[0:1, 2 * P:3 * P], ends[:, 1:2], S.ident[:, :]).then_inc(passed, 1)
                    pe.wait_ge(given, 4 + 2 * back)
                    pe.matmul(p_s[:, 2:3], carry[0:1, back * HEADS:back * HEADS + P], S.ones[0:1, 0:1], start=True, stop=True).then_inc(passed, 1)
                for w, strip in enumerate((peak, fwd)):
                    pe.wait_ge(given, 7 + w)
                    for j, m in QUADS:
                        turn(j, m, lambda c: strip[:, c * P:(c + 1) * P])


def weighted_sum(nc, S, E, sem, name, edge, spill, acc, odd):
    hot_ready, added, done, cleared, mixed, beside, apart = (
        sem(name + n) for n in ("hot", "added", "done", "cleared", "mixed", "beside", "apart"))
    QUARTS = RING // GRP
    arrived = [sem(f"{name}row{q}") for q in range(QUARTS)]
    with ExitStack() as ctx:
        hot = ctx.enter_context(nc.sbuf_tensor(name + "hots", [P, PAIR, P], FP32))
        rows = ctx.enter_context(nc.sbuf_tensor(name + "rows", [P, RING, ACCW], FP32))
        banks = [ctx.enter_context(nc.psum_tensor(f"{name}bank{u}", [P, 512], FP32)) for u in range(GRP)]

        def quarter(q):
            return rows[:, q * GRP:(q + 1) * GRP, :]
        with nc.Block() as block:
            @block.sync
            def _(sp):
                with sp.Fori(0, CHUNKS // RING) as i:
                    for q in range(QUARTS):
                        sp.wait_ge(done, i * RING + GRP * (q + 1))
                        sp.dma_start(quarter(q)[:, :, 0:CH], spill[:, bass.ds(i * RING + q * GRP, GRP), :]).then_inc(arrived[q], 16)

            @block.gpsimd
            def _(pool):
                with pool.Fori(0, CHUNKS // RING) as i:
                    for q in range(QUARTS):
                        pool.wait_ge(arrived[q], i * 16 + 16)
                        part = quarter(q)[:, :, 0:CH].rearrange("p a (h c) -> p a h c", h=HEADS)
                        weight = edge[:, bass.ds(i * RING + q * GRP, GRP), 0:HEADS].unsqueeze(3).to_broadcast([P, GRP, HEADS, HC])
                        pool.tensor_tensor(part, part, weight, ALU.mult).then_inc(mixed, 1)

            @block.scalar
            def _(act):
                clear_accumulator(act, S, odd, cleared)
                with act.Fori(0, CHUNKS // RING) as i:
                    for q in range(QUARTS):
                        act.wait_ge(done, i * RING + GRP * (q + 1))
                        act.copy(quarter(q)[:, :, CH:], edge[:, bass.ds(i * RING + q * GRP, GRP), :]).then_inc(beside, 1)
                        act.wait_ge(done, i * RING + (GRP * q + RING - GRP))
                        for u in range(q * GRP, (q + 1) * GRP):
                            ins = act.activation(hot[:, u % PAIR, :], S.col[:, 0:P], ACT.Abs, scale=-1.0, bias=E.local[:, bass.ds(i * RING + u, 1)])
                        ins.then_inc(apart, 1)
                        act.wait_ge(apart, i * QUARTS + (q + 1))
                        group = hot[:, q % 2 * GRP:(q % 2 + 1) * GRP, :]
                        act.activation(group, group, ACT.Relu, scale=-1.0, bias=S.ones[:, 0:1]).then_inc(hot_ready, 1)

            @block.vector
            def _(v):
                v.memset(acc[:, :], 0.0).then_inc(cleared, 1)
                v.wait_ge(cleared, 2)
                hot_and_add(nc, S, E, v, name, None, None, [acc, odd], ACCW, banks, hot_ready, added, done)

            @block.tensor
            def _(pe):
                pe.sem_inc(done, RING)
                with pe.Fori(0, CHUNKS // RING) as i:
                    for u in range(RING):
                        pe.wait_ge(added, i * RING + (u + 1))
                        if u % GRP == 0:
                            pe.wait_ge(hot_ready, i * QUARTS + (u // GRP + 1))
                            pe.wait_ge(mixed, i * QUARTS + (u // GRP + 1))
                            pe.wait_ge(beside, i * QUARTS + (u // GRP + 1))
                        pe.matmul(banks[u % GRP][:, 0:ACCW], hot[:, u % PAIR, :], rows[:, u, :], start=True, stop=True).then_inc(done, 1)


def finish_attention(nc, S, sem, name, acc, odd, h, own_scores, b, result, relu):
    U = 5
    own, loaded, lowered, weighed, scaled, ready = (sem(name + n) for n in ("own", "loaded", "lowered", "weighed", "scaled", "ready"))
    with ExitStack() as ctx:
        bias = ctx.enter_context(nc.sbuf_tensor(name + "bias", [P, CH], FP32))
        weight = ctx.enter_context(nc.sbuf_tensor(name + "weight", [P, BLOCKS, HEADS], FP32))
        total = ctx.enter_context(nc.sbuf_tensor(name + "total", [P, BLOCKS, HEADS], FP32))
        A, B = blocks_of(acc), blocks_of(odd)
        own_logit = own_scores[:, :, HEADS:]

        def per_head(ap):
            return ap.rearrange("p b (h c) -> p b h c", h=HEADS)

        def wide(ap, n=BLOCKS):
            return ap.unsqueeze(3).to_broadcast([P, n, HEADS, HC])
        with nc.Block() as block:
            @block.sync
            def _(sp):
                sp.dma_start(bias[:, :], b.partition_broadcast(P)).then_inc(loaded, 16)
                sp.wait_ge(loaded, 16)

            @block.gpsimd
            def _(pool):
                pool.wait_ge(weighed, 1)
                for s in range(0, BLOCKS, U):
                    part = per_head(h[:, s:s + U, 0:CH])
                    pool.tensor_tensor(part, part, wide(weight[:, s:s + U, :], U), ALU.mult).then_inc(scaled, 1)

            @block.scalar
            def _(act):
                act.wait_ge(lowered, 1)
                act.activation(weight[:, :, :], weight[:, :, :], ACT.Exp).then_inc(weighed, 1)
                if relu:
                    for s in range(0, BLOCKS, U):
                        act.wait_ge(ready, s // U + 1)
                        act.activation(result[:, s:s + U, :], result[:, s:s + U, :], ACT.Relu)

            @block.vector
            def _(v):
                step = Chain(v, own)
                step(v.tensor_tensor(A[:, :, CH:], A[:, :, CH:], B[:, :, CH:], ALU.add))
                step(v.tensor_scalar(weight[:, :, :], A[:, :, CH + 2 * HEADS:], -1.0, 1.0, ALU.mult, ALU.add))
                step(v.tensor_tensor(weight[:, :, :], weight[:, :, :], own_logit, ALU.mult))
                step(v.tensor_tensor(weight[:, :, :], weight[:, :, :], A[:, :, CH + HEADS:CH + 2 * HEADS], ALU.add))
                v.tensor_tensor(weight[:, :, :], own_logit, weight[:, :, :], ALU.subtract).then_inc(lowered, 1)
                step(v.tensor_tensor(result[:, :, :], A[:, :, 0:CH], B[:, :, 0:CH], ALU.add))
                v.wait_ge(weighed, 1)
                step(v.scalar_tensor_tensor(total[:, :, :], A[:, :, CH:CH + HEADS], 1e-16, weight[:, :, :], ALU.add, ALU.add))
                step(v.reciprocal(total[:, :, :], total[:, :, :]))
                v.wait_ge(loaded, 16)
                for s in range(0, BLOCKS, U):
                    part = result[:, s:s + U, :]
                    v.wait_ge(scaled, s // U + 1)
                    step(v.tensor_tensor(part, part, h[:, s:s + U, 0:CH], ALU.add))
                    step(v.tensor_tensor(per_head(part), per_head(part), wide(total[:, s:s + U, :], U), ALU.mult))
                    v.tensor_tensor(part, part, bias[:, :].unsqueeze(1).to_broadcast([P, U, CH]), ALU.add).then_inc(ready, 1)


def attention_layer(nc, S, E, name, x, w, a_src, a_dst, b, heads, acc, result, relu, node_table, spill, round_of_gathers):
    with ExitStack() as ctx:
        def sb(n, shape, dt=FP32):
            return ctx.enter_context(nc.sbuf_tensor(name + n, shape, dt))
        h = sb("h", [P, BLOCKS, HROW])
        own_scores = sb("own_scores", [P, BLOCKS, 2 * HEADS])
        with Semaphores(nc) as sem:
            attention_features(nc, S, sem, name + "f_", x, w, a_src, a_dst, heads, h, own_scores, node_table)
        with ExitStack() as inner:
            edge = inner.enter_context(nc.sbuf_tensor(name + "edge", [P, CHUNKS, 3 * HEADS], FP32))
            with Semaphores(nc) as sem:
                look_up_and_gather(nc, S, E, sem, name + "l_", own_scores, 2 * HEADS, edge[:, :, HEADS:], node_table, edge, spill, round_of_gathers)
            with Semaphores(nc) as sem:
                softmax_weights(nc, S, E, sem, name + "s_", edge)
                odd = inner.enter_context(nc.sbuf_tensor(name + "odd", [P, BLOCKS * ACCW], FP32))
                weighted_sum(nc, S, E, sem, name + "w_", edge, spill, acc, odd)
            with Semaphores(nc) as sem:
                finish_attention(nc, S, sem, name + "n_", acc, odd, h, own_scores, b, result, relu)


def gnn(nc, x, src, dst, edge_type_7, L0_gnn_gn1_w, L0_gnn_gn1_b, L0_gnn_conv1_w, L0_gnn_gn2_w, L0_gnn_gn2_b, L0_gnn_conv2_w,
        L1_gnn_W1, L1_gnn_att_src1, L1_gnn_att_dst1, L1_gnn_b1, L1_gnn_W2, L1_gnn_att_src2, L1_gnn_att_dst2, L1_gnn_b2, out):
    WIDE = CHUNKS + EXTRA
    feature_table = nc.dram_tensor("feature_table", [TYPES * TROWS, CH], FP32).ap()
    node_table = nc.dram_tensor("node_table", [BLOCKS * P, HROW], FP32).ap()
    spill = nc.dram_tensor("spill", [P, CHUNKS, CH], FP32).ap()
    with ExitStack() as ctx:
        S = Shared()

        def keep(stack, n, shape, dt=FP32):
            return stack.enter_context(nc.sbuf_tensor(n, shape, dt))
        S.arrived = [ctx.enter_context(nc.semaphore(f"arrived{u}")) for u in range(RING)]
        S.col = keep(ctx, "col", [P, WIDE])
        S.col_h = keep(ctx, "col_h", [P, CHUNKS], FP16)
        S.row = keep(ctx, "row", [P, 1])
        S.ident = keep(ctx, "ident", [P, P])
        S.ident_b = keep(ctx, "ident_b", [P, P], BF16)
        S.above = keep(ctx, "above", [P, P])
        S.down = keep(ctx, "down", [P, P])
        S.up = keep(ctx, "up", [P, P])
        S.ones = keep(ctx, "ones", [P, P])
        S.zeros = keep(ctx, "zeros", [P, CHUNKS], FP16)
        x_sb = ctx.enter_context(nc.sbuf_tensor("x_sb", [P, BLOCKS, CH], FP32))
        acc = ctx.enter_context(nc.sbuf_tensor("acc", [P, BLOCKS * ACCW], FP32))
        sums = blocks_of(acc)[:, :, 0:CH]

        def lasting(name):
            return ctx.enter_context(nc.semaphore(name))
        by_dst = Placement(nc, ctx, lasting, "by_dst_", 12, FP32)
        with ExitStack() as conv:
            by_src = Placement(nc, conv, lasting, "by_src_", 15, BF16)
            S.col_i = keep(conv, "col_i", [P, WIDE], INT32)
            S.row_i = keep(conv, "row_i", [P, 1], INT32)
            S.weight = keep(conv, "weight", [P, WIDE])
            S.etype = keep(conv, "etype", [P, CHUNKS])
            counts = keep(conv, "counts", [P, BLOCKS, TYPES])
            with ExitStack() as lists:
                S.src_i = keep(lists, "src_i", [P, CPAD], INT32)
                S.dst_i = keep(lists, "dst_i", [P, CPAD], INT32)
                by_src.key_i, by_dst.key_i = S.src_i, S.dst_i
                with ExitStack() as types:
                    S.type_i = keep(types, "type_i", [P, CPAD], INT32)
                    S.pay = keep(types, "pay", [P, CPAD])
                    S.key_lane = keep(types, "key_lane", [P, CPAD])
                    S.key_bin = keep(types, "key_bin", [P, CPAD])
                    by_src.scratch(nc, types, "s_")
                    with Semaphores(nc) as sem:
                        constants(nc, S, sem, src, dst, edge_type_7)
                        x_loaded = load_nodes(nc, S, sem, x, x_sb)
                        rank_edges(nc, S, by_src, conv_payload(S))
                        group_norm(nc, S, sem, "n0_", x_sb[:, :, :], sums, L0_gnn_gn1_w, L0_gnn_gn1_b, x_loaded)
                        typed_features(nc, S, sem, "f0_", sums, L0_gnn_conv1_w, feature_table, move=(by_src, counts))
                with Semaphores(nc) as sem:
                    gather_and_add(nc, S, by_src, sem, "a0_", feature_table, acc, 0, counts=counts)
                by_dst.scratch(nc, lists, "d_")
                with Semaphores(nc) as sem:
                    group_norm(nc, S, sem, "n1_", sums, sums, L0_gnn_gn2_w, L0_gnn_gn2_b)
                    typed_features(nc, S, sem, "f1_", sums, L0_gnn_conv2_w, feature_table, rank=(by_dst, attention_payload(S)))
                    gather_and_add(nc, S, by_src, sem, "a1_", feature_table, acc, 1, other=by_dst)
        with Semaphores(nc) as sem:
            add_and_norm(nc, S, sem, "m0_", x_sb, sums, 2.0)
        attention_layer(nc, S, by_dst, "g0_", x_sb, L1_gnn_W1, L1_gnn_att_src1, L1_gnn_att_dst1, L1_gnn_b1, HEADS, acc, sums, True,
                        node_table, spill, 0)
        attention_layer(nc, S, by_dst, "g1_", sums, L1_gnn_W2, L1_gnn_att_src2, L1_gnn_att_dst2, L1_gnn_b2, 1, acc, sums, False,
                        node_table, spill, 1)
        with Semaphores(nc) as sem:
            add_and_norm(nc, S, sem, "m1_", x_sb, sums, 1.0, out)


def load_nodes(nc, S, sem, x, x_sb):
    loaded, cleared = sem("x_loaded"), sem("x_cleared")
    with nc.Block() as block:
        @block.vector
        def _(v):
            v.memset(x_sb[:, BLOCKS - 1, :], 0.0).then_inc(cleared, 1)

        @block.sync
        def _(sp):
            sp.dma_start(x_sb[:, 0:BLOCKS - 1, :], x[0:(BLOCKS - 1) * P, :].rearrange("(b p) c -> p b c", p=P)).then_inc(loaded, 16)
            sp.wait_ge(cleared, 1)
            sp.dma_start(x_sb[0:LAST, BLOCKS - 1, :], x[(BLOCKS - 1) * P:, :]).then_inc(loaded, 16)
    return loaded


_INS = ["x", "src", "dst", "edge_type_7", "L0_gnn_gn1_w", "L0_gnn_gn1_b", "L0_gnn_conv1_w", "L0_gnn_gn2_w", "L0_gnn_gn2_b",
        "L0_gnn_conv2_w", "L1_gnn_W1", "L1_gnn_att_src1", "L1_gnn_att_dst1", "L1_gnn_b1", "L1_gnn_W2", "L1_gnn_att_src2",
        "L1_gnn_att_dst2", "L1_gnn_b2"]


def kernel(**inputs):
    import numpy as np
    from concourse import bacc
    from concourse.bass_utils import run_bass_kernel_spmd

    nc = bacc.Bacc("TRN2", target_bir_lowering=False, num_devices=1)
    arrays, args = {}, []
    for name in _INS:
        a = np.ascontiguousarray(inputs[name])
        arrays[f"in_{name}"] = a
        args.append(nc.dram_tensor(f"in_{name}", a.shape, mybir.dt.from_np(a.dtype), kind="ExternalInput").ap())
    args.append(nc.dram_tensor("out", (NODES, CH), FP32, kind="ExternalOutput").ap())
    gnn(nc, *args)
    return run_bass_kernel_spmd(nc, [arrays], core_ids=[0]).results[0]["out"]
```
